# Optimizing a Trainium2 kernel written in Bass

```python
import numpy as np
import jax
import jax.numpy as jnp

def _softmax(x, axis=-1):
    return jax.nn.softmax(x, axis=axis)

def _gelu(x):
    return jax.nn.gelu(x, approximate=True)

def _silu(x):
    return jax.nn.silu(x)

def _sigmoid(x):
    return jax.nn.sigmoid(x)

def _layernorm(x, axis=-1, eps=1e-05):
    m = jnp.mean(x, axis=axis, keepdims=True)
    v = jnp.var(x, axis=axis, keepdims=True)
    return (x - m) / jnp.sqrt(v + eps)

def _scatter_add(tgt, idx, src, axis=0):
    return tgt.at[idx].add(src)

def _segment_sum(src, seg, n):
    return jax.ops.segment_sum(src, seg, n)
kernel_name = 'mk_vit_tower_d2_tok_img256_r4_dd1f3c'

def setup_inputs(seed: int=0):
    np.random.seed(seed)
    _w = jnp.asarray

    def _rec_inputs():
        import jax
        import jax.numpy as jnp
        _rk = jax.random.key(seed)
        x = -0.000222058 + 0.999998 * jax.random.normal(jax.random.fold_in(_rk, 1), (8, 3, 128, 128), jnp.float32)
        return x
    x = _rec_inputs()

    def _L0_tok_setup():
        import jax, jax.numpy as jnp
        import numpy as np
        P = 16
        NUM_HEADS = 8
        WINDOW = 64

        def _layer_norm(x, w, b, eps=1e-05):
            mu = jnp.mean(x, axis=-1, keepdims=True)
            var = jnp.var(x, axis=-1, keepdims=True)
            return (x - mu) * jax.lax.rsqrt(var + eps) * w + b

        def _sinusoidal_pe(num_patches, num_features, dtype):
            pos = jnp.arange(num_patches, dtype=jnp.float32)[:, None]
            i = jnp.arange(0, num_features, 2, dtype=jnp.float32)
            div = jnp.exp(-jnp.log(10000.0) * i / num_features)
            ang = pos * div
            pe = jnp.stack([jnp.sin(ang), jnp.cos(ang)], axis=-1).reshape(num_patches, num_features)
            return pe.astype(dtype)

        def _ffn(x, w1, b1, w2, b2):
            h = jax.nn.gelu(jnp.einsum('bnd,hd->bnh', x, w1) + b1)
            return jnp.einsum('bnh,dh->bnd', h, w2) + b2

        def _windowed_attention(x, qkv_w, qkv_b, proj_w, proj_b):
            B, N, D = x.shape
            hd = D // NUM_HEADS
            qkv = jnp.einsum('bnd,ed->bne', x, qkv_w) + qkv_b
            qkv = qkv.reshape(B, N, 3, NUM_HEADS, hd)
            q, k, v = (qkv[:, :, 0], qkv[:, :, 1], qkv[:, :, 2])
            nw = N // WINDOW
            q = q.reshape(B, nw, WINDOW, NUM_HEADS, hd).transpose(0, 3, 1, 2, 4)
            k = k.reshape(B, nw, WINDOW, NUM_HEADS, hd).transpose(0, 3, 1, 2, 4)
            v = v.reshape(B, nw, WINDOW, NUM_HEADS, hd).transpose(0, 3, 1, 2, 4)
            scale = 1.0 / jnp.sqrt(jnp.asarray(hd, x.dtype))
            scores = jnp.einsum('bhwqd,bhwkd->bhwqk', q, k) * scale
            attn = jax.nn.softmax(scores, axis=-1)
            out = jnp.einsum('bhwqk,bhwkd->bhwqd', attn, v)
            out = out.transpose(0, 2, 3, 1, 4).reshape(B, N, D)
            return jnp.einsum('bnd,ed->bne', out, proj_w) + proj_b
        key = jax.random.key(seed)
        ks = jax.random.split(key, 8)
        D, HF = (64, 256)
        s = lambda fan: 1.0 / np.sqrt(fan)
        return {'x': jax.random.normal(ks[0], (32, 3, 128, 128), jnp.float32), 'conv_w': jax.random.normal(ks[1], (D, 3, P, P), jnp.float32) * s(3 * P * P), 'conv_b': jnp.zeros((D,), jnp.float32), 'ln_w': jnp.ones((D,), jnp.float32), 'ln_b': jnp.zeros((D,), jnp.float32), 'qkv_w': jax.random.normal(ks[2], (3 * D, D), jnp.float32) * s(D), 'qkv_b': jnp.zeros((3 * D,), jnp.float32), 'proj_w': jax.random.normal(ks[3], (D, D), jnp.float32) * s(D), 'proj_b': jnp.zeros((D,), jnp.float32), 'ff_w1': jax.random.normal(ks[4], (HF, D), jnp.float32) * s(D), 'ff_b1': jnp.zeros((HF,), jnp.float32), 'ff_w2': jax.random.normal(ks[5], (D, HF), jnp.float32) * s(HF), 'ff_b2': jnp.zeros((D,), jnp.float32)}
    _L0_tok_all = _L0_tok_setup()
    _L0_tok_in = {k: v for k, v in _L0_tok_all.items() if k in ('conv_w', 'conv_b', 'ln_w', 'ln_b', 'qkv_w', 'qkv_b', 'proj_w', 'proj_b', 'ff_w1', 'ff_b1', 'ff_w2', 'ff_b2')}
    del _L0_tok_all

    def _L0_attn_setup():
        import jax, jax.numpy as jnp
        import numpy as np
        key = jax.random.key(seed)
        ks = jax.random.split(key, 4)
        B, S, D = (4, 1024, 64)
        x = jax.random.normal(ks[0], (B, S, D), dtype=jnp.float32)
        Wq = jax.random.normal(ks[1], (D, D), dtype=jnp.float32) * 0.02
        Wk = jax.random.normal(ks[2], (D, D), dtype=jnp.float32) * 0.02
        Wv = jax.random.normal(ks[3], (D, D), dtype=jnp.float32) * 0.02
        bq = jnp.zeros((D,), dtype=jnp.float32)
        bk = jnp.zeros((D,), dtype=jnp.float32)
        bv = jnp.zeros((D,), dtype=jnp.float32)
        return {'x': x, 'Wq': Wq, 'bq': bq, 'Wk': Wk, 'bk': bk, 'Wv': Wv, 'bv': bv}
    _L0_attn_all = _L0_attn_setup()
    _L0_attn_in = {k: v for k, v in _L0_attn_all.items() if k in ('Wq', 'bq', 'Wk', 'bk', 'Wv', 'bv')}
    del _L0_attn_all

    def _L0_ffn_setup():
        import jax, jax.numpy as jnp
        import numpy as np
        B, T, C = (64, 96, 64)
        NH, NKV = (4, 2)
        HD = C // NH
        NREP = NH // NKV
        NE, TOPK = (8, 2)
        HID = int(8 / 3 * C)
        EPS_RMS = 1e-06

        def _rope_tables(t_len):
            inv_freq = 1.0 / 10000.0 ** (np.arange(0, HD, 2, dtype=np.float32) / HD)
            t = np.arange(t_len, dtype=np.float32)
            freqs = np.outer(t, inv_freq)
            emb = np.concatenate([freqs, freqs], axis=-1)
            return (jnp.asarray(np.cos(emb)), jnp.asarray(np.sin(emb)))

        def _rotate_half(x):
            h = x.shape[-1] // 2
            return jnp.concatenate([-x[..., h:], x[..., :h]], axis=-1)

        def _rmsnorm(v, w):
            return v * jax.lax.rsqrt(jnp.mean(v * v, axis=-1, keepdims=True) + EPS_RMS) * w
        key = jax.random.key(seed)
        ks = jax.random.split(key, 10)
        s = lambda k, shape: jax.random.normal(k, shape, jnp.float32) * 0.02
        return {'x': jax.random.normal(ks[0], (B, T, C), jnp.float32), 'ln1_w': jnp.ones((C,), jnp.float32), 'ln2_w': jnp.ones((C,), jnp.float32), 'wq': s(ks[1], (NH * HD, C)), 'wk': s(ks[2], (NKV * HD, C)), 'wv': s(ks[3], (NKV * HD, C)), 'wo': s(ks[4], (C, C)), 'router_w': s(ks[5], (NE, C)), 'w1': s(ks[6], (NE, HID, C)), 'w2': s(ks[7], (NE, C, HID)), 'w3': s(ks[8], (NE, HID, C))}
    _L0_ffn_all = _L0_ffn_setup()
    _L0_ffn_in = {k: v for k, v in _L0_ffn_all.items() if k in ('ln1_w', 'ln2_w', 'wq', 'wk', 'wv', 'wo', 'router_w', 'w1', 'w2', 'w3')}
    del _L0_ffn_all

    def _L1_attn_setup():
        import jax, jax.numpy as jnp
        import numpy as np
        N, F, C, H = (32, 1024, 64, 8)
        D = C // H
        EPS_ATTN = 1e-06
        EPS_LN = 1e-05

        def layer_norm(x, g, b):
            mu = jnp.mean(x, axis=-1, keepdims=True)
            var = jnp.var(x, axis=-1, keepdims=True)
            return (x - mu) * jax.lax.rsqrt(var + EPS_LN) * g + b
        key = jax.random.key(seed)
        ks = jax.random.split(key, 8)
        s = 1.0 / np.sqrt(C)
        return {'x': jax.random.normal(ks[0], (N, F, C), jnp.float32), 'Wqkv': jax.random.uniform(ks[1], (3 * C, C), jnp.float32, -s, s), 'ln1_g': jnp.ones((C,), jnp.float32), 'ln1_b': jnp.zeros((C,), jnp.float32), 'W1': jax.random.uniform(ks[2], (C, C), jnp.float32, -s, s), 'b1': jax.random.uniform(ks[3], (C,), jnp.float32, -s, s), 'W2': jax.random.uniform(ks[4], (C, C), jnp.float32, -s, s), 'b2': jax.random.uniform(ks[5], (C,), jnp.float32, -s, s), 'ln2_g': jnp.ones((C,), jnp.float32), 'ln2_b': jnp.zeros((C,), jnp.float32)}
    _L1_attn_all = _L1_attn_setup()
    _L1_attn_in = {k: v for k, v in _L1_attn_all.items() if k in ('Wqkv', 'ln1_g', 'ln1_b', 'W1', 'b1', 'W2', 'b2', 'ln2_g', 'ln2_b')}
    del _L1_attn_all

    def _L1_ffn_setup():
        import math
        import jax, jax.numpy as jnp
        import numpy as np
        CAPACITY_FACTOR = 1.25
        key = jax.random.key(seed)
        ks = jax.random.split(key, 5)
        B, L, D, F, E = (8, 2048, 64, 256, 8)
        h = jax.random.normal(ks[0], (B, L, D), dtype=jnp.float32)
        gate_w = jax.random.normal(ks[1], (D, E), dtype=jnp.float32) * 0.02
        gate_b = jnp.zeros((E,), dtype=jnp.float32)
        w1 = jax.random.normal(ks[2], (E, D, F), dtype=jnp.float32) * (1.0 / math.sqrt(D))
        b1 = jnp.zeros((E, F), dtype=jnp.float32)
        w2 = jax.random.normal(ks[3], (E, F, D), dtype=jnp.float32) * (1.0 / math.sqrt(F))
        b2 = jnp.zeros((E, D), dtype=jnp.float32)
        return {'h': h, 'gate_w': gate_w, 'gate_b': gate_b, 'w1': w1, 'b1': b1, 'w2': w2, 'b2': b2}
    _L1_ffn_all = _L1_ffn_setup()
    _L1_ffn_in = {k: v for k, v in _L1_ffn_all.items() if k in ('gate_w', 'gate_b', 'w1', 'b1', 'w2', 'b2')}
    del _L1_ffn_all
    return {'x': x, 'L0_tok_conv_w': _L0_tok_in['conv_w'], 'L0_tok_conv_b': _L0_tok_in['conv_b'], 'L0_tok_ln_w': _L0_tok_in['ln_w'], 'L0_tok_ln_b': _L0_tok_in['ln_b'], 'L0_tok_qkv_w': _L0_tok_in['qkv_w'], 'L0_tok_qkv_b': _L0_tok_in['qkv_b'], 'L0_tok_proj_w': _L0_tok_in['proj_w'], 'L0_tok_proj_b': _L0_tok_in['proj_b'], 'L0_tok_ff_w1': _L0_tok_in['ff_w1'], 'L0_tok_ff_b1': _L0_tok_in['ff_b1'], 'L0_tok_ff_w2': _L0_tok_in['ff_w2'], 'L0_tok_ff_b2': _L0_tok_in['ff_b2'], 'L0_attn_Wq': _L0_attn_in['Wq'], 'L0_attn_bq': _L0_attn_in['bq'], 'L0_attn_Wk': _L0_attn_in['Wk'], 'L0_attn_bk': _L0_attn_in['bk'], 'L0_attn_Wv': _L0_attn_in['Wv'], 'L0_attn_bv': _L0_attn_in['bv'], 'L0_ffn_ln1_w': _L0_ffn_in['ln1_w'], 'L0_ffn_ln2_w': _L0_ffn_in['ln2_w'], 'L0_ffn_wq': _L0_ffn_in['wq'], 'L0_ffn_wk': _L0_ffn_in['wk'], 'L0_ffn_wv': _L0_ffn_in['wv'], 'L0_ffn_wo': _L0_ffn_in['wo'], 'L0_ffn_router_w': _L0_ffn_in['router_w'], 'L0_ffn_w1': _L0_ffn_in['w1'], 'L0_ffn_w2': _L0_ffn_in['w2'], 'L0_ffn_w3': _L0_ffn_in['w3'], 'L1_attn_Wqkv': _L1_attn_in['Wqkv'], 'L1_attn_ln1_g': _L1_attn_in['ln1_g'], 'L1_attn_ln1_b': _L1_attn_in['ln1_b'], 'L1_attn_W1': _L1_attn_in['W1'], 'L1_attn_b1': _L1_attn_in['b1'], 'L1_attn_W2': _L1_attn_in['W2'], 'L1_attn_b2': _L1_attn_in['b2'], 'L1_attn_ln2_g': _L1_attn_in['ln2_g'], 'L1_attn_ln2_b': _L1_attn_in['ln2_b'], 'L1_ffn_gate_w': _L1_ffn_in['gate_w'], 'L1_ffn_gate_b': _L1_ffn_in['gate_b'], 'L1_ffn_w1': _L1_ffn_in['w1'], 'L1_ffn_b1': _L1_ffn_in['b1'], 'L1_ffn_w2': _L1_ffn_in['w2'], 'L1_ffn_b2': _L1_ffn_in['b2']}

def reference(x, L0_tok_conv_w, L0_tok_conv_b, L0_tok_ln_w, L0_tok_ln_b, L0_tok_qkv_w, L0_tok_qkv_b, L0_tok_proj_w, L0_tok_proj_b, L0_tok_ff_w1, L0_tok_ff_b1, L0_tok_ff_w2, L0_tok_ff_b2, L0_attn_Wq, L0_attn_bq, L0_attn_Wk, L0_attn_bk, L0_attn_Wv, L0_attn_bv, L0_ffn_ln1_w, L0_ffn_ln2_w, L0_ffn_wq, L0_ffn_wk, L0_ffn_wv, L0_ffn_wo, L0_ffn_router_w, L0_ffn_w1, L0_ffn_w2, L0_ffn_w3, L1_attn_Wqkv, L1_attn_ln1_g, L1_attn_ln1_b, L1_attn_W1, L1_attn_b1, L1_attn_W2, L1_attn_b2, L1_attn_ln2_g, L1_attn_ln2_b, L1_ffn_gate_w, L1_ffn_gate_b, L1_ffn_w1, L1_ffn_b1, L1_ffn_w2, L1_ffn_b2):
    import jax
    import jax.numpy as jnp

    def _L0_tok_ref(x, conv_w, conv_b, ln_w, ln_b, qkv_w, qkv_b, proj_w, proj_b, ff_w1, ff_b1, ff_w2, ff_b2):
        import jax, jax.numpy as jnp
        import numpy as np
        P = 16
        NUM_HEADS = 8
        WINDOW = 64

        def _layer_norm(x, w, b, eps=1e-05):
            mu = jnp.mean(x, axis=-1, keepdims=True)
            var = jnp.var(x, axis=-1, keepdims=True)
            return (x - mu) * jax.lax.rsqrt(var + eps) * w + b

        def _sinusoidal_pe(num_patches, num_features, dtype):
            pos = jnp.arange(num_patches, dtype=jnp.float32)[:, None]
            i = jnp.arange(0, num_features, 2, dtype=jnp.float32)
            div = jnp.exp(-jnp.log(10000.0) * i / num_features)
            ang = pos * div
            pe = jnp.stack([jnp.sin(ang), jnp.cos(ang)], axis=-1).reshape(num_patches, num_features)
            return pe.astype(dtype)

        def _ffn(x, w1, b1, w2, b2):
            h = jax.nn.gelu(jnp.einsum('bnd,hd->bnh', x, w1) + b1)
            return jnp.einsum('bnh,dh->bnd', h, w2) + b2

        def _windowed_attention(x, qkv_w, qkv_b, proj_w, proj_b):
            B, N, D = x.shape
            hd = D // NUM_HEADS
            qkv = jnp.einsum('bnd,ed->bne', x, qkv_w) + qkv_b
            qkv = qkv.reshape(B, N, 3, NUM_HEADS, hd)
            q, k, v = (qkv[:, :, 0], qkv[:, :, 1], qkv[:, :, 2])
            nw = N // WINDOW
            q = q.reshape(B, nw, WINDOW, NUM_HEADS, hd).transpose(0, 3, 1, 2, 4)
            k = k.reshape(B, nw, WINDOW, NUM_HEADS, hd).transpose(0, 3, 1, 2, 4)
            v = v.reshape(B, nw, WINDOW, NUM_HEADS, hd).transpose(0, 3, 1, 2, 4)
            scale = 1.0 / jnp.sqrt(jnp.asarray(hd, x.dtype))
            scores = jnp.einsum('bhwqd,bhwkd->bhwqk', q, k) * scale
            attn = jax.nn.softmax(scores, axis=-1)
            out = jnp.einsum('bhwqk,bhwkd->bhwqd', attn, v)
            out = out.transpose(0, 2, 3, 1, 4).reshape(B, N, D)
            return jnp.einsum('bnd,ed->bne', out, proj_w) + proj_b
        B, C, H, W = x.shape
        D = conv_w.shape[0]
        nH, nW = (H // P, W // P)
        patches = x.reshape(B, C, nH, P, nW, P).transpose(0, 2, 4, 1, 3, 5).reshape(B, nH * nW, C * P * P)
        h = jnp.einsum('bnp,dp->bnd', patches, conv_w.reshape(D, -1)) + conv_b
        h = _layer_norm(h, ln_w, ln_b)
        h = h + _sinusoidal_pe(h.shape[1], D, h.dtype)
        identity = h
        h = _ffn(h, ff_w1, ff_b1, ff_w2, ff_b2)
        h = _windowed_attention(h, qkv_w, qkv_b, proj_w, proj_b)
        h = h + identity
        identity = h
        h = _ffn(h, ff_w1, ff_b1, ff_w2, ff_b2)
        return h + identity

    def _L0_attn_ref(x, Wq, bq, Wk, bk, Wv, bv):
        import jax, jax.numpy as jnp
        import numpy as np
        Q = jnp.einsum('bsd,de->bse', x, Wq) + bq
        K = jnp.einsum('bsd,de,->bse'.replace(',->', '->'), x, Wk) + bk
        V = jnp.einsum('bsd,de->bse', x, Wv) + bv
        scale = 1.0 / jnp.sqrt(jnp.asarray(Q.shape[-1], dtype=jnp.float32))
        scores = jnp.einsum('bqd,bkd->bqk', Q, K) * scale
        weights = jax.nn.softmax(scores, axis=-1)
        return jnp.einsum('bqk,bkd->bqd', weights, V)

    def _L0_ffn_ref(x, ln1_w, ln2_w, wq, wk, wv, wo, router_w, w1, w2, w3):
        import jax, jax.numpy as jnp
        import numpy as np
        B, T, C = (64, 96, 64)
        NH, NKV = (4, 2)
        HD = C // NH
        NREP = NH // NKV
        NE, TOPK = (8, 2)
        HID = int(8 / 3 * C)
        EPS_RMS = 1e-06

        def _rope_tables(t_len):
            inv_freq = 1.0 / 10000.0 ** (np.arange(0, HD, 2, dtype=np.float32) / HD)
            t = np.arange(t_len, dtype=np.float32)
            freqs = np.outer(t, inv_freq)
            emb = np.concatenate([freqs, freqs], axis=-1)
            return (jnp.asarray(np.cos(emb)), jnp.asarray(np.sin(emb)))

        def _rotate_half(x):
            h = x.shape[-1] // 2
            return jnp.concatenate([-x[..., h:], x[..., :h]], axis=-1)

        def _rmsnorm(v, w):
            return v * jax.lax.rsqrt(jnp.mean(v * v, axis=-1, keepdims=True) + EPS_RMS) * w
        Bx, Tx, Cx = x.shape
        h = _rmsnorm(x, ln1_w)
        q = (h @ wq.T).reshape(Bx, Tx, NH, HD).transpose(0, 2, 1, 3)
        k = (h @ wk.T).reshape(Bx, Tx, NKV, HD).transpose(0, 2, 1, 3)
        v = (h @ wv.T).reshape(Bx, Tx, NKV, HD).transpose(0, 2, 1, 3)
        cos, sin = _rope_tables(Tx)
        cos, sin = (cos[None, None], sin[None, None])
        q = q * cos + _rotate_half(q) * sin
        k = k * cos + _rotate_half(k) * sin
        k = jnp.repeat(k, NREP, axis=1)
        v = jnp.repeat(v, NREP, axis=1)
        scores = jnp.einsum('bhtd,bhsd->bhts', q, k) / jnp.sqrt(jnp.float32(HD))
        causal = jnp.tril(jnp.ones((Tx, Tx), dtype=bool))
        scores = jnp.where(causal[None, None], scores, jnp.float32(-1e+30))
        att = jax.nn.softmax(scores, axis=-1)
        y = jnp.einsum('bhts,bhsd->bhtd', att, v).transpose(0, 2, 1, 3).reshape(Bx, Tx, Cx)
        x = x + y @ wo.T
        flat = _rmsnorm(x, ln2_w).reshape(-1, Cx)
        probs = jax.nn.softmax(flat @ router_w.T, axis=-1)
        tp, ti = jax.lax.top_k(probs, TOPK)
        tp = tp / (jnp.sum(tp, axis=-1, keepdims=True) + 1e-09)
        weights = jnp.sum(tp[..., None] * jax.nn.one_hot(ti, NE, dtype=flat.dtype), axis=1)
        out = jnp.zeros_like(flat)
        for e in range(NE):
            hh = jax.nn.silu(flat @ w1[e].T) * (flat @ w3[e].T)
            out = out + weights[:, e:e + 1] * (hh @ w2[e].T)
        return x + out.reshape(Bx, Tx, Cx)

    def _L1_attn_ref(x, Wqkv, ln1_g, ln1_b, W1, b1, W2, b2, ln2_g, ln2_b):
        import jax, jax.numpy as jnp
        import numpy as np
        N, F, C, H = (32, 1024, 64, 8)
        D = C // H
        EPS_ATTN = 1e-06
        EPS_LN = 1e-05

        def layer_norm(x, g, b):
            mu = jnp.mean(x, axis=-1, keepdims=True)
            var = jnp.var(x, axis=-1, keepdims=True)
            return (x - mu) * jax.lax.rsqrt(var + EPS_LN) * g + b
        n, f, c = x.shape
        qkv = jnp.einsum('nfc,oc->nfo', x, Wqkv)
        q, k, v = jnp.split(qkv, 3, axis=-1)
        q = q.reshape(n, f, H, D)
        k = k.reshape(n, f, H, D)
        v = v.reshape(n, f, H, D)
        q = jax.nn.elu(q) + 1.0
        k = jax.nn.elu(k) + 1.0
        kv = jnp.einsum('nshd,nshm->nhmd', k, v)
        ksum = jnp.sum(k, axis=1)
        z = 1.0 / (jnp.einsum('nlhd,nhd->nlh', q, ksum) + EPS_ATTN)
        t = jnp.einsum('nlhd,nhmd,nlh->nlhm', q, kv, z)
        t = t.reshape(n, f, c)
        x1 = layer_norm(t + x, ln1_g, ln1_b)
        h = jax.nn.gelu(jnp.einsum('nfc,oc->nfo', x1, W1) + b1, approximate=False)
        y = jnp.einsum('nfc,oc->nfo', h, W2) + b2
        return layer_norm(y + x1, ln2_g, ln2_b)

    def _L1_ffn_ref(h, gate_w, gate_b, w1, b1, w2, b2):
        import math
        import jax, jax.numpy as jnp
        import numpy as np
        CAPACITY_FACTOR = 1.25
        B, L, D = h.shape
        E = gate_w.shape[1]
        T = B * L
        C = max(1, math.ceil(CAPACITY_FACTOR * T / E))
        x = h.reshape(T, D)
        logits = x @ gate_w + gate_b
        probs = jax.nn.softmax(logits, axis=-1)
        idx = jnp.argmax(probs, axis=-1)
        prb = jnp.take_along_axis(probs, idx[:, None], axis=1)[:, 0]
        one_hot = jax.nn.one_hot(idx, E, dtype=jnp.float32)
        pos = (jnp.cumsum(one_hot, axis=0) * one_hot).sum(-1).astype(jnp.int32) - 1
        kept = pos < C
        pos_safe = jnp.where(kept, pos, C)
        buf = jnp.zeros((E, C, D), dtype=h.dtype).at[idx, pos_safe].set(x, mode='drop')
        hmid = jax.nn.relu(jnp.einsum('ecd,edf->ecf', buf, w1) + b1[:, None, :])
        ybuf = jnp.einsum('ecf,efd->ecd', hmid, w2) + b2[:, None, :]
        pos_g = jnp.minimum(pos, C - 1)
        y_tok = ybuf[idx, pos_g] * (prb * kept)[:, None]
        y = y_tok.reshape(B, L, D)
        y = jnp.nan_to_num(y, nan=0.0, posinf=10000.0, neginf=-10000.0)
        return y
    h = _L0_tok_ref(x, L0_tok_conv_w, L0_tok_conv_b, L0_tok_ln_w, L0_tok_ln_b, L0_tok_qkv_w, L0_tok_qkv_b, L0_tok_proj_w, L0_tok_proj_b, L0_tok_ff_w1, L0_tok_ff_b1, L0_tok_ff_w2, L0_tok_ff_b2)
    h = h + _L0_attn_ref(_layernorm(h, axis=-1), L0_attn_Wq, L0_attn_bq, L0_attn_Wk, L0_attn_bk, L0_attn_Wv, L0_attn_bv)
    h = h + _L0_ffn_ref(_layernorm(h, axis=-1), L0_ffn_ln1_w, L0_ffn_ln2_w, L0_ffn_wq, L0_ffn_wk, L0_ffn_wv, L0_ffn_wo, L0_ffn_router_w, L0_ffn_w1, L0_ffn_w2, L0_ffn_w3)
    h = h + _L1_attn_ref(_layernorm(h, axis=-1), L1_attn_Wqkv, L1_attn_ln1_g, L1_attn_ln1_b, L1_attn_W1, L1_attn_b1, L1_attn_W2, L1_attn_b2, L1_attn_ln2_g, L1_attn_ln2_b)
    h = h + _L1_ffn_ref(_layernorm(h, axis=-1), L1_ffn_gate_w, L1_ffn_gate_b, L1_ffn_w1, L1_ffn_b1, L1_ffn_w2, L1_ffn_b2)
    return h

_drawn_inputs = setup_inputs


def setup_inputs(seed=0):
    import zlib

    import numpy as np

    out = dict(_drawn_inputs(seed))
    spreads = {'L0_tok_conv_b': (0.0, 0.1),
     'L0_tok_ln_w': (1.0, 0.2),
     'L0_tok_ln_b': (0.0, 0.1),
     'L0_tok_qkv_b': (0.0, 0.1),
     'L0_tok_proj_b': (0.0, 0.1),
     'L0_tok_ff_b1': (0.0, 0.1),
     'L0_tok_ff_b2': (0.0, 0.1),
     'L0_attn_bq': (0.0, 0.8),
     'L0_attn_bk': (0.0, 2.0),
     'L0_attn_bv': (0.0, 0.1),
     'L0_ffn_ln1_w': (1.0, 0.6),
     'L0_ffn_ln2_w': (1.0, 0.6),
     'L1_attn_ln1_g': (1.0, 0.2),
     'L1_attn_ln1_b': (0.0, 0.301),
     'L1_attn_ln2_g': (1.0, 0.2),
     'L1_attn_ln2_b': (0.0, 0.305),
     'L1_ffn_gate_b': (0.0, 0.388),
     'L1_ffn_b1': (0.0, 2.0),
     'L1_ffn_b2': (0.0, 2.0)}
    factors = {'L0_attn_Wq': 8.0,
     'L0_attn_Wk': 8.0,
     'L0_ffn_wq': 8.0,
     'L0_ffn_wk': 8.0,
     'L0_ffn_wv': 8.0,
     'L0_ffn_wo': 8.0,
     'L0_ffn_router_w': 8.0,
     'L0_ffn_w1': 8.0,
     'L0_ffn_w2': 8.0,
     'L0_ffn_w3': 8.0,
     'L1_attn_b1': 6.642,
     'L1_ffn_gate_w': 3.179,
     'L1_ffn_w1': 2.886,
     'L1_attn_b2': 3.221}
    for name, (base, spread) in spreads.items():
        noise = np.random.default_rng([zlib.crc32(name.encode()), seed]).standard_normal(out[name].shape)
        drawn = base * np.exp(spread * noise) if base else spread * noise
        out[name] = jnp.asarray(drawn.astype(out[name].dtype))
    for name, factor in factors.items():
        out[name] = (out[name] * factor).astype(out[name].dtype)
    return out
```

```python
from contextlib import ExitStack

import numpy as np

import concourse.bass as bass
from concourse import mybir

F32 = mybir.dt.float32
F32R = mybir.dt.float32r
BF16 = mybir.dt.bfloat16
U32 = mybir.dt.uint32
ALU = mybir.AluOpType
ACT = mybir.ActivationFunctionType
AX_X = mybir.AxisListType.X

P = 128
B, D, N = 8, 64, 64
T = B * N
NC = T // P
KC = 3 * 16 * 16 // P
HF = 256
NE = 8
HID = int(8 / 3 * D)
HC = -(-NE * HID // P)
HALF = T // 2
CAP = -(-5 * T // (4 * NE))
NEG = -1e30
FLOAT_MAX = float(np.finfo(np.float32).max)
INF_TO = 1e4


def layout(parts):
    at, n = {}, 0
    for name, width in parts:
        at[name] = (n, n + width)
        n += width
    return at, n


ROWS, ROWS_N = layout([("ln_w", D), ("ln_b", D), ("pe", D), ("ff_b2", D), ("ln1_g", D), ("ln1_b", D),
                       ("ln2_g", D), ("ln2_b", D)])
COLS, COLS_N = layout([("conv_b", 1), ("ff_b2", 1), ("ln1_w", 1), ("ln2_w", 1), ("moe_b1", 2 * NE)])
W65, W65_N = layout([("ff1", HF), ("q8", P), ("k8", P), ("v8", D), ("proj", D), ("aq", D), ("ak", D), ("av", D),
                     ("l1w1", D), ("l1w2", D), ("gate", NE)])
W64, W64_N = layout([("fq", P), ("fqr", P), ("fk", P), ("fkr", P), ("fv", D), ("fo", D), ("router", NE),
                     ("lq", D), ("lkv", P)])
CON, CON_N = layout([("ident", P), ("mask8", 8), ("vmask8", D), ("mask4", 4), ("vmask4", D), ("cos", N),
                     ("sin", N), ("causal", N), ("pair", P), ("bm", 72), ("iota8", NE), ("slots", CAP),
                     ("slotid", 1), ("expert", NE)])


def vit_tower(nc: bass.Bass, pat, wconv, rows, cols, w65, w64, ff2, f13, fw2, m1, m2, mb2, con, sel, tri, out):
    with ExitStack() as ctx:
        def sb(name, shape, dt=F32):
            return ctx.enter_context(nc.sbuf_tensor(name, shape, dt))

        def sem(name):
            return ctx.enter_context(nc.semaphore(name))

        ps = ctx.enter_context(nc.psum_tensor("ps", [P, 8, 512], F32))

        rows_s = sb("rows_s", [P, ROWS_N])
        cols_s = sb("cols_s", [P, COLS_N])
        w65_s = sb("w65_s", [D + 1, W65_N])
        w64_s = sb("w64_s", [D, W64_N])
        ff2_s = sb("ff2_s", [P, 2, D])
        fw2_s = sb("fw2_s", [P, HC, D])
        m2_s = sb("m2_s", [P, NE, 2, D])
        mb2_s = sb("mb2_s", [CAP, NE, D])
        con_s = sb("con_s", [P, CON_N])
        sel_s = sb("sel_s", [3 * NE, HC * P], BF16)
        tri_s = sb("tri_s", [P, 2, P], BF16)

        def row(name):
            return rows_s[:, ROWS[name][0]:ROWS[name][1]]

        def col(name, n=P):
            return cols_s[0:n, COLS[name][0]:COLS[name][1]]

        def w5(name):
            return w65_s[:, W65[name][0]:W65[name][1]]

        def w4(name):
            return w64_s[:, W64[name][0]:W64[name][1]]

        def con_(name, n=P):
            return con_s[0:n, CON[name][0]:CON[name][1]]

        ident = con_("ident")
        f13h = sb("f13h", [P, 2, HC * P], F32R)
        f13l = sb("f13l", [P, 2, HC * P], F32R)
        m1h = sb("m1h", [P, NE, 2 * P], F32R)
        m1l = sb("m1l", [P, NE, 2 * P], F32R)

        lnb_pe = sb("lnb_pe", [P, D])
        mhalf = sb("mhalf", [P, 2 * NC])

        def stats_tiles(name):
            return sb(name + "_st", [P, NC, 6]), sb(name + "_mv", [P, NC, 2]), sb(name + "_ve", [P, NC, 2]), \
                sb(name + "_rs", [P, NC, 2])

        ln = {k: stats_tiles(k) for k in ("emb", "pre_attn", "pre_ffn", "rms", "pre_l1", "l1a", "l1b", "pre_moe")}
        yn = sb("yn", [P, NC, D])
        h0 = sb("h0", [P, NC, D])
        mx8 = sb("mx8", [P, NC, 8])
        ri8 = sb("ri8", [P, NC, 4, 2])
        o8 = sb("o8", [P, NC, D])
        h1 = sb("h1", [P, NC, D])
        h1b = sb("h1b", [P, NC, D])
        h2 = sb("h2", [P, NC, D])
        n2 = sb("n2", [P, NC, D])
        av = sb("av", [P, NC, D])
        nmx = sb("nmx", [P, NC])
        suma = sb("suma", [P, NC])
        ria = sb("ria", [P, NC])
        h3 = sb("h3", [P, NC, D])
        x3 = sb("x3", [P, NC, D])
        r3 = sb("r3", [P, NC, D])
        q4_bd = sb("q4_bd", [P, NC, P])
        k4 = sb("k4", [P, NC, N])
        v4 = sb("v4", [P, B, 2, 34])
        mx4 = sb("mx4", [P, NC, 4])
        ri4 = sb("ri4", [P, NC, 2, 2])
        o4 = sb("o4", [P, NC, D])
        x4 = sb("x4", [P, NC, D])
        hx = sb("hx", [P, NC, D])
        fl = sb("fl", [P, NC, 2, D])
        flT = sb("flT", [P, T])
        fs = sb("fs", [P, T], F32R)
        top8 = sb("top8", [P, NC, 8])
        topi = sb("topi", [P, NC, 8], U32)
        topf = sb("topf", [P, NC, 8])
        lse = sb("lse", [P, NC, 8])
        lexp = sb("lexp", [P, NC, 8])
        lsum = sb("lsum", [P, NC])
        oh = sb("oh", [P, NC, 8])
        oh2 = sb("oh2", [P, NC, 8])
        wsel = sb("wsel", [P, NC, 8])
        wtot = sb("wtot", [P, NC])
        wden = sb("wden", [P, NC])
        winv = sb("winv", [P, NC])
        gat = sb("gat", [P, NC, 8])
        gpart = sb("gpart", [P, NC, 3, 8])
        gbf = sb("gbf", [P, NC, 2, 8], BF16)
        grem = sb("grem", [P, NC, 8])
        gT = sb("gT", [3 * NE, T], BF16)
        h4 = sb("h4", [P, NC, D])
        x5 = sb("x5", [P, NC, D])
        v1 = sb("v1", [P, NC, 2, 72])
        zden = sb("zden", [P, NC, 8])
        z = sb("z", [P, NC, 8])
        x1T = sb("x1T", [D + 1, T])
        g5 = sb("g5", [D + 1, T])
        h5 = sb("h5", [P, NC, D])
        x7T = sb("x7T", [D + 1, T])
        lg = sb("lg", [P, NC, 8])
        top1 = sb("top1", [P, NC, 8])
        toi1 = sb("toi1", [P, NC, 8], U32)
        tof1 = sb("tof1", [P, NC, 8])
        lse1 = sb("lse1", [P, NC, 8])
        lex1 = sb("lex1", [P, NC, 8])
        lsu1 = sb("lsu1", [P, NC])
        prob = sb("prob", [P, NC])
        oh1 = sb("oh1", [P, NC, 8])
        oh1b = sb("oh1b", [P, NC, 8], BF16)
        code = sb("code", [P, NC])

        with ExitStack() as first_stages:
            def early(name, shape, dt=F32):
                return first_stages.enter_context(nc.sbuf_tensor(name, shape, dt))

            pat_s = early("pat_s", [P, KC, T])
            wconv_s = early("wconv_s", [P, KC, D])
            conv_f = early("conv_f", [D, T])
            g0 = early("g0", [P, 2, T])
            k8x = early("k8x", [P, NC, 8, N])
            s8 = early("s8", [P, NC, 8, N])
            pT8 = early("pT8", [P, NC, 4, P])
            v8 = early("v8", [P, B, 4, 18])
            q_bd = early("q_bd", [P, NC, P])
            k8 = early("k8", [P, NC, N])
            sel_f = early("sel_f", [3 * NE, HC * P])
            tri_f = early("tri_f", [P, 2, P])
            f13_s = early("f13_s", [P, 2, HC * P])
            m1_s = early("m1_s", [P, NE, 2 * P])
            rope = early("rope", [P, 2, NC, 2, N])
            aqk = early("aqk", [D, 2, T])
            sa = early("sa", [P, NC, P])
            paT = early("paT", [P, NC, P])
            h0T = early("h0T", [D + 1, T])
            fT = early("fT", [D + 1, T])
            o8T = early("o8T", [D + 1, T])
            o4T = early("o4T", [D, T])
            r3T = early("r3T", [D, T])

            k4x, s4, pT4 = k8x[:, :, 0:4, :], s8[:, :, 0:4, :], pT8[:, :, 0:2, :]

        moeT = sb("moeT", [D, T])
        x5T = sb("x5T", [D, T])
        eq = sb("eq", [D, T])
        rq = sb("rq", [D, T])
        phq = sb("phq", [D, T])
        ek = sb("ek", [P, NC, D])
        rk = sb("rk", [P, NC, D])
        phk = sb("phk", [P, NC, D])
        t5 = sb("t5", [P, NC, D])
        y5 = sb("y5", [P, NC, D])
        yn5 = sb("yn5", [P, NC, D])
        x1 = sb("x1", [P, NC, D])
        y6 = sb("y6", [P, NC, D])
        yn6 = sb("yn6", [P, NC, D])
        ln6 = sb("ln6", [P, NC, D])
        asil = sb("asil", [P, 2, T])
        hgb = sb("hgb", [P, 2, T])
        kv = sb("kv", [D, B, 72])
        x7 = sb("x7", [P, NC, D])
        x7s = sb("x7s", [P, NC, 2, D], F32R)
        disp = sb("disp", [P, NC, NE, CAP], F32R)
        bufT = sb("bufT", [P, NE, CAP], F32R)
        codb = sb("codb", [CAP, T])
        combT = sb("combT", [CAP, NE, T], F32R)
        hid = sb("hid", [P, NE, 2, CAP])
        ybf = sb("ybf", [CAP, NE, D])
        ybs = sb("ybs", [CAP, NE, 2, D], F32R)
        yt1 = sb("yt1", [P, NC, D])
        yt2 = sb("yt2", [P, NC, D])
        yt3 = sb("yt3", [P, NC, D])
        finite = sb("finite", [P, NC, D], U32)
        above = sb("above", [P, NC, D])
        below = sb("below", [P, NC, D])
        ynum = sb("ynum", [P, NC, D])
        h6 = sb("h6", [P, NC, D])
        posn = sb("posn", [P, NC, 8])
        codt = sb("codt", [P, NC, 8])
        keep = sb("keep", [P, NC, 8])

        in_conv, in_pat, in_small, in_w, in_big = sem("in_conv"), [sem("in_pat0"), sem("in_pat1")], \
            sem("in_small"), sem("in_w"), sem("in_big")
        out_stored = sem("out_stored")
        dve_step, act_step, pool_step = sem("dve_step"), sem("act_step"), sem("pool_step")
        S = {}
        for name in """setup mconst conv_ps conv_f conv_t emb_ve emb_rs h0 h0_ps h0T ff1a_ps g0 ff2a_ps fT qk8_ps v8_ps
            k8 k8x v8 s8_ps s8 p8 pT8_ps pT8 o8_ps o8 o8T_ps o8T proj_ps h1 h1T_ps h1T ff1b_ps g1 ff2b_ps h2
            a_ve a_rs n2 n2T_ps n2T aqk_ps av_ps aqk av sa_ps sa pa paT_ps paT oa_ps h3 f_ve f_rs r3 r3T_ps
            r3T q4_ps k4_ps v4_ps q4bd k4x v4 s4_ps s4 p4 pT4_ps pT4 o4_ps o4 o4T_ps o4T wo_ps x4 r_ve r_rs
            fl flT_ps fs rt_ps lse lexp gpart gT_ps gT split a_ps b_ps gc_ps asil hgb moe_ps moeT moeTb_ps
            h4 l_ve l_rs x5 x5T_ps x5T lq_ps lkv_ps eq ek phq phk kv_ps kv t5_ps y5 m_ve m_rs x1 x1T_ps x1T
            l1h_ps g5 l1y_ps y6 n_ve n_rs e_ve e_rs x7 x7T_ps x7T g_ps lse1 lex1 oh1b cum_ps disp bufT_ps
            bufT code cod_ps codb combT hid_ps hid y_ps ybs comb_ps h6""".split():
            S[name] = sem(name)

        block = ctx.enter_context(nc.Block())

        def half(h):
            return slice(h * HALF, (h + 1) * HALF)

        def chunks(h):
            return slice(2 * h, 2 * h + 2)

        def tok(c):
            return slice(c * P, (c + 1) * P)

        def bank(h, i):
            return ps[:, 4 * h + i, :]

        @block.sync
        def _(sp):
            sp.dma_start(wconv_s[:], wconv).then_inc(in_conv, 16)
            sp.dma_start(pat_s[:, :, half(0)], pat[:, :, half(0)]).then_inc(in_pat[0], 16)
            sp.dma_start(con_s[:], con).then_inc(in_small, 16)
            sp.dma_start(cols_s[:], cols).then_inc(in_small, 16)
            sp.dma_start(rows_s[:], rows).then_inc(in_small, 16)
            sp.dma_start(pat_s[:, :, half(1)], pat[:, :, half(1)]).then_inc(in_pat[1], 16)
            sp.dma_start(w65_s[:], w65).then_inc(in_w, 16)
            sp.dma_start(ff2_s[:], ff2).then_inc(in_w, 16)
            sp.dma_start(w64_s[:], w64).then_inc(in_w, 16)
            sp.dma_start(f13_s[:], f13).then_inc(in_big, 16)
            sp.dma_start(m1_s[:], m1).then_inc(in_big, 16)
            sp.dma_start(fw2_s[:], fw2).then_inc(in_big, 16)
            sp.dma_start(sel_f[:], sel).then_inc(in_big, 16)
            sp.dma_start(m2_s[:], m2).then_inc(in_big, 16)
            sp.dma_start(mb2_s[:], mb2).then_inc(in_big, 16)
            sp.dma_start(tri_f[:], tri).then_inc(in_big, 16)
            sp.wait_ge(S["h6"], 2)
            sp.dma_start(out.rearrange("(c p) d -> p c d", p=P), h6[:]).then_inc(out_stored, 16)
            sp.wait_ge(out_stored, 16)

        @block.gpsimd
        def _(pool):
            pool.memset(mhalf[:], -0.5).then_inc(S["mconst"], 1)
            pool.memset(q_bd[:], 0.0)
            pool.memset(q4_bd[:], 0.0)
            pool.memset(v1[:], 0.0).then_inc(S["setup"], 1)

            def rsqrt(name, ve_ready, rs_ready, n):
                for h in range(2):
                    pool.wait_ge(S[ve_ready], h + 1)
                    ve, rs = ln[name][2], ln[name][3]
                    pool.tensor_tensor(rs[:, chunks(h), 0:n], ve[:, chunks(h), 0:n],
                                       mhalf[:, 0:2 * n].rearrange("p (c n) -> p c n", n=n),
                                       ALU.pow).then_inc(S[rs_ready], 1)

            pool.wait_ge(S["mconst"], 1)
            rsqrt("emb", "emb_ve", "emb_rs", 1)
            pool.wait_ge(in_big, 16 * 7)
            pool.tensor_copy(sel_s[:], sel_f[:])
            pool.tensor_copy(tri_s[:], tri_f[:]).then_inc(S["split"], 1)
            pool.wait_ge(S["split"], 3)
            for j in range(2):
                pool.tensor_tensor(f13l[:, j], f13_s[:, j], f13h[:, j], ALU.subtract)
            pool.tensor_tensor(m1l[:], m1_s[:], m1h[:], ALU.subtract).then_inc(S["split"], 1)
            rsqrt("pre_attn", "a_ve", "a_rs", 1)
            rsqrt("pre_ffn", "f_ve", "f_rs", 2)
            rsqrt("rms", "r_ve", "r_rs", 1)
            rsqrt("pre_l1", "l_ve", "l_rs", 1)
            rsqrt("l1a", "m_ve", "m_rs", 1)
            rsqrt("l1b", "n_ve", "n_rs", 1)
            rsqrt("pre_moe", "e_ve", "e_rs", 1)

        @block.vector
        def _(dve):
            steps = [0]

            def link(ins):
                steps[0] += 1
                ins.then_inc(dve_step, 1)
                dve.wait_ge(dve_step, steps[0])

            def stats(name, src, h, eps, ready):
                st, mv_, ve, _ = ln[name]
                for c in range(2 * h, 2 * h + 2):
                    last = dve.bn_stats(st[:, c, :], src[:, c - 2 * h, :])
                link(last)
                for c in range(2 * h, 2 * h + 2):
                    last = dve.bn_aggr(mv_[:, c, :], st[:, c, :])
                link(last)
                dve.tensor_scalar(ve[:, chunks(h), 0:1], mv_[:, chunks(h), 1:2], eps, None,
                                  ALU.add).then_inc(S[ready], 1)

            def mean(name, c):
                return ln[name][1][:, c, 0:1]

            def rstd(name, c, i=0):
                return ln[name][3][:, c, i:i + 1]

            for tile in (h0T, fT, o8T, x1T, g5, x7T):
                dve.memset(tile[D:D + 1, :], 1.0)
            dve.memset(v8[:, :, :, 16:18], 0.0)
            link(dve.memset(v4[:, :, :, 32:34], 0.0))
            for i in range(2):
                dve.memset(v8[i * N:(i + 1) * N, :, :, 16 + i:17 + i], 1.0)
                last = dve.memset(v4[i * N:(i + 1) * N, :, :, 32 + i:33 + i], 1.0)
            last.then_inc(S["setup"], 1)
            dve.wait_ge(in_small, 48)
            link(dve.tensor_tensor(lnb_pe[:], row("ln_b"), row("pe"), ALU.add))

            for h in range(2):
                dve.wait_ge(S["conv_t"], h + 1)
                stats("emb", bank(h, 1)[:, 0:P].rearrange("p (c d) -> p c d", c=2), h, 1e-5, "emb_ve")
            for h in range(2):
                dve.wait_ge(S["emb_rs"], h + 1)
                for c in range(2 * h, 2 * h + 2):
                    src = bank(h, 1)[:, (c % 2) * D:(c % 2 + 1) * D]
                    last = dve.scalar_tensor_tensor(yn[:, c, :], src, mean("emb", c), row("ln_w"), ALU.subtract,
                                                    ALU.mult)
                link(last)
                for c in range(2 * h, 2 * h + 2):
                    last = dve.scalar_tensor_tensor(h0[:, c, :], yn[:, c, :], rstd("emb", c), lnb_pe[:], ALU.mult,
                                                    ALU.add)
                last.then_inc(S["h0"], 1)

            dve.wait_ge(in_big, 16 * 7)
            for j in range(2):
                last = dve.tensor_copy(f13h[:, j], f13_s[:, j])
            last.then_inc(S["split"], 1)
            dve.tensor_copy(m1h[:], m1_s[:]).then_inc(S["split"], 1)

            dve.wait_ge(S["setup"], 2)
            for h in range(2):
                dve.wait_ge(S["qk8_ps"], h + 1)
                pq = bank(h, 1).rearrange("p (w c i t) -> p w c i t", w=2, c=2, i=2)
                for i in range(2):
                    rr = slice(i * D, (i + 1) * D)
                    dve.tensor_copy(k8[rr, chunks(h), :], pq[rr, 1, :, i, :])
                    last = dve.tensor_copy(q_bd[rr, chunks(h), i * N:(i + 1) * N], pq[rr, 0, :, i, :])
                link(last)
                dve.tensor_tensor(k8x[:, chunks(h)],
                                  k8[:, chunks(h), :].unsqueeze(2).to_broadcast([P, 2, 8, N]),
                                  con_("mask8").unsqueeze(1).unsqueeze(3).to_broadcast([P, 2, 8, N]),
                                  ALU.mult).then_inc(S["k8x"], 1)
                dve.wait_ge(S["v8_ps"], h + 1)
                dve.tensor_tensor(v8[:, 4 * h:4 * h + 4, :, 0:16],
                                  bank(h, 2)[:, 0:4 * D].rearrange("p (b g d) -> p b g d", b=4, g=4),
                                  con_("vmask8").rearrange("p (g d) -> p g d", g=4).unsqueeze(1)
                                  .to_broadcast([P, 4, 4, 16]), ALU.mult).then_inc(S["v8"], 1)
            for c in range(NC):
                h = c // 2
                src = bank(h, (3, 0)[c % 2]).rearrange("p (g k) -> p g k", g=8)
                dve.wait_ge(S["s8_ps"], c + 1)
                link(dve.tensor_reduce(mx8[:, c, :], src, AX_X, ALU.max))
                dve.tensor_tensor(s8[:, c], src, mx8[:, c, :].unsqueeze(2).to_broadcast([P, 8, N]),
                                  ALU.subtract).then_inc(S["s8"], 1)
            for c in range(NC):
                dve.wait_ge(S["pT8_ps"], c + 1)
                dve.tensor_copy(pT8[:, c], bank(c // 2, (1, 2)[c % 2]).rearrange("p (g t) -> p g t", g=4)).then_inc(
                    S["pT8"], 1)
            for c in range(NC):
                dve.wait_ge(S["o8_ps"], 2 * (c // 2) + 2)
                src = bank(c // 2, 3)[:, (c % 2) * 72:(c % 2 + 1) * 72].rearrange("p (g d) -> p g d", g=4)
                link(dve.reciprocal(ri8[:, c], src[:, :, 16:18]))
                dve.tensor_tensor(o8[:, c, :].rearrange("p (g i d) -> p g i d", g=4, i=2),
                                  src[:, :, 0:16].rearrange("p g (i d) -> p g i d", i=2),
                                  ri8[:, c].unsqueeze(3).to_broadcast([P, 4, 2, 8]), ALU.mult).then_inc(S["o8"], 1)
            for h in range(2):
                dve.wait_ge(S["proj_ps"], h + 1)
                dve.tensor_tensor(h1[:, chunks(h)], bank(h, 1)[:, 0:P].rearrange("p (c d) -> p c d", c=2),
                                  h0[:, chunks(h)], ALU.add).then_inc(S["h1"], 1)
            for h in range(2):
                dve.wait_ge(S["h1"], h + 1)
                link(dve.tensor_tensor(h1b[:, chunks(h)], h1[:, chunks(h)],
                                       row("ff_b2").unsqueeze(1).to_broadcast([P, 2, D]), ALU.add))
            for h in range(2):
                dve.wait_ge(S["ff2b_ps"], h + 1)
                link(dve.tensor_tensor(h2[:, chunks(h)], bank(h, 0)[:, 0:P].rearrange("p (c d) -> p c d", c=2),
                                       h1b[:, chunks(h)], ALU.add))
                stats("pre_attn", h2[:, chunks(h)], h, 1e-5, "a_ve")
            for h in range(2):
                dve.wait_ge(S["a_rs"], h + 1)
                for c in range(2 * h, 2 * h + 2):
                    last = dve.tensor_scalar(n2[:, c], h2[:, c], mean("pre_attn", c), rstd("pre_attn", c),
                                             ALU.subtract, ALU.mult)
                last.then_inc(S["n2"], 1)

            for h in range(2):
                dve.wait_ge(S["av_ps"], h + 1)
                dve.tensor_copy(av[:, chunks(h)], bank(h, 3)[:, 0:P].rearrange("p (c d) -> p c d", c=2)).then_inc(
                    S["av"], 1)
            for h in range(2):
                dve.wait_ge(S["sa_ps"], h + 1)
                for c in range(2 * h, 2 * h + 2):
                    last = dve.scalar_tensor_tensor(sa[:, c], bank(h, 0)[:, (c % 2) * P:(c % 2 + 1) * P],
                                                    float(D) ** -0.5, con_("pair"), ALU.mult, ALU.add)
                link(last)
                dve.tensor_reduce(nmx[:, chunks(h)], sa[:, chunks(h)], AX_X, ALU.max, negate=True).then_inc(S["sa"], 1)
            for h in range(2):
                dve.wait_ge(S["paT_ps"], h + 1)
                dve.tensor_copy(paT[:, chunks(h)], bank(h, 1)[:, 0:2 * P].rearrange("p (c d) -> p c d", c=2)).then_inc(
                    S["paT"], 1)
            for h in range(2):
                dve.wait_ge(S["pa"], 2 * h + 2)
                link(dve.reciprocal(ria[:, chunks(h)], suma[:, chunks(h)]))
                dve.wait_ge(S["oa_ps"], h + 1)
                for c in range(2 * h, 2 * h + 2):
                    last = dve.scalar_tensor_tensor(h3[:, c], bank(h, 2)[:, (c % 2) * D:(c % 2 + 1) * D],
                                                    ria[:, c:c + 1], h2[:, c], ALU.mult, ALU.add)
                last.then_inc(S["h3"], 1)
            for h in range(2):
                dve.wait_ge(S["h3"], h + 1)
                st, mv_, ve, _ = ln["pre_ffn"]
                for c in range(2 * h, 2 * h + 2):
                    last = dve.bn_stats(st[:, c, :], h3[:, c, :])
                link(last)
                for c in range(2 * h, 2 * h + 2):
                    last = dve.bn_aggr(mv_[:, c, :], st[:, c, :])
                link(last)
                dve.tensor_scalar(ve[:, chunks(h), 0:1], mv_[:, chunks(h), 1:2], 1e-5, None, ALU.add)
                dve.tensor_scalar(ve[:, chunks(h), 1:2], mv_[:, chunks(h), 1:2], 1.0 + 1e-6, 1e-11, ALU.mult,
                                  ALU.add).then_inc(S["f_ve"], 1)
            for h in range(2):
                dve.wait_ge(S["f_rs"], h + 1)
                for c in range(2 * h, 2 * h + 2):
                    last = dve.tensor_scalar(r3[:, c], h3[:, c], mean("pre_ffn", c), rstd("pre_ffn", c, 1),
                                             ALU.subtract, ALU.mult)
                last.then_inc(S["r3"], 1)
                for c in range(2 * h, 2 * h + 2):
                    last = dve.tensor_scalar(x3[:, c], h3[:, c], mean("pre_ffn", c), rstd("pre_ffn", c),
                                             ALU.subtract, ALU.mult)
                link(last)
            for h in range(2):
                for w, ready in ((0, "q4_ps"), (1, "k4_ps")):
                    dve.wait_ge(S[ready], h + 1)
                    src = bank(h, w).rearrange("p (r c i t) -> p r c i t", r=2, c=2, i=2)
                    for i in range(2):
                        rr = slice(i * D, (i + 1) * D)
                        dve.tensor_tensor(rope[rr, w, chunks(h), 0, :], src[rr, 0, :, i, :],
                                          con_s[rr, CON["cos"][0]:CON["cos"][1]].unsqueeze(1).to_broadcast([D, 2, N]),
                                          ALU.mult)
                        last = dve.tensor_tensor(
                            rope[rr, w, chunks(h), 1, :], src[rr, 1, :, i, :],
                            con_s[rr, CON["sin"][0]:CON["sin"][1]].unsqueeze(1).to_broadcast([D, 2, N]), ALU.mult)
                    link(last)
                    if w == 0:
                        for i in range(2):
                            rr = slice(i * D, (i + 1) * D)
                            last = dve.tensor_tensor(q4_bd[rr, chunks(h), i * N:(i + 1) * N],
                                                     rope[rr, 0, chunks(h), 0, :], rope[rr, 0, chunks(h), 1, :], ALU.add)
                        last.then_inc(S["q4bd"], 1)
                    else:
                        link(dve.tensor_tensor(k4[:, chunks(h)], rope[:, 1, chunks(h), 0, :],
                                               rope[:, 1, chunks(h), 1, :], ALU.add))
                        dve.tensor_tensor(k4x[:, chunks(h)],
                                          k4[:, chunks(h), :].unsqueeze(2).to_broadcast([P, 2, 4, N]),
                                          con_("mask4").unsqueeze(1).unsqueeze(3).to_broadcast([P, 2, 4, N]),
                                          ALU.mult).then_inc(S["k4x"], 1)
                dve.wait_ge(S["v4_ps"], h + 1)
                dve.tensor_tensor(v4[:, 4 * h:4 * h + 4, :, 0:32],
                                  bank(h, 2)[:, 0:4 * D].rearrange("p (b g d) -> p b g d", b=4, g=2),
                                  con_("vmask4").rearrange("p (g d) -> p g d", g=2).unsqueeze(1)
                                  .to_broadcast([P, 4, 2, 32]), ALU.mult).then_inc(S["v4"], 1)
            for c in range(NC):
                dve.wait_ge(S["s4_ps"], 2 * (c // 2) + 2)
                src = bank(c // 2, 3)[:, (c % 2) * 256:(c % 2 + 1) * 256].rearrange("p (g k) -> p g k", g=4)
                link(dve.tensor_tensor(s4[:, c], src, con_("causal").unsqueeze(1).to_broadcast([P, 4, N]), ALU.add))
                link(dve.tensor_reduce(mx4[:, c, :], s4[:, c], AX_X, ALU.max))
                dve.tensor_tensor(s4[:, c], s4[:, c], mx4[:, c, :].unsqueeze(2).to_broadcast([P, 4, N]),
                                  ALU.subtract).then_inc(S["s4"], 1)
            for c in range(NC):
                dve.wait_ge(S["o4_ps"], 2 * (c // 2) + 2)
                src = bank(c // 2, 1)[:, (c % 2) * 68:(c % 2 + 1) * 68].rearrange("p (g d) -> p g d", g=2)
                link(dve.reciprocal(ri4[:, c], src[:, :, 32:34]))
                dve.tensor_tensor(o4[:, c, :].rearrange("p (g i d) -> p g i d", g=2, i=2),
                                  src[:, :, 0:32].rearrange("p g (i d) -> p g i d", i=2),
                                  ri4[:, c].unsqueeze(3).to_broadcast([P, 2, 2, 16]), ALU.mult).then_inc(S["o4"], 1)
            for h in range(2):
                dve.wait_ge(S["wo_ps"], h + 1)
                link(dve.tensor_tensor(x4[:, chunks(h)], bank(h, 3)[:, 0:P].rearrange("p (c d) -> p c d", c=2),
                                       x3[:, chunks(h)], ALU.add))
                st, mv_, ve, _ = ln["rms"]
                for c in range(2 * h, 2 * h + 2):
                    last = dve.bn_stats(st[:, c, :], x4[:, c, :])
                link(last)
                for c in range(2 * h, 2 * h + 2):
                    last = dve.bn_aggr(mv_[:, c, :], st[:, c, :])
                link(last)
                link(dve.tensor_tensor(ve[:, chunks(h), 1:2], mv_[:, chunks(h), 0:1], mv_[:, chunks(h), 0:1],
                                       ALU.mult))
                dve.scalar_tensor_tensor(ve[:, chunks(h), 0], mv_[:, chunks(h), 1], 1e-6,
                                         ve[:, chunks(h), 1], ALU.add, ALU.add).then_inc(S["r_ve"], 1)
            for h in range(2):
                dve.wait_ge(S["r_rs"], h + 1)
                for c in range(2 * h, 2 * h + 2):
                    last = dve.tensor_scalar(fl[:, c], x4[:, c].unsqueeze(1).to_broadcast([P, 2, D]),
                                             rstd("rms", c), None, ALU.mult)
                last.then_inc(S["fl"], 1)
            for h in range(2):
                dve.wait_ge(S["flT_ps"], h + 1)
                link(dve.tensor_scalar(flT[:, half(h)], bank(h, 0)[:, 0:HALF], col("ln2_w"), None, ALU.mult))
                link(dve.tensor_copy(fs[:, half(h)], flT[:, half(h)]))
                dve.tensor_tensor(fs[D:P, half(h)], flT[D:P, half(h)], fs[D:P, half(h)],
                                  ALU.subtract).then_inc(S["fs"], 1)
            for h in range(2):
                cs = chunks(h)
                dve.wait_ge(S["rt_ps"], h + 1)
                src = bank(h, 1)[:, 0:16].rearrange("p (c e) -> p c e", c=2)
                for c in range(2):
                    last = dve.max(top8[:, 2 * h + c, :], src[:, c, :])
                link(last)
                dve.tensor_tensor(lse[:, cs], src, top8[:, cs, 0:1].to_broadcast([P, 2, 8]),
                                  ALU.subtract).then_inc(S["lse"], 1)
                for c in range(2):
                    last = dve.max_index(topi[:, 2 * h + c, :], top8[:, 2 * h + c, :], src[:, c, :])
                link(last)
                link(dve.tensor_copy(topf[:, cs], topi[:, cs]))
                iota = con_("iota8").unsqueeze(1).to_broadcast([P, 2, 8])
                dve.tensor_tensor(oh[:, cs], iota, topf[:, cs, 0:1].to_broadcast([P, 2, 8]), ALU.is_equal)
                link(dve.tensor_tensor(oh2[:, cs], iota, topf[:, cs, 1:2].to_broadcast([P, 2, 8]), ALU.is_equal))
                link(dve.tensor_tensor(oh[:, cs], oh[:, cs], oh2[:, cs], ALU.add))
                dve.wait_ge(S["lexp"], h + 1)
                dve.tensor_tensor(wsel[:, cs], lexp[:, cs], oh[:, cs], ALU.mult)
                link(dve.tensor_reduce(lsum[:, cs], lexp[:, cs], AX_X, ALU.add))
                link(dve.tensor_reduce(wtot[:, cs], wsel[:, cs], AX_X, ALU.add))
                link(dve.scalar_tensor_tensor(wden[:, cs], lsum[:, cs], 1e-9, wtot[:, cs], ALU.mult, ALU.add))
                link(dve.reciprocal(winv[:, cs], wden[:, cs]))
                link(dve.tensor_tensor(gat[:, cs], wsel[:, cs], winv[:, cs].unsqueeze(2).to_broadcast([P, 2, 8]),
                                       ALU.mult))
                link(dve.tensor_copy(gbf[:, cs, 0], gat[:, cs]))
                dve.tensor_copy(gpart[:, cs, 0], gbf[:, cs, 0])
                link(dve.tensor_tensor(grem[:, cs], gat[:, cs], gbf[:, cs, 0], ALU.subtract))
                link(dve.tensor_copy(gbf[:, cs, 1], grem[:, cs]))
                dve.tensor_copy(gpart[:, cs, 1], gbf[:, cs, 1])
                dve.tensor_tensor(gpart[:, cs, 2], grem[:, cs], gbf[:, cs, 1],
                                  ALU.subtract).then_inc(S["gpart"], 1)
            for i in range(HC):
                dve.wait_ge(S["asil"], i + 1)
                dve.wait_ge(S["gc_ps"], i + 1)
                link(dve.tensor_tensor(asil[:, i % 2], asil[:, i % 2], ps[:, (1, 5)[i % 2], :], ALU.mult))
                dve.wait_ge(S["b_ps"], i + 1)
                if i >= 2:
                    dve.wait_ge(S["moe_ps"], i - 1)
                dve.tensor_tensor(hgb[:, i % 2], asil[:, i % 2], ps[:, (3, 7)[i % 2], :], ALU.mult).then_inc(
                    S["hgb"], 1)
            for h in range(2):
                link(dve.tensor_tensor(hx[:, chunks(h)], h3[:, chunks(h)], x4[:, chunks(h)], ALU.add))
            for h in range(2):
                dve.wait_ge(S["moeTb_ps"], 2)
                link(dve.tensor_tensor(h4[:, chunks(h)],
                                       ps[:, 2, h * P:(h + 1) * P].rearrange("p (c d) -> p c d", c=2),
                                       hx[:, chunks(h)], ALU.add))
                stats("pre_l1", h4[:, chunks(h)], h, 1e-5, "l_ve")
            for h in range(2):
                dve.wait_ge(S["l_rs"], h + 1)
                for c in range(2 * h, 2 * h + 2):
                    last = dve.tensor_scalar(x5[:, c], h4[:, c], mean("pre_l1", c), rstd("pre_l1", c),
                                             ALU.subtract, ALU.mult)
                last.then_inc(S["x5"], 1)
            for i in range(2):
                last = dve.memset(v1[i * N:(i + 1) * N, :, i, D:72], 1.0)
            link(last)
            for h in range(2):
                dve.wait_ge(S["lkv_ps"], h + 1)
                src = bank(h, 1)[:, 0:256].rearrange("p (c w d) -> p c w d", c=2, w=2)
                dve.wait_ge(S["ek"], h + 1)
                for i in range(2):
                    rr = slice(i * N, (i + 1) * N)
                    dve.tensor_copy(v1[rr, chunks(h), i, 0:D], src[rr, :, 1, :])
                dve.scalar_tensor_tensor(phk[:, chunks(h)], ek[:, chunks(h)], 1.0, rk[:, chunks(h)], ALU.min,
                                         ALU.add).then_inc(S["phk"], 1)
                dve.wait_ge(S["eq"], h + 1)
                dve.scalar_tensor_tensor(phq[:, half(h)], eq[:, half(h)], 1.0, rq[:, half(h)], ALU.min,
                                         ALU.add).then_inc(S["phq"], 1)
            for h in range(2):
                dve.wait_ge(S["kv_ps"], h + 1)
                dve.tensor_tensor(kv[:, 4 * h:4 * h + 4],
                                  bank(h, 2)[0:D, 0:288].rearrange("p (b d) -> p b d", b=4),
                                  con_("bm", D).unsqueeze(1).to_broadcast([D, 4, 72]), ALU.mult).then_inc(S["kv"], 1)
            for h in range(2):
                cs = chunks(h)
                dve.wait_ge(S["t5_ps"], h + 1)
                src = bank(h, 3)[:, 0:144].rearrange("p (c d) -> p c d", c=2)
                link(dve.tensor_scalar(zden[:, cs], src[:, :, D:72], 1e-6, None, ALU.add))
                link(dve.reciprocal(z[:, cs], zden[:, cs]))
                link(dve.tensor_tensor(t5[:, cs].rearrange("p c (g d) -> p c g d", g=8),
                                       src[:, :, 0:D].rearrange("p c (g d) -> p c g d", g=8),
                                       z[:, cs].unsqueeze(3).to_broadcast([P, 2, 8, 8]), ALU.mult))
                link(dve.tensor_tensor(y5[:, cs], t5[:, cs], x5[:, cs], ALU.add))
                stats("l1a", y5[:, cs], h, 1e-5, "m_ve")
            for h in range(2):
                dve.wait_ge(S["m_rs"], h + 1)
                for c in range(2 * h, 2 * h + 2):
                    last = dve.scalar_tensor_tensor(yn5[:, c], y5[:, c], mean("l1a", c), row("ln1_g"),
                                                    ALU.subtract, ALU.mult)
                link(last)
                for c in range(2 * h, 2 * h + 2):
                    last = dve.scalar_tensor_tensor(x1[:, c], yn5[:, c], rstd("l1a", c), row("ln1_b"), ALU.mult,
                                                    ALU.add)
                last.then_inc(S["x1"], 1)
            for h in range(2):
                dve.wait_ge(S["l1y_ps"], h + 1)
                dve.wait_ge(S["x1"], h + 1)
                link(dve.tensor_tensor(y6[:, chunks(h)], bank(h, 2)[:, 0:P].rearrange("p (c d) -> p c d", c=2),
                                       x1[:, chunks(h)], ALU.add))
                stats("l1b", y6[:, chunks(h)], h, 1e-5, "n_ve")
            for h in range(2):
                cs = chunks(h)
                dve.wait_ge(S["n_rs"], h + 1)
                for c in range(2 * h, 2 * h + 2):
                    last = dve.scalar_tensor_tensor(yn6[:, c], y6[:, c], mean("l1b", c), row("ln2_g"),
                                                    ALU.subtract, ALU.mult)
                link(last)
                for c in range(2 * h, 2 * h + 2):
                    last = dve.scalar_tensor_tensor(ln6[:, c], yn6[:, c], rstd("l1b", c), row("ln2_b"), ALU.mult,
                                                    ALU.add)
                link(last)
                link(dve.tensor_tensor(h5[:, cs], ln6[:, cs], h4[:, cs], ALU.add))
                stats("pre_moe", h5[:, cs], h, 1e-5, "e_ve")
            for h in range(2):
                cs = chunks(h)
                dve.wait_ge(S["e_rs"], h + 1)
                for c in range(2 * h, 2 * h + 2):
                    last = dve.tensor_scalar(x7[:, c], h5[:, c], mean("pre_moe", c), rstd("pre_moe", c),
                                             ALU.subtract, ALU.mult)
                last.then_inc(S["x7"], 1)
                dve.wait_ge(S["x7"], h + 1)
                link(dve.tensor_copy(x7s[:, cs, 0], x7[:, cs]))
                link(dve.tensor_tensor(x7s[:, cs, 1], x7[:, cs], x7s[:, cs, 0], ALU.subtract))
            for h in range(2):
                cs = chunks(h)
                dve.wait_ge(S["g_ps"], h + 1)
                src = bank(h, 0)[:, 0:16].rearrange("p (c e) -> p c e", c=2)
                for c in range(2):
                    last = dve.max(top1[:, 2 * h + c, :], src[:, c, :])
                link(last)
                dve.tensor_tensor(lse1[:, cs], src, top1[:, cs, 0:1].to_broadcast([P, 2, 8]),
                                  ALU.subtract).then_inc(S["lse1"], 1)
                for c in range(2):
                    last = dve.max_index(toi1[:, 2 * h + c, :], top1[:, 2 * h + c, :], src[:, c, :])
                link(last)
                link(dve.tensor_copy(tof1[:, cs], toi1[:, cs]))
                iota = con_("iota8").unsqueeze(1).to_broadcast([P, 2, 8])
                link(dve.tensor_tensor(oh1[:, cs], iota, tof1[:, cs, 0:1].to_broadcast([P, 2, 8]), ALU.is_equal))
                dve.tensor_copy(oh1b[:, cs], oh1[:, cs]).then_inc(S["oh1b"], 1)
            for h in range(2):
                cs = chunks(h)
                dve.wait_ge(S["cum_ps"], h + 1)
                link(dve.tensor_tensor(posn[:, cs], bank(h, 1)[:, 0:16].rearrange("p (c e) -> p c e", c=2),
                                       oh1[:, cs], ALU.mult))
                for c in range(2 * h, 2 * h + 2):
                    last = dve.tensor_tensor(disp[:, c], con_("slots").unsqueeze(1).to_broadcast([P, NE, CAP]),
                                             posn[:, c].unsqueeze(2).to_broadcast([P, NE, CAP]), ALU.is_equal)
                last.then_inc(S["disp"], 1)
                link(dve.tensor_scalar(keep[:, cs], posn[:, cs], float(CAP), None, ALU.is_le))
                link(dve.tensor_tensor(codt[:, cs], con_("expert").unsqueeze(1).to_broadcast([P, 2, 8]),
                                       posn[:, cs], ALU.add))
                link(dve.tensor_tensor(codt[:, cs], codt[:, cs], oh1[:, cs], ALU.mult))
                link(dve.tensor_tensor(codt[:, cs], codt[:, cs], keep[:, cs], ALU.mult))
                dve.tensor_reduce(code[:, cs], codt[:, cs], AX_X, ALU.add).then_inc(S["code"], 1)
                dve.wait_ge(S["lex1"], h + 1)
                link(dve.tensor_reduce(lsu1[:, cs], lex1[:, cs], AX_X, ALU.add))
                link(dve.reciprocal(prob[:, cs], lsu1[:, cs]))
            dve.wait_ge(S["cod_ps"], 1)
            link(dve.tensor_copy(codb[:], ps[0:CAP, 3, :]))
            for i in range(2):
                dve.wait_ge(S["bufT_ps"], i + 1)
                last = dve.tensor_copy(bufT[:, 4 * i:4 * i + 4],
                                       ps[:, (2, 6)[i], 0:320].rearrange("p (e s) -> p e s", e=4))
                last.then_inc(S["bufT"], 1)
            for e in range(NE):
                last = dve.tensor_scalar(combT[:, e], codb[:], con_("slotid", CAP), float(128 * e), ALU.subtract,
                                         ALU.is_equal)
            last.then_inc(S["combT"], 1)
            dve.wait_ge(S["y_ps"], 1)
            link(dve.tensor_tensor(ybf[:], ps[0:CAP, 5, :].rearrange("p (e d) -> p e d", e=NE), mb2_s[:], ALU.add))
            link(dve.tensor_copy(ybs[:, :, 0], ybf[:]))
            dve.tensor_tensor(ybs[:, :, 1], ybf[:], ybs[:, :, 0], ALU.subtract).then_inc(S["ybs"], 1)
            for h in range(2):
                cs = chunks(h)
                dve.wait_ge(S["comb_ps"], h + 1)
                src = ps[:, (1, 7)[h], 0:256].rearrange("p (c w d) -> p c w d", c=2, w=2)
                link(dve.tensor_copy(yt1[:, cs], src[:, :, 0, :]))
                link(dve.tensor_tensor(yt2[:, cs], src[:, :, 1, :], yt1[:, cs], ALU.add))
                link(dve.tensor_tensor(yt3[:, cs], yt2[:, cs], prob[:, cs].unsqueeze(2).to_broadcast([P, 2, D]),
                                       ALU.mult))
                dve.tensor_scalar(finite[:, cs], yt3[:, cs], 0.0, 0.0, ALU.mult, ALU.is_equal)
                dve.tensor_scalar(above[:, cs], yt3[:, cs], FLOAT_MAX, INF_TO, ALU.is_gt, ALU.mult)
                link(dve.tensor_scalar(below[:, cs], yt3[:, cs], -FLOAT_MAX, -INF_TO, ALU.is_lt, ALU.mult))
                link(dve.tensor_tensor(ynum[:, cs], above[:, cs], below[:, cs], ALU.add))
                link(dve.copy_predicated(ynum[:, cs], finite[:, cs], yt3[:, cs]))
                dve.tensor_tensor(h6[:, cs], ynum[:, cs], h5[:, cs], ALU.add).then_inc(S["h6"], 1)

        @block.scalar
        def _(act):
            def evac(dst, src, ready, n, done, bias=None):
                act.wait_ge(S[ready], n)
                if bias is None:
                    act.activation(dst, src, ACT.Copy).then_inc(S[done], 1)
                else:
                    act.activation(dst, src, ACT.Identity, bias=bias).then_inc(S[done], 1)

            act.wait_ge(in_small, 48)
            for h in range(2):
                evac(conv_f[:, half(h)], bank(h, 0)[0:D, 0:HALF], "conv_ps", h + 1, "conv_f", col("conv_b", D))
            for h in range(2):
                evac(h0T[0:D, half(h)], bank(h, 2)[0:D, 0:HALF], "h0_ps", h + 1, "h0T")
            for h in range(2):
                act.wait_ge(S["ff1a_ps"], h + 1)
                act.activation(g0[:, :, half(h)], bank(h, 3).rearrange("p (j t) -> p j t", j=2),
                               ACT.Gelu_apprx_tanh).then_inc(S["g0"], 1)
            for h in range(2):
                evac(fT[0:D, half(h)], bank(h, 0)[0:D, 0:HALF], "ff2a_ps", h + 1, "fT", col("ff_b2", D))
            for c in range(NC):
                act.wait_ge(S["s8"], c + 1)
                act.activation(s8[:, c], s8[:, c], ACT.Exp).then_inc(S["p8"], 1)
            for h in range(2):
                evac(o8T[0:D, half(h)], bank(h, 0)[0:D, 0:HALF], "o8T_ps", h + 1, "o8T")
            for h in range(2):
                evac(h0T[0:D, half(h)], bank(h, 2)[0:D, 0:HALF], "h1T_ps", h + 1, "h1T")
            for h in range(2):
                act.wait_ge(S["ff1b_ps"], h + 1)
                act.activation(g0[:, :, half(h)], bank(h, 3).rearrange("p (j t) -> p j t", j=2),
                               ACT.Gelu_apprx_tanh).then_inc(S["g1"], 1)
            for h in range(2):
                evac(fT[0:D, half(h)], bank(h, 1)[0:D, 0:HALF], "n2T_ps", h + 1, "n2T")
            for h in range(2):
                evac(aqk[:, :, half(h)], bank(h, 2)[0:D, :].rearrange("p (w t) -> p w t", w=2), "aqk_ps", h + 1, "aqk")
            for h in range(2):
                act.wait_ge(S["sa"], h + 1)
                for c in range(2 * h, 2 * h + 2):
                    act.activation(sa[:, c], sa[:, c], ACT.Exp, bias=nmx[:, c:c + 1],
                                   accum_out=suma[:, c:c + 1]).then_inc(S["pa"], 1)
            for h in range(2):
                act.wait_ge(S["r3T_ps"], h + 1)
                act.activation(r3T[:, half(h)], bank(h, 3)[0:D, 0:HALF], ACT.Copy,
                               scale=col("ln1_w", D)).then_inc(S["r3T"], 1)
            for c in range(NC):
                act.wait_ge(S["s4"], c + 1)
                act.activation(s4[:, c], s4[:, c], ACT.Exp).then_inc(S["p4"], 1)
            for h in range(2):
                evac(pT4[:, chunks(h)], bank(h, 0).rearrange("p (c g t) -> p c g t", c=2, g=2), "pT4_ps", h + 1, "pT4")
            for h in range(2):
                evac(o4T[:, half(h)], bank(h, 2)[0:D, 0:HALF], "o4T_ps", h + 1, "o4T")
            for h in range(2):
                act.wait_ge(S["lse"], h + 1)
                act.activation(lexp[:, chunks(h)], lse[:, chunks(h)], ACT.Exp).then_inc(S["lexp"], 1)
            for h in range(2):
                evac(gT[:, half(h)], bank(h, 2)[0:3 * NE, 0:HALF], "gT_ps", h + 1, "gT")
            for i in range(HC):
                act.wait_ge(S["a_ps"], i + 1)
                if i >= 2:
                    act.wait_ge(S["hgb"], i - 1)
                act.activation(asil[:, i % 2], ps[:, (0, 4)[i % 2], :], ACT.Silu).then_inc(S["asil"], 1)
            act.wait_ge(S["moe_ps"], HC)
            for h in range(2):
                act.activation(moeT[:, half(h)], ps[0:D, 6, half(h)], ACT.Copy).then_inc(S["moeT"], 1)
            for h in range(2):
                evac(x5T[:, half(h)], bank(h, 3)[0:D, 0:HALF], "x5T_ps", h + 1, "x5T")
            for h in range(2):
                act.wait_ge(S["lkv_ps"], h + 1)
                src = bank(h, 1)[:, 0:256].rearrange("p (c w d) -> p c w d", c=2, w=2)[:, :, 0, :]
                act.activation(rk[:, chunks(h)], src, ACT.Relu)
                act.activation(ek[:, chunks(h)], src, ACT.Exp).then_inc(S["ek"], 1)
                act.wait_ge(S["lq_ps"], h + 1)
                act.activation(rq[:, half(h)], bank(h, 0)[0:D, 0:HALF], ACT.Relu)
                act.activation(eq[:, half(h)], bank(h, 0)[0:D, 0:HALF], ACT.Exp).then_inc(S["eq"], 1)
            for h in range(2):
                evac(x1T[0:D, half(h)], bank(h, 0)[0:D, 0:HALF], "x1T_ps", h + 1, "x1T")
            for h in range(2):
                act.wait_ge(S["l1h_ps"], h + 1)
                act.activation(g5[0:D, half(h)], bank(h, 1)[0:D, 0:HALF], ACT.Gelu).then_inc(S["g5"], 1)
            for h in range(2):
                evac(x7T[0:D, half(h)], bank(h, 3)[0:D, 0:HALF], "x7T_ps", h + 1, "x7T")
            for h in range(2):
                act.wait_ge(S["lse1"], h + 1)
                act.activation(lex1[:, chunks(h)], lse1[:, chunks(h)], ACT.Exp).then_inc(S["lex1"], 1)
            for e in range(NE):
                act.wait_ge(S["hid_ps"], e + 1)
                for j in range(2):
                    k = COLS["moe_b1"][0] + 2 * e + j
                    last = act.activation(hid[:, e, j], ps[:, (0, 4)[e % 2], j * CAP:(j + 1) * CAP], ACT.Relu,
                                          bias=cols_s[:, k:k + 1])
                last.then_inc(S["hid"], 1)

        @block.tensor
        def _(pe):
            def flip(dst, src, n=P):
                return pe.transpose(dst, src, con_s[0:n, 0:n])

            pe.wait_ge(in_conv, 16)
            for h in range(2):
                pe.wait_ge(in_pat[h], 16)
                for k in range(KC):
                    last = pe.matmul(bank(h, 0)[0:D, 0:HALF], wconv_s[:, k, :], pat_s[:, k, half(h)],
                                     start=(k == 0), stop=(k == KC - 1))
                last.then_inc(S["conv_ps"], 1)
            pe.wait_ge(in_small, 48)
            for h in range(2):
                pe.wait_ge(S["conv_f"], h + 1)
                for c in range(2):
                    last = flip(bank(h, 1)[:, c * D:(c + 1) * D], conv_f[:, tok(2 * h + c)], D)
                last.then_inc(S["conv_t"], 1)

            def rows_to_features(h, b, src, ready, done, need=None):
                pe.wait_ge(S[ready], need if need else h + 1)
                for c in range(2):
                    last = flip(bank(h, b)[0:D, tok(c)], src[:, 2 * h + c, :])
                last.then_inc(S[done], 1)

            for h in range(2):
                rows_to_features(h, 2, h0, "h0", "h0_ps")
            pe.wait_ge(in_w, 48)
            pe.wait_ge(S["setup"], 2)

            def ff1(h, src, ready, done):
                pe.wait_ge(S[ready], h + 1)
                for j in range(2):
                    last = pe.matmul(bank(h, 3)[:, j * HALF:(j + 1) * HALF], w5("ff1")[:, j * P:(j + 1) * P],
                                     src[:, half(h)], start=True, stop=True)
                last.then_inc(S[done], 1)

            for h in range(2):
                ff1(h, h0T, "h0T", "ff1a_ps")
            for h in range(2):
                pe.wait_ge(S["g0"], h + 1)
                for j in range(2):
                    last = pe.matmul(bank(h, 0)[0:D, 0:HALF], ff2_s[:, j, :], g0[:, j, half(h)],
                                     start=(j == 0), stop=(j == 1))
                last.then_inc(S["ff2a_ps"], 1)
            for h in range(2):
                pe.wait_ge(S["fT"], h + 1)
                pe.matmul(bank(h, 1)[:, 0:HALF], w5("q8"), fT[:, half(h)], start=True, stop=True)
                pe.matmul(bank(h, 1)[:, HALF:T], w5("k8"), fT[:, half(h)], start=True,
                          stop=True).then_inc(S["qk8_ps"], 1)
                for b in range(4):
                    t0 = h * HALF + b * N
                    for i in range(2):
                        last = pe.matmul(bank(h, 2)[i * N:(i + 1) * N, b * D:(b + 1) * D], fT[:, t0:t0 + N],
                                         w5("v8"), start=True, stop=True)
                last.then_inc(S["v8_ps"], 1)
            for c in range(NC):
                pe.wait_ge(S["k8x"], c // 2 + 1)
                pe.matmul(bank(c // 2, (3, 0)[c % 2]), q_bd[:, c, :], k8x[:, c].rearrange("p g k -> p (g k)"),
                          start=True, stop=True).then_inc(S["s8_ps"], 1)
            for c in range(NC):
                pe.wait_ge(S["p8"], c + 1)
                if c % 2:
                    pe.wait_ge(S["v8"], c // 2 + 1)
                for g in range(4):
                    last = flip(bank(c // 2, (1, 2)[c % 2])[:, g * P:(g + 1) * P],
                                s8[:, c].rearrange("p g k -> p (g k)")[:, g * P:(g + 1) * P])
                last.then_inc(S["pT8_ps"], 1)
            for c in range(NC):
                pe.wait_ge(S["pT8"], c + 1)
                pe.wait_ge(S["v8"], c // 2 + 1)
                pe.wait_ge(S["s8"], min(NC, 2 * (c // 2) + 2))
                for i in range(2):
                    for g in range(4):
                        at = (c % 2) * 72 + g * 18
                        last = pe.matmul(bank(c // 2, 3)[i * N:(i + 1) * N, at:at + 18],
                                         pT8[:, c, g, i * N:(i + 1) * N], v8[:, 2 * c + i, g, :], start=True, stop=True)
                last.then_inc(S["o8_ps"], 1)
            for h in range(2):
                rows_to_features(h, 0, o8, "o8", "o8T_ps", 2 * h + 2)
            for h in range(2):
                pe.wait_ge(S["o8T"], h + 1)
                for c in range(2):
                    last = pe.matmul(bank(h, 1)[:, c * D:(c + 1) * D], o8T[:, tok(2 * h + c)], w5("proj"),
                                     start=True, stop=True)
                last.then_inc(S["proj_ps"], 1)
            for h in range(2):
                rows_to_features(h, 2, h1, "h1", "h1T_ps")
            for h in range(2):
                ff1(h, h0T, "h1T", "ff1b_ps")
            for h in range(2):
                pe.wait_ge(S["g1"], h + 1)
                for c in range(2):
                    for j in range(2):
                        last = pe.matmul(bank(h, 0)[:, c * D:(c + 1) * D], g0[:, j, tok(2 * h + c)], ff2_s[:, j, :],
                                         start=(j == 0), stop=(j == 1))
                last.then_inc(S["ff2b_ps"], 1)
            for h in range(2):
                rows_to_features(h, 1, n2, "n2", "n2T_ps")
            for h in range(2):
                pe.wait_ge(S["n2T"], h + 1)
                pe.matmul(bank(h, 2)[0:D, 0:HALF], w5("aq"), fT[:, half(h)], start=True, stop=True)
                pe.matmul(bank(h, 2)[0:D, HALF:T], w5("ak"), fT[:, half(h)], start=True,
                          stop=True).then_inc(S["aqk_ps"], 1)
                for c in range(2):
                    last = pe.matmul(bank(h, 3)[:, c * D:(c + 1) * D], fT[:, tok(2 * h + c)], w5("av"),
                                     start=True, stop=True)
                last.then_inc(S["av_ps"], 1)
            for h in range(2):
                pe.wait_ge(S["aqk"], h + 1)
                for c in range(2):
                    last = pe.matmul(bank(h, 0)[:, c * P:(c + 1) * P], aqk[:, 0, tok(2 * h + c)],
                                     aqk[:, 1, tok(2 * h + c)], start=True, stop=True)
                last.then_inc(S["sa_ps"], 1)
            for h in range(2):
                pe.wait_ge(S["pa"], 2 * h + 2)
                for c in range(2):
                    last = flip(bank(h, 1)[:, c * P:(c + 1) * P], sa[:, 2 * h + c, :])
                last.then_inc(S["paT_ps"], 1)
            for h in range(2):
                pe.wait_ge(S["paT"], h + 1)
                pe.wait_ge(S["av"], h + 1)
                for c in range(2):
                    last = pe.matmul(bank(h, 2)[:, c * D:(c + 1) * D], paT[:, 2 * h + c, :], av[:, 2 * h + c, :],
                                     start=True, stop=True)
                last.then_inc(S["oa_ps"], 1)
            for h in range(2):
                rows_to_features(h, 3, r3, "r3", "r3T_ps")
            for h in range(2):
                pe.wait_ge(S["r3T"], h + 1)
                for w, (a, b, done) in enumerate((("fq", "fqr", "q4_ps"), ("fk", "fkr", "k4_ps"))):
                    pe.matmul(bank(h, w)[:, 0:HALF], w4(a), r3T[:, half(h)], start=True, stop=True)
                    pe.matmul(bank(h, w)[:, HALF:T], w4(b), r3T[:, half(h)], start=True,
                              stop=True).then_inc(S[done], 1)
                for b in range(4):
                    t0 = h * HALF + b * N
                    for i in range(2):
                        last = pe.matmul(bank(h, 2)[i * N:(i + 1) * N, b * D:(b + 1) * D], r3T[:, t0:t0 + N],
                                         w4("fv"), start=True, stop=True)
                last.then_inc(S["v4_ps"], 1)
            for c in range(NC):
                pe.wait_ge(S["k4x"], c // 2 + 1)
                pe.matmul(bank(c // 2, 3)[:, (c % 2) * 256:(c % 2 + 1) * 256], q4_bd[:, c, :],
                          k4x[:, c].rearrange("p g k -> p (g k)"), start=True, stop=True).then_inc(S["s4_ps"], 1)
            for h in range(2):
                for c in range(2 * h, 2 * h + 2):
                    pe.wait_ge(S["p4"], c + 1)
                    for g in range(2):
                        at = (c % 2) * 256 + g * P
                        last = flip(bank(h, 0)[:, at:at + P],
                                    s4[:, c].rearrange("p g k -> p (g k)")[:, g * P:(g + 1) * P])
                last.then_inc(S["pT4_ps"], 1)
            for c in range(NC):
                pe.wait_ge(S["pT4"], c // 2 + 1)
                pe.wait_ge(S["v4"], c // 2 + 1)
                for i in range(2):
                    for g in range(2):
                        at = (c % 2) * 68 + g * 34
                        last = pe.matmul(bank(c // 2, 1)[i * N:(i + 1) * N, at:at + 34],
                                         pT4[:, c, g, i * N:(i + 1) * N], v4[:, 2 * c + i, g, :], start=True, stop=True)
                last.then_inc(S["o4_ps"], 1)
            for h in range(2):
                rows_to_features(h, 2, o4, "o4", "o4T_ps", 2 * h + 2)
            for h in range(2):
                pe.wait_ge(S["o4T"], h + 1)
                for c in range(2):
                    last = pe.matmul(bank(h, 3)[:, c * D:(c + 1) * D], o4T[:, tok(2 * h + c)], w4("fo"),
                                     start=True, stop=True)
                last.then_inc(S["wo_ps"], 1)
            for h in range(2):
                pe.wait_ge(S["fl"], h + 1)
                for c in range(2):
                    last = flip(bank(h, 0)[:, tok(c)], fl[:, 2 * h + c].rearrange("p w d -> p (w d)"))
                last.then_inc(S["flT_ps"], 1)
            for h in range(2):
                pe.wait_ge(S["fs"], h + 1)
                for c in range(2):
                    last = pe.matmul(bank(h, 1)[:, c * NE:(c + 1) * NE], flT[0:D, tok(2 * h + c)], w4("router"),
                                     start=True, stop=True)
                last.then_inc(S["rt_ps"], 1)
            pe.wait_ge(S["split"], 4)

            def up(i):
                if i >= 2:
                    pe.wait_ge(S["asil"], i - 1)
                    pe.wait_ge(S["hgb"], i - 1)
                for j, b, done in ((0, (0, 4)[i % 2], "a_ps"), (1, (3, 7)[i % 2], "b_ps")):
                    pe.matmul(ps[:, b, :], f13h[:, j, i * P:(i + 1) * P], fs[:], start=True, stop=False)
                    pe.matmul(ps[:, b, :], f13l[:, j, i * P:(i + 1) * P], fs[:], start=False,
                              stop=True).then_inc(S[done], 1)

            def gates(i):
                pe.matmul(ps[:, (1, 5)[i % 2], :], sel_s[:, i * P:(i + 1) * P], gT[:], start=True,
                          stop=True).then_inc(S["gc_ps"], 1)

            up(0)
            up(1)
            for h in range(2):
                pe.wait_ge(S["gpart"], h + 1)
                for c in range(2):
                    last = flip(bank(h, 2)[0:3 * NE, tok(c)], gpart[:, 2 * h + c].rearrange("p w e -> p (w e)"))
                last.then_inc(S["gT_ps"], 1)
            pe.wait_ge(S["gT"], 2)
            gates(0)
            gates(1)
            for i in range(HC):
                if i + 2 < HC:
                    up(i + 2)
                    gates(i + 2)
                pe.wait_ge(S["hgb"], i + 1)
                pe.matmul(ps[0:D, 6, :], fw2_s[:, i, :], hgb[:, i % 2], start=(i == 0),
                          stop=(i == HC - 1)).then_inc(S["moe_ps"], 1)
            for h in range(2):
                pe.wait_ge(S["moeT"], h + 1)
                for c in range(2):
                    last = flip(ps[:, 2, (2 * h + c) * D:(2 * h + c + 1) * D], moeT[:, tok(2 * h + c)], D)
                last.then_inc(S["moeTb_ps"], 1)
            for h in range(2):
                rows_to_features(h, 3, x5, "x5", "x5T_ps")
            for h in range(2):
                pe.wait_ge(S["x5T"], h + 1)
                for c in range(2):
                    last = pe.matmul(bank(h, 1)[:, c * P:(c + 1) * P], x5T[:, tok(2 * h + c)], w4("lkv"),
                                     start=True, stop=True)
                last.then_inc(S["lkv_ps"], 1)
                pe.matmul(bank(h, 0)[0:D, 0:HALF], w4("lq"), x5T[:, half(h)], start=True,
                          stop=True).then_inc(S["lq_ps"], 1)
            for h in range(2):
                pe.wait_ge(S["phk"], h + 1)
                for c in range(2):
                    last = pe.matmul(bank(h, 2)[0:D, c * 144:(c + 1) * 144], phk[:, 2 * h + c, :],
                                     v1[:, 2 * h + c].rearrange("p i d -> p (i d)"), start=True, stop=True)
                last.then_inc(S["kv_ps"], 1)
            for h in range(2):
                pe.wait_ge(S["phq"], h + 1)
                pe.wait_ge(S["kv"], h + 1)
                for b in range(4):
                    last = pe.matmul(bank(h, 3)[(b % 2) * N:(b % 2 + 1) * N, (b // 2) * 72:(b // 2 + 1) * 72],
                                     phq[:, h * HALF + b * N:h * HALF + (b + 1) * N], kv[:, 4 * h + b, :],
                                     start=True, stop=True)
                last.then_inc(S["t5_ps"], 1)
            for h in range(2):
                rows_to_features(h, 0, x1, "x1", "x1T_ps")
            for h in range(2):
                pe.wait_ge(S["x1T"], h + 1)
                pe.matmul(bank(h, 1)[0:D, 0:HALF], w5("l1w1"), x1T[:, half(h)], start=True,
                          stop=True).then_inc(S["l1h_ps"], 1)
            for h in range(2):
                pe.wait_ge(S["g5"], h + 1)
                for c in range(2):
                    last = pe.matmul(bank(h, 2)[:, c * D:(c + 1) * D], g5[:, tok(2 * h + c)], w5("l1w2"),
                                     start=True, stop=True)
                last.then_inc(S["l1y_ps"], 1)
            for h in range(2):
                rows_to_features(h, 3, x7, "x7", "x7T_ps")
            for h in range(2):
                pe.wait_ge(S["x7T"], h + 1)
                for c in range(2):
                    last = pe.matmul(bank(h, 0)[:, c * NE:(c + 1) * NE], x7T[:, tok(2 * h + c)], w5("gate"),
                                     start=True, stop=True)
                last.then_inc(S["g_ps"], 1)
            for h in range(2):
                pe.wait_ge(S["oh1b"], h + 1)
                for c in range(2 * h, 2 * h + 2):
                    dst = bank(h, 1)[:, (c % 2) * NE:(c % 2 + 1) * NE]
                    for c0 in range(c):
                        pe.matmul(dst, tri_s[:, 1, :], oh1b[:, c0], start=(c0 == 0), stop=False)
                    last = pe.matmul(dst, tri_s[:, 0, :], oh1b[:, c], start=(c == 0), stop=True)
                last.then_inc(S["cum_ps"], 1)
            pe.wait_ge(S["disp"], 2)
            for i in range(2):
                for c in range(NC):
                    last = pe.matmul(ps[:, (2, 6)[i], 0:320], x7s[:, c].rearrange("p w d -> p (w d)"),
                                     disp[:, c, 4 * i:4 * i + 4].rearrange("p e s -> p (e s)"),
                                     start=(c == 0), stop=(c == NC - 1))
                last.then_inc(S["bufT_ps"], 1)
            pe.wait_ge(S["code"], 2)
            for c in range(NC):
                last = pe.matmul(ps[0:CAP, 3, tok(c)], code[:, c:c + 1].to_broadcast([P, CAP]), ident,
                                 start=True, stop=True)
            last.then_inc(S["cod_ps"], 1)
            for e in range(NE):
                pe.wait_ge(S["bufT"], e // 4 + 1)
                if e >= 2:
                    pe.wait_ge(S["hid"], e - 1)
                for j in range(2):
                    dst = ps[:, (0, 4)[e % 2], j * CAP:(j + 1) * CAP]
                    pe.matmul(dst, m1h[:, e, j * P:(j + 1) * P], bufT[:, e], start=True, stop=False)
                    last = pe.matmul(dst, m1l[:, e, j * P:(j + 1) * P], bufT[:, e], start=False, stop=True)
                last.then_inc(S["hid_ps"], 1)
            for e in range(NE):
                pe.wait_ge(S["hid"], e + 1)
                for j in range(2):
                    last = pe.matmul(ps[0:CAP, 5, e * D:(e + 1) * D], hid[:, e, j], m2_s[:, e, j, :],
                                     start=(j == 0), stop=(j == 1))
            last.then_inc(S["y_ps"], 1)
            pe.wait_ge(S["combT"], 1)
            pe.wait_ge(S["ybs"], 1)
            for h in range(2):
                for c in range(2):
                    for e in range(NE):
                        last = pe.matmul(ps[:, (1, 7)[h], c * P:(c + 1) * P], combT[:, e, tok(2 * h + c)],
                                         ybs[:, e].rearrange("p w d -> p (w d)"), start=(e == 0), stop=(e == NE - 1))
                last.then_inc(S["comb_ps"], 1)


def constants():
    f = np.float32
    con = np.zeros((P, CON_N), f)

    def put(name, a):
        a = np.asarray(a, f)
        con[:a.shape[0], CON[name][0]:CON[name][1]] = a

    feat = np.arange(P) % D
    side = np.arange(P) // D
    put("ident", np.eye(P))
    put("mask8", (feat[:, None] // 8 == np.arange(8)) / np.sqrt(8.0))
    put("vmask8", (np.arange(D)[None] // 8 % 2) == side[:, None])
    put("mask4", (feat[:, None] // 16 == np.arange(4)) / np.sqrt(16.0))
    put("vmask4", (np.arange(D)[None] // 16 % 2) == side[:, None])
    inv = (1.0 / 10000.0 ** (np.arange(0, 16, 2, dtype=f) / 16)).astype(f)
    freqs = np.outer(np.arange(N, dtype=f), inv)
    emb = np.concatenate([freqs, freqs], -1)
    sign = np.where(np.arange(16) < 8, -1.0, 1.0)
    put("cos", np.cos(emb).T[feat % 16])
    put("sin", (np.sin(emb) * sign).T[feat % 16])
    put("causal", np.where(np.arange(N)[None] <= feat[:, None], 0.0, NEG))
    put("pair", np.where(side[:, None] == side[None], 0.0, NEG))
    bm = np.zeros((D, 72))
    bm[:, :D] = np.arange(D)[:, None] // 8 == np.arange(D)[None] // 8
    bm[:, D:] = np.arange(D)[:, None] // 8 == np.arange(8)[None]
    put("bm", bm)
    put("iota8", np.tile(np.arange(NE), (P, 1)))
    put("slots", np.tile(np.arange(1, CAP + 1), (P, 1)))
    put("slotid", np.arange(1, P + 1)[:, None])
    put("expert", np.tile(128 * np.arange(NE) + 0, (P, 1)))
    expert = np.minimum(np.arange(HC * P) // HID, NE - 1)
    sel = np.tile(expert[None] == np.arange(NE)[:, None], (3, 1)).astype(f)
    tri = np.stack([np.triu(np.ones((P, P))), np.ones((P, P))], 1).astype(f)
    pos = np.arange(N, dtype=f)[:, None]
    div = np.exp(-np.log(f(10000.0)) * np.arange(0, D, 2, dtype=f) / D).astype(f)
    ang = (pos * div).astype(f)
    pe = np.stack([np.sin(ang), np.cos(ang)], -1).reshape(N, D).astype(f)
    return con, sel, tri, np.tile(pe, (2, 1))


def kernel(**inputs):
    import concourse.bacc as _bacc
    from concourse.bass_utils import run_bass_kernel_spmd as _run

    a = {k: np.asarray(v) for k, v in inputs.items()}
    f = np.float32
    con, sel, tri, pe = constants()

    pat = a["x"].reshape(B, 3, 8, 2, 8, 8, 16).transpose(4, 6, 1, 3, 0, 2, 5).reshape(P, KC, T)
    wconv = a["L0_tok_conv_w"].reshape(D, 3, 2, 8, 16).transpose(3, 4, 1, 2, 0).reshape(P, KC, D)

    def bcast(v):
        return np.broadcast_to(v[None], (P, D))

    rows = np.concatenate([bcast(a["L0_tok_ln_w"]), bcast(a["L0_tok_ln_b"]), pe, bcast(a["L0_tok_ff_b2"]),
                           bcast(a["L1_attn_ln1_g"]), bcast(a["L1_attn_ln1_b"]), bcast(a["L1_attn_ln2_g"]),
                           bcast(a["L1_attn_ln2_b"])], 1)
    cols = np.concatenate([np.tile(a["L0_tok_conv_b"], 2)[:, None], np.tile(a["L0_tok_ff_b2"], 2)[:, None],
                           np.tile(a["L0_ffn_ln1_w"], 2)[:, None], np.tile(a["L0_ffn_ln2_w"], 2)[:, None],
                           a["L1_ffn_b1"].reshape(NE * 2, P).T], 1)

    def with_bias(w, b):
        return np.concatenate([w, b[None]], 0)

    qkv, qkvb = a["L0_tok_qkv_w"].T, a["L0_tok_qkv_b"]
    q8, k8, v8 = (with_bias(qkv[:, i * D:(i + 1) * D], qkvb[i * D:(i + 1) * D]) for i in range(3))
    w65 = np.concatenate([with_bias(a["L0_tok_ff_w1"].T, a["L0_tok_ff_b1"]), q8, q8, k8, k8, v8,
                          with_bias(a["L0_tok_proj_w"].T, a["L0_tok_proj_b"]),
                          with_bias(a["L0_attn_Wq"], a["L0_attn_bq"]), with_bias(a["L0_attn_Wk"], a["L0_attn_bk"]),
                          with_bias(a["L0_attn_Wv"], a["L0_attn_bv"]), with_bias(a["L1_attn_W1"].T, a["L1_attn_b1"]),
                          with_bias(a["L1_attn_W2"].T, a["L1_attn_b2"]),
                          with_bias(a["L1_ffn_gate_w"], a["L1_ffn_gate_b"])], 1)
    head = np.arange(D) // 16
    other = (np.arange(D) % 16 + 8) % 16
    fq = a["L0_ffn_wq"].T
    fk = a["L0_ffn_wk"].T[:, head // 2 * 16 + np.arange(D) % 16]
    fkr = a["L0_ffn_wk"].T[:, head // 2 * 16 + other]
    fqr = fq[:, head * 16 + other]
    fv = a["L0_ffn_wv"].T[:, head // 2 * 16 + np.arange(D) % 16]
    wl = a["L1_attn_Wqkv"].T
    w64 = np.concatenate([fq, fq, fqr, fqr, fk, fk, fkr, fkr, fv, a["L0_ffn_wo"].T, a["L0_ffn_router_w"].T,
                          wl[:, 0:D], wl[:, D:3 * D]], 1)
    ff2 = a["L0_tok_ff_w2"].T.reshape(2, P, D).transpose(1, 0, 2)
    pad = HC * P - NE * HID

    def stacked(w):
        w = np.pad(w.reshape(NE * HID, D).T, ((0, 0), (0, pad)))
        return np.concatenate([w, w], 0)

    f13 = np.stack([stacked(a["L0_ffn_w1"]), stacked(a["L0_ffn_w3"])], 1)
    fw2 = np.pad(a["L0_ffn_w2"].transpose(0, 2, 1).reshape(NE * HID, D), ((0, pad), (0, 0)))
    fw2 = fw2.reshape(HC, P, D).transpose(1, 0, 2)
    m1 = np.tile(a["L1_ffn_w1"].transpose(1, 0, 2), (2, 1, 1))
    m2 = a["L1_ffn_w2"].reshape(NE, 2, P, D).transpose(2, 0, 1, 3)
    mb2 = np.broadcast_to(a["L1_ffn_b2"][None], (CAP, NE, D))
    sent = dict(pat=pat, wconv=wconv, rows=rows, cols=cols, w65=w65, w64=w64, ff2=ff2, f13=f13, fw2=fw2, m1=m1, m2=m2,
                mb2=mb2, con=con, sel=sel, tri=tri)

    nc = _bacc.Bacc("TRN2", target_bir_lowering=False, num_devices=1)
    arrays, args = {}, {}
    for name, v in sent.items():
        v = np.ascontiguousarray(v)
        arrays[f"in_{name}"] = v
        args[name] = nc.dram_tensor(f"in_{name}", v.shape, mybir.dt.from_np(v.dtype), kind="ExternalInput").ap()
    args["out"] = nc.dram_tensor("out_0", (T, D), F32, kind="ExternalOutput").ap()
    vit_tower(nc, **args)
    r = _run(nc, [arrays], core_ids=[0])
    return r.results[0]["out_0"].reshape(B, N, D)
```

```python
from contextlib import ExitStack

import numpy as np

import concourse.bass as bass
from concourse import mybir

F32 = mybir.dt.float32
F32R = mybir.dt.float32r
BF16 = mybir.dt.bfloat16
U32 = mybir.dt.uint32
ALU = mybir.AluOpType
ACT = mybir.ActivationFunctionType
AX_X = mybir.AxisListType.X

P = 128
B, D, N = 8, 64, 64
T = B * N
NC = T // P
KC = 3 * 16 * 16 // P
HF = 256
NE = 8
HID = int(8 / 3 * D)
HC = -(-NE * HID // P)
HALF = T // 2
CAP = -(-5 * T // (4 * NE))
NEG = -1e30
COMB_DVE = (1, 2, 3, 4, 5, 7)
NORMS = ["emb", "pre_attn", "pre_ffn", "rms", "pre_l1", "l1a", "l1b", "pre_moe"]
KEEP_CLOCK = {
    ("in_conv", 0): (24, 1),
}
RING = 5
LEAD = 3
LAG = 3
PAT_PARTS = [slice(0, 2), slice(2, 4), slice(4, KC)]
FLOAT_MAX = float(np.finfo(np.float32).max)
INF_TO = 1e4


def layout(parts):
    at, n = {}, 0
    for name, width in parts:
        at[name] = (n, n + width)
        n += width
    return at, n


ROWS, ROWS_N = layout([("ln_w", D), ("ln_b", D), ("pe", D), ("ff_b2", D), ("ln1_g", D), ("ln1_b", D),
                       ("ln2_g", D), ("ln2_b", D)])
COLS, COLS_N = layout([("conv_b", 1), ("ff_b2", 1), ("ln1_w", 1), ("ln2_w", 1), ("moe_b1", 2 * NE)])
W65, W65_N = layout([("ff1", HF), ("q8", P), ("k8", P), ("v8", D), ("proj", D), ("aq", D), ("ak", D), ("av", D),
                     ("l1w1", D), ("l1w2", D), ("gate", NE)])
W64, W64_N = layout([("fq", P), ("fqr", P), ("fk", P), ("fkr", P), ("fv", D), ("fo", D), ("router", NE),
                     ("lq", D), ("lkv", P)])
CON, CON_N = layout([("ident", P), ("mask8", 8), ("vmask8", D), ("mask4", 4), ("vmask4", D), ("cos", N),
                     ("sin", N), ("causal", N), ("pair", P), ("bm", 72), ("iota8", NE), ("slots", CAP),
                     ("slotid", 1), ("expert", NE)])


def vit_tower(nc: bass.Bass, pat, wconv, rows, cols, w65, w64, ff2, f13, fw2, m1, m2, mb2, con, sel, tri, out):
    with ExitStack() as ctx:
        def sb(name, shape, dt=F32):
            return ctx.enter_context(nc.sbuf_tensor(name, shape, dt))

        def sem(name):
            return ctx.enter_context(nc.semaphore(name))

        ps = ctx.enter_context(nc.psum_tensor("ps", [P, 8, 512], F32))

        rows_s = sb("rows_s", [P, ROWS_N])
        cols_s = sb("cols_s", [P, COLS_N])
        w65_s = sb("w65_s", [D + 1, W65_N])
        w64_s = sb("w64_s", [D, W64_N])
        ff2_s = sb("ff2_s", [P, 2, D])
        fw2s = sb("fw2s", [P, HC, 2, D], F32R)
        m2_s = sb("m2_s", [P, NE, 2, D])
        mb2_s = sb("mb2_s", [CAP, NE, D])
        con_s = sb("con_s", [P, CON_N])
        sel_s = sb("sel_s", [2 * NE, HC * P], F32R)
        tri_s = sb("tri_s", [P, 2, P], BF16)

        def row(name):
            return rows_s[:, ROWS[name][0]:ROWS[name][1]]

        def col(name, n=P):
            return cols_s[0:n, COLS[name][0]:COLS[name][1]]

        def w5(name):
            return w65_s[:, W65[name][0]:W65[name][1]]

        def w4(name):
            return w64_s[:, W64[name][0]:W64[name][1]]

        def con_(name, n=P):
            return con_s[0:n, CON[name][0]:CON[name][1]]

        ident = con_("ident")
        idle = sb("idle", [P, 512], BF16)
        spare = sb("spare", [1, 2])
        f13h = sb("f13h", [P, 2, HC * P], F32R)
        f13l = sb("f13l", [P, 2, HC * P], F32R)
        m1h = sb("m1h", [P, NE, 2 * P], F32R)
        m1l = sb("m1l", [P, NE, 2 * P], F32R)

        lnb_pe = sb("lnb_pe", [P, D])
        mhalf = sb("mhalf", [P, 2 * NC])

        def stats_tiles(name):
            return sb(name + "_st", [P, NC, 6]), sb(name + "_mv", [P, NC, 2]), sb(name + "_ve", [P, NC, 2]), \
                sb(name + "_rs", [P, NC, 2])

        ln = {k: stats_tiles(k) for k in NORMS}
        yn = sb("yn", [P, NC, D])
        h0 = sb("h0", [P, NC, D])
        mx8 = sb("mx8", [P, NC, 8])
        ri8 = sb("ri8", [P, NC, 4, 2])
        o8 = sb("o8", [P, NC, D])
        h1 = sb("h1", [P, NC, D])
        h1b = sb("h1b", [P, NC, D])
        h2 = sb("h2", [P, NC, D])
        n2 = sb("n2", [P, NC, D])
        av = sb("av", [P, NC, D])
        nmx = sb("nmx", [P, NC])
        suma = sb("suma", [P, NC])
        ria = sb("ria", [P, NC])
        h3 = sb("h3", [P, NC, D])
        x3 = sb("x3", [P, NC, D])
        r3 = sb("r3", [P, NC, D])
        q4_bd = sb("q4_bd", [P, NC, P])
        k4 = sb("k4", [P, NC, N])
        v4 = sb("v4", [P, B, 2, 34])
        mx4 = sb("mx4", [P, NC, 4])
        ri4 = sb("ri4", [P, NC, 2, 2])
        o4 = sb("o4", [P, NC, D])
        x4 = sb("x4", [P, NC, D])
        hx = sb("hx", [P, NC, D])
        fl = sb("fl", [P, NC, 2, D])
        flT = sb("flT", [P, T])
        fs = sb("fs", [P, T], F32R)
        top8 = sb("top8", [P, NC, 8])
        topi = sb("topi", [P, NC, 8], U32)
        topf = sb("topf", [P, NC, 8])
        lse = sb("lse", [P, NC, 8])
        lexp = sb("lexp", [P, NC, 8])
        lsum = sb("lsum", [P, NC])
        oh = sb("oh", [P, NC, 8])
        oh2 = sb("oh2", [P, NC, 8])
        wsel = sb("wsel", [P, NC, 8])
        wtot = sb("wtot", [P, NC])
        wden = sb("wden", [P, NC])
        winv = sb("winv", [P, NC])
        gat = sb("gat", [P, NC, 8])
        gpart = sb("gpart", [P, NC, 2, 8], F32R)
        gT = sb("gT", [2 * NE, T], F32R)
        h4 = sb("h4", [P, NC, D])
        x5 = sb("x5", [P, NC, D])
        zden = sb("zden", [P, NC, 8])
        z = sb("z", [P, NC, 8])
        h5 = sb("h5", [P, NC, D])
        lg = sb("lg", [P, NC, 8])
        top1 = sb("top1", [P, NC, 8])
        toi1 = sb("toi1", [P, NC, 8], U32)
        tof1 = sb("tof1", [P, NC, 8])
        lse1 = sb("lse1", [P, NC, 8])
        lex1 = sb("lex1", [P, NC, 8])
        lsu1 = sb("lsu1", [P, NC])
        prob = sb("prob", [P, NC])
        oh1 = sb("oh1", [P, NC, 8])
        oh1b = sb("oh1b", [P, NC, 8], BF16)
        code = sb("code", [P, NC])

        with ExitStack() as first_stages:
            def early(name, shape, dt=F32):
                return first_stages.enter_context(nc.sbuf_tensor(name, shape, dt))

            pat_s = early("pat_s", [P, KC, T])
            wconv_s = early("wconv_s", [P, KC, D])
            conv_f = early("conv_f", [D, T])
            g0 = early("g0", [P, 2, T])
            k8x = early("k8x", [P, NC, 8, N])
            s8 = early("s8", [P, NC, 8, N])
            pT8 = early("pT8", [P, NC, 4, P])
            v8 = early("v8", [P, B, 4, 18])
            q_bd = early("q_bd", [P, NC, P])
            k8 = early("k8", [P, NC, N])
            sel_f = early("sel_f", [2 * NE, HC * P])
            tri_f = early("tri_f", [P, 2, P])
            fw2_s = early("fw2_s", [P, HC, D])
            f13_s = early("f13_s", [P, 2, HC * P])
            m1_s = early("m1_s", [P, NE, 2 * P])
            rope = early("rope", [P, 2, NC, 2, N])
            aqk = early("aqk", [D, 2, T])
            sa = early("sa", [P, NC, P])
            paT = early("paT", [P, NC, P])
            h0T = early("h0T", [D + 1, T])
            fT = early("fT", [D + 1, T])
            o8T = early("o8T", [D + 1, T])
            o4T = early("o4T", [D, T])
            r3T = early("r3T", [D, T])

            k4x, s4, pT4 = k8x[:, :, 0:4, :], s8[:, :, 0:4, :], pT8[:, :, 0:2, :]

        x1T = sb("x1T", [D + 1, T])
        g5 = sb("g5", [D + 1, T])
        x7T = sb("x7T", [D + 1, T])
        v1 = sb("v1", [P, NC, 2, 72])
        h4a = sb("h4a", [P, NC, D])
        x5T = sb("x5T", [D, T])
        eq = sb("eq", [D, T])
        rq = sb("rq", [D, T])
        phq = sb("phq", [D, T])
        ek = sb("ek", [P, NC, D])
        rk = sb("rk", [P, NC, D])
        phk = sb("phk", [P, NC, D])
        t5 = sb("t5", [P, NC, D])
        y5 = sb("y5", [P, NC, D])
        yn5 = sb("yn5", [P, NC, D])
        x1 = sb("x1", [P, NC, D])
        y6 = sb("y6", [P, NC, D])
        yn6 = sb("yn6", [P, NC, D])
        h4b = sb("h4b", [P, NC, D])
        kv = sb("kv", [D, B, 72])
        x7 = sb("x7", [P, NC, D])
        x7s = sb("x7s", [P, NC, 2, D], F32R)
        posn = sb("posn", [P, NC, 8])
        codt = sb("codt", [P, NC, 8])
        keep = sb("keep", [P, NC, 8])

        with ExitStack() as first_experts:
            def moe(name, shape, dt=F32):
                return first_experts.enter_context(nc.sbuf_tensor(name, shape, dt))

            asil = moe("asil", [P, 2, T])
            hgb = moe("hgb", [P, RING, T])
            hgs = moe("hgs", [P, RING, 2, T], F32R)
            moeT = moe("moeT", [P, T])

        disp = sb("disp", [P, NC, NE, CAP], F32R)
        bufT = sb("bufT", [P, NE, CAP], F32R)
        codb = sb("codb", [CAP, T])
        combT = sb("combT", [CAP, NE, T], F32R)
        hid = sb("hid", [P, NE, 2, CAP])
        ybf = sb("ybf", [CAP, NE, D])
        ybs = sb("ybs", [CAP, NE, 2, D], F32R)
        ylow = sb("ylow", [P, NC, D])
        y7 = sb("y7", [P, NC, D])
        finite = sb("finite", [P, NC, D], U32)
        above = sb("above", [P, NC, D])
        below = sb("below", [P, NC, D])
        ynum = sb("ynum", [P, NC, D])
        h6 = sb("h6", [P, NC, D])

        in_conv, in_pat, in_small, in_w, in_big = sem("in_conv"), [sem("in_pat%d" % n) for n in range(len(PAT_PARTS))], \
            sem("in_small"), sem("in_w"), sem("in_big")
        out_stored = sem("out_stored")
        dve_step, act_step, pool_step = sem("dve_step"), sem("act_step"), sem("pool_step")
        S = {}
        for name in """hid_dve combT_pool prob ylow idle late_setup hgh hgl setup mconst conv_ps conv_f conv_t h0 h0_ps h0T ff1a_ps g0
            ff2a_ps fT qk8_ps v8_ps k8 k8x v8 s8_ps s8 p8 pT8_ps pT8 o8_ps o8 o8T_ps o8T proj_ps h1 h1T_ps
            h1T ff1b_ps g1 ff2b_ps h2 n2 n2T_ps n2T aqk_ps av_ps aqk av sa_ps sa pa paT_ps paT oa_ps h3 r3
            r3T_ps r3T q4_ps k4_ps v4_ps q4bd k4x v4 s4_ps s4 p4 pT4_ps pT4 o4_ps o4 o4T_ps o4T wo_ps x4 fl
            flT_ps fs rt_ps lse lexp gpart gT_ps gT split a_ps b_ps gc_ps asil sb hgb moe_ps moeT moeTb_ps h4
            x5 x5T_ps x5T lq_ps lkv_ps eq ek phq phk kv_ps kv t5_ps y5 x1 x1T_ps x1T l1h_ps g5 l1y_ps y6 x7
            x7T_ps x7T g_ps lse1 lex1 oh1b cum_ps disp bufT_ps bufT code cod_ps codb combT hid_ps hid y_ps
            ybs comb_ps h6 variance rstd""".split():
            S[name] = sem(name)

        block = ctx.enter_context(nc.Block())

        def norm_count(name, h):
            return 2 * NORMS.index(name) + h + 1

        def half(h):
            return slice(h * HALF, (h + 1) * HALF)

        def chunks(h):
            return slice(2 * h, 2 * h + 2)

        def tok(c):
            return slice(c * P, (c + 1) * P)

        def bank(h, i):
            return ps[:, 4 * h + i, :]

        @block.sync
        def _(sp):
            sp.dma_start(wconv_s[:], wconv).then_inc(in_conv, 16)
            sp.dma_start(cols_s[:], cols).then_inc(in_conv, 16)
            for n, at in enumerate(PAT_PARTS):
                sp.dma_start(pat_s[:, at], pat[:, at]).then_inc(in_pat[n], 16)
            sp.dma_start(con_s[:], con).then_inc(in_small, 16)
            sp.dma_start(rows_s[:], rows).then_inc(in_small, 16)
            sp.dma_start(w65_s[:], w65).then_inc(in_w, 16)
            sp.dma_start(ff2_s[:], ff2).then_inc(in_w, 16)
            sp.dma_start(w64_s[:], w64).then_inc(in_w, 16)
            sp.dma_start(f13_s[:], f13).then_inc(in_big, 16)
            sp.dma_start(m1_s[:], m1).then_inc(in_big, 16)
            sp.dma_start(fw2_s[:], fw2).then_inc(in_big, 16)
            sp.dma_start(sel_f[:], sel).then_inc(in_big, 16)
            sp.dma_start(m2_s[:], m2).then_inc(in_big, 16)
            sp.dma_start(mb2_s[:], mb2).then_inc(in_big, 16)
            sp.dma_start(tri_f[:], tri).then_inc(in_big, 16)
            for h in range(2):
                sp.wait_ge(S["h6"], h + 1)
                sp.dma_start(out.rearrange("(c p) d -> p c d", p=P)[:, chunks(h)], h6[:, chunks(h)]).then_inc(
                    out_stored, 16)
            sp.wait_ge(out_stored, 32)

        @block.gpsimd
        def _(pool):
            pool.memset(mhalf[:], -0.5).then_inc(S["mconst"], 1)
            pool.memset(q_bd[:], 0.0)
            pool.memset(q4_bd[:], 0.0).then_inc(S["setup"], 1)

            def rsqrt(name, n):
                for h in range(2):
                    pool.wait_ge(S["variance"], norm_count(name, h))
                    ve, rs = ln[name][2], ln[name][3]
                    pool.tensor_tensor(rs[:, chunks(h), 0:n], ve[:, chunks(h), 0:n],
                                       mhalf[:, 0:2 * n].rearrange("p (c n) -> p c n", n=n),
                                       ALU.pow).then_inc(S["rstd"], 1)

            pool.wait_ge(S["mconst"], 1)
            rsqrt("emb", 1)
            pool.wait_ge(in_big, 16 * 7)
            pool.tensor_copy(sel_s[:], sel_f[:])
            pool.tensor_copy(tri_s[:], tri_f[:]).then_inc(S["split"], 1)
            pool.wait_ge(S["split"], 3)
            for j in range(2):
                pool.tensor_tensor(f13l[:, j], f13_s[:, j], f13h[:, j], ALU.subtract)
            pool.tensor_tensor(fw2s[:, :, 1], fw2_s[:], fw2s[:, :, 0], ALU.subtract)
            pool.tensor_tensor(m1l[:], m1_s[:], m1h[:], ALU.subtract).then_inc(S["split"], 1)
            rsqrt("pre_attn", 1)
            rsqrt("pre_ffn", 2)
            rsqrt("rms", 1)
            for i in range(HC):
                pool.wait_ge(S["hgh"], i + 1)
                if i >= RING:
                    pool.wait_ge(S["moe_ps"], i - RING + 1)
                pool.tensor_tensor(hgs[:, i % RING, 1], hgb[:, i % RING], hgs[:, i % RING, 0],
                                   ALU.subtract).then_inc(S["hgl"], 1)
            pool.memset(v1[:], 0.0).then_inc(S["late_setup"], 1)
            for n, tile in enumerate((x1T, g5, x7T)):
                pool.wait_ge(S["late_setup"], n + 1)
                pool.memset(tile[D:D + 1, :], 1.0).then_inc(S["late_setup"], 1)
            pool.wait_ge(S["late_setup"], 4)
            rsqrt("pre_l1", 1)
            rsqrt("l1a", 1)
            rsqrt("l1b", 1)
            rsqrt("pre_moe", 1)
            pool.wait_ge(S["codb"], 1)
            for e in range(NE):
                if e not in COMB_DVE:
                    pool.tensor_scalar(combT[:, e], codb[:], con_("slotid", CAP), float(128 * e), ALU.subtract,
                                       ALU.is_equal).then_inc(S["combT_pool"], 1)

        @block.vector
        def _(dve):
            steps = [0]

            def link(ins):
                steps[0] += 1
                ins.then_inc(dve_step, 1)
                dve.wait_ge(dve_step, steps[0])

            def stats(name, src, h, eps):
                st, mv_, ve, _ = ln[name]
                for c in range(2 * h, 2 * h + 2):
                    last = dve.bn_stats(st[:, c, :], src[:, c - 2 * h, :])
                link(last)
                for c in range(2 * h, 2 * h + 2):
                    last = dve.bn_aggr(mv_[:, c, :], st[:, c, :])
                link(last)
                dve.tensor_scalar(ve[:, chunks(h), 0:1], mv_[:, chunks(h), 1:2], eps, None,
                                  ALU.add).then_inc(S["variance"], 1)

            def mean(name, c):
                return ln[name][1][:, c, 0:1]

            def rstd(name, c, i=0):
                return ln[name][3][:, c, i:i + 1]

            dve.memset(spare[:], 0.0)
            dve.memset(idle[:], 0.0).then_inc(S["idle"], 1)
            for tile in (h0T, fT, o8T):
                dve.memset(tile[D:D + 1, :], 1.0)
            dve.memset(v8[:, :, :, 16:18], 0.0)
            link(dve.memset(v4[:, :, :, 32:34], 0.0))
            for i in range(2):
                dve.memset(v8[i * N:(i + 1) * N, :, :, 16 + i:17 + i], 1.0)
                last = dve.memset(v4[i * N:(i + 1) * N, :, :, 32 + i:33 + i], 1.0)
            last.then_inc(S["setup"], 1)
            dve.wait_ge(in_small, 32)
            link(dve.tensor_tensor(lnb_pe[:], row("ln_b"), row("pe"), ALU.add))

            for h in range(2):
                dve.wait_ge(S["conv_t"], h + 1)
                stats("emb", bank(h, 1)[:, 0:P].rearrange("p (c d) -> p c d", c=2), h, 1e-5)
            for h in range(2):
                dve.wait_ge(S["rstd"], norm_count("emb", h))
                for c in range(2 * h, 2 * h + 2):
                    src = bank(h, 1)[:, (c % 2) * D:(c % 2 + 1) * D]
                    last = dve.scalar_tensor_tensor(yn[:, c, :], src, mean("emb", c), row("ln_w"), ALU.subtract,
                                                    ALU.mult)
                link(last)
                for c in range(2 * h, 2 * h + 2):
                    last = dve.scalar_tensor_tensor(h0[:, c, :], yn[:, c, :], rstd("emb", c), lnb_pe[:], ALU.mult,
                                                    ALU.add)
                last.then_inc(S["h0"], 1)

            dve.wait_ge(in_big, 16 * 7)
            for j in range(2):
                last = dve.tensor_copy(f13h[:, j], f13_s[:, j])
            last.then_inc(S["split"], 1)
            dve.tensor_copy(fw2s[:, :, 0], fw2_s[:])
            dve.tensor_copy(m1h[:], m1_s[:]).then_inc(S["split"], 1)

            dve.wait_ge(S["setup"], 2)
            for h in range(2):
                dve.wait_ge(S["qk8_ps"], h + 1)
                pq = bank(h, 1).rearrange("p (w c i t) -> p w c i t", w=2, c=2, i=2)
                for i in range(2):
                    rr = slice(i * D, (i + 1) * D)
                    dve.tensor_copy(k8[rr, chunks(h), :], pq[rr, 1, :, i, :])
                    last = dve.tensor_copy(q_bd[rr, chunks(h), i * N:(i + 1) * N], pq[rr, 0, :, i, :])
                link(last)
                dve.tensor_tensor(k8x[:, chunks(h)],
                                  k8[:, chunks(h), :].unsqueeze(2).to_broadcast([P, 2, 8, N]),
                                  con_("mask8").unsqueeze(1).unsqueeze(3).to_broadcast([P, 2, 8, N]),
                                  ALU.mult).then_inc(S["k8x"], 1)
                dve.wait_ge(S["v8_ps"], h + 1)
                dve.tensor_tensor(v8[:, 4 * h:4 * h + 4, :, 0:16],
                                  bank(h, 2)[:, 0:4 * D].rearrange("p (b g d) -> p b g d", b=4, g=4),
                                  con_("vmask8").rearrange("p (g d) -> p g d", g=4).unsqueeze(1)
                                  .to_broadcast([P, 4, 4, 16]), ALU.mult).then_inc(S["v8"], 1)
            for c in range(NC):
                h = c // 2
                src = bank(h, (3, 0)[c % 2]).rearrange("p (g k) -> p g k", g=8)
                dve.wait_ge(S["s8_ps"], c + 1)
                link(dve.tensor_reduce(mx8[:, c, :], src, AX_X, ALU.max))
                dve.tensor_tensor(s8[:, c], src, mx8[:, c, :].unsqueeze(2).to_broadcast([P, 8, N]),
                                  ALU.subtract).then_inc(S["s8"], 1)
            for c in range(NC):
                dve.wait_ge(S["pT8_ps"], c + 1)
                dve.tensor_copy(pT8[:, c], bank(c // 2, (1, 2)[c % 2]).rearrange("p (g t) -> p g t", g=4)).then_inc(
                    S["pT8"], 1)
            for c in range(NC):
                dve.wait_ge(S["o8_ps"], 2 * (c // 2) + 2)
                src = bank(c // 2, 3)[:, (c % 2) * 72:(c % 2 + 1) * 72].rearrange("p (g d) -> p g d", g=4)
                link(dve.reciprocal(ri8[:, c], src[:, :, 16:18]))
                dve.tensor_tensor(o8[:, c, :].rearrange("p (g i d) -> p g i d", g=4, i=2),
                                  src[:, :, 0:16].rearrange("p g (i d) -> p g i d", i=2),
                                  ri8[:, c].unsqueeze(3).to_broadcast([P, 4, 2, 8]), ALU.mult).then_inc(S["o8"], 1)
            for h in range(2):
                dve.wait_ge(S["proj_ps"], h + 1)
                dve.tensor_tensor(h1[:, chunks(h)], bank(h, 1)[:, 0:P].rearrange("p (c d) -> p c d", c=2),
                                  h0[:, chunks(h)], ALU.add).then_inc(S["h1"], 1)
            for h in range(2):
                dve.wait_ge(S["h1"], h + 1)
                link(dve.tensor_tensor(h1b[:, chunks(h)], h1[:, chunks(h)],
                                       row("ff_b2").unsqueeze(1).to_broadcast([P, 2, D]), ALU.add))
            for h in range(2):
                dve.wait_ge(S["ff2b_ps"], h + 1)
                link(dve.tensor_tensor(h2[:, chunks(h)], bank(h, 0)[:, 0:P].rearrange("p (c d) -> p c d", c=2),
                                       h1b[:, chunks(h)], ALU.add))
                stats("pre_attn", h2[:, chunks(h)], h, 1e-5)
            for h in range(2):
                dve.wait_ge(S["rstd"], norm_count("pre_attn", h))
                for c in range(2 * h, 2 * h + 2):
                    last = dve.tensor_scalar(n2[:, c], h2[:, c], mean("pre_attn", c), rstd("pre_attn", c),
                                             ALU.subtract, ALU.mult)
                last.then_inc(S["n2"], 1)

            for h in range(2):
                dve.wait_ge(S["av_ps"], h + 1)
                dve.tensor_copy(av[:, chunks(h)], bank(h, 3)[:, 0:P].rearrange("p (c d) -> p c d", c=2)).then_inc(
                    S["av"], 1)
            for h in range(2):
                dve.wait_ge(S["sa_ps"], h + 1)
                for c in range(2 * h, 2 * h + 2):
                    last = dve.scalar_tensor_tensor(sa[:, c], bank(h, 0)[:, (c % 2) * P:(c % 2 + 1) * P],
                                                    float(D) ** -0.5, con_("pair"), ALU.mult, ALU.add)
                link(last)
                dve.tensor_reduce(nmx[:, chunks(h)], sa[:, chunks(h)], AX_X, ALU.max, negate=True).then_inc(S["sa"], 1)
            for h in range(2):
                dve.wait_ge(S["paT_ps"], h + 1)
                dve.tensor_copy(paT[:, chunks(h)], bank(h, 1)[:, 0:2 * P].rearrange("p (c d) -> p c d", c=2)).then_inc(
                    S["paT"], 1)
            for h in range(2):
                dve.wait_ge(S["pa"], 2 * h + 2)
                link(dve.reciprocal(ria[:, chunks(h)], suma[:, chunks(h)]))
                dve.wait_ge(S["oa_ps"], h + 1)
                for c in range(2 * h, 2 * h + 2):
                    last = dve.scalar_tensor_tensor(h3[:, c], bank(h, 2)[:, (c % 2) * D:(c % 2 + 1) * D],
                                                    ria[:, c:c + 1], h2[:, c], ALU.mult, ALU.add)
                last.then_inc(S["h3"], 1)
            for h in range(2):
                dve.wait_ge(S["h3"], h + 1)
                st, mv_, ve, _ = ln["pre_ffn"]
                for c in range(2 * h, 2 * h + 2):
                    last = dve.bn_stats(st[:, c, :], h3[:, c, :])
                link(last)
                for c in range(2 * h, 2 * h + 2):
                    last = dve.bn_aggr(mv_[:, c, :], st[:, c, :])
                link(last)
                dve.tensor_scalar(ve[:, chunks(h), 0:1], mv_[:, chunks(h), 1:2], 1e-5, None, ALU.add)
                dve.tensor_scalar(ve[:, chunks(h), 1:2], mv_[:, chunks(h), 1:2], 1.0 + 1e-6, 1e-11, ALU.mult,
                                  ALU.add).then_inc(S["variance"], 1)
            for h in range(2):
                dve.wait_ge(S["rstd"], norm_count("pre_ffn", h))
                for c in range(2 * h, 2 * h + 2):
                    last = dve.tensor_scalar(r3[:, c], h3[:, c], mean("pre_ffn", c), rstd("pre_ffn", c, 1),
                                             ALU.subtract, ALU.mult)
                last.then_inc(S["r3"], 1)
                for c in range(2 * h, 2 * h + 2):
                    last = dve.tensor_scalar(x3[:, c], h3[:, c], mean("pre_ffn", c), rstd("pre_ffn", c),
                                             ALU.subtract, ALU.mult)
                link(last)
            for h in range(2):
                for w, ready in ((0, "q4_ps"), (1, "k4_ps")):
                    dve.wait_ge(S[ready], h + 1)
                    src = bank(h, w).rearrange("p (r c i t) -> p r c i t", r=2, c=2, i=2)
                    for i in range(2):
                        rr = slice(i * D, (i + 1) * D)
                        dve.tensor_tensor(rope[rr, w, chunks(h), 0, :], src[rr, 0, :, i, :],
                                          con_s[rr, CON["cos"][0]:CON["cos"][1]].unsqueeze(1).to_broadcast([D, 2, N]),
                                          ALU.mult)
                        last = dve.tensor_tensor(
                            rope[rr, w, chunks(h), 1, :], src[rr, 1, :, i, :],
                            con_s[rr, CON["sin"][0]:CON["sin"][1]].unsqueeze(1).to_broadcast([D, 2, N]), ALU.mult)
                    link(last)
                    if w == 0:
                        for i in range(2):
                            rr = slice(i * D, (i + 1) * D)
                            last = dve.tensor_tensor(q4_bd[rr, chunks(h), i * N:(i + 1) * N],
                                                     rope[rr, 0, chunks(h), 0, :], rope[rr, 0, chunks(h), 1, :], ALU.add)
                        last.then_inc(S["q4bd"], 1)
                    else:
                        link(dve.tensor_tensor(k4[:, chunks(h)], rope[:, 1, chunks(h), 0, :],
                                               rope[:, 1, chunks(h), 1, :], ALU.add))
                        dve.tensor_tensor(k4x[:, chunks(h)],
                                          k4[:, chunks(h), :].unsqueeze(2).to_broadcast([P, 2, 4, N]),
                                          con_("mask4").unsqueeze(1).unsqueeze(3).to_broadcast([P, 2, 4, N]),
                                          ALU.mult).then_inc(S["k4x"], 1)
                dve.wait_ge(S["v4_ps"], h + 1)
                dve.tensor_tensor(v4[:, 4 * h:4 * h + 4, :, 0:32],
                                  bank(h, 2)[:, 0:4 * D].rearrange("p (b g d) -> p b g d", b=4, g=2),
                                  con_("vmask4").rearrange("p (g d) -> p g d", g=2).unsqueeze(1)
                                  .to_broadcast([P, 4, 2, 32]), ALU.mult).then_inc(S["v4"], 1)
            for c in range(NC):
                dve.wait_ge(S["s4_ps"], 2 * (c // 2) + 2)
                src = bank(c // 2, 3)[:, (c % 2) * 256:(c % 2 + 1) * 256].rearrange("p (g k) -> p g k", g=4)
                link(dve.tensor_tensor(s4[:, c], src, con_("causal").unsqueeze(1).to_broadcast([P, 4, N]), ALU.add))
                link(dve.tensor_reduce(mx4[:, c, :], s4[:, c], AX_X, ALU.max))
                dve.tensor_tensor(s4[:, c], s4[:, c], mx4[:, c, :].unsqueeze(2).to_broadcast([P, 4, N]),
                                  ALU.subtract).then_inc(S["s4"], 1)
            for c in range(NC):
                dve.wait_ge(S["o4_ps"], 2 * (c // 2) + 2)
                src = bank(c // 2, 1)[:, (c % 2) * 68:(c % 2 + 1) * 68].rearrange("p (g d) -> p g d", g=2)
                link(dve.reciprocal(ri4[:, c], src[:, :, 32:34]))
                dve.tensor_tensor(o4[:, c, :].rearrange("p (g i d) -> p g i d", g=2, i=2),
                                  src[:, :, 0:32].rearrange("p g (i d) -> p g i d", i=2),
                                  ri4[:, c].unsqueeze(3).to_broadcast([P, 2, 2, 16]), ALU.mult).then_inc(S["o4"], 1)
            for h in range(2):
                dve.wait_ge(S["wo_ps"], h + 1)
                link(dve.tensor_tensor(x4[:, chunks(h)], bank(h, 3)[:, 0:P].rearrange("p (c d) -> p c d", c=2),
                                       x3[:, chunks(h)], ALU.add))
                st, mv_, ve, _ = ln["rms"]
                for c in range(2 * h, 2 * h + 2):
                    last = dve.bn_stats(st[:, c, :], x4[:, c, :])
                link(last)
                for c in range(2 * h, 2 * h + 2):
                    last = dve.bn_aggr(mv_[:, c, :], st[:, c, :])
                link(last)
                link(dve.tensor_tensor(ve[:, chunks(h), 1:2], mv_[:, chunks(h), 0:1], mv_[:, chunks(h), 0:1],
                                       ALU.mult))
                dve.scalar_tensor_tensor(ve[:, chunks(h), 0], mv_[:, chunks(h), 1], 1e-6,
                                         ve[:, chunks(h), 1], ALU.add, ALU.add).then_inc(S["variance"], 1)
            for h in range(2):
                dve.wait_ge(S["rstd"], norm_count("rms", h))
                for c in range(2 * h, 2 * h + 2):
                    last = dve.tensor_scalar(fl[:, c], x4[:, c].unsqueeze(1).to_broadcast([P, 2, D]),
                                             rstd("rms", c), None, ALU.mult)
                last.then_inc(S["fl"], 1)
            for h in range(2):
                dve.wait_ge(S["flT_ps"], h + 1)
                link(dve.tensor_scalar(flT[:, half(h)], bank(h, 0)[:, 0:HALF], col("ln2_w"), None, ALU.mult))
                link(dve.tensor_copy(fs[:, half(h)], flT[:, half(h)]))
                dve.tensor_tensor(fs[D:P, half(h)], flT[D:P, half(h)], fs[D:P, half(h)],
                                  ALU.subtract).then_inc(S["fs"], 1)
            dve.wait_ge(S["rt_ps"], 1)
            src = ps[:, 1, 0:NC * NE].rearrange("p (c e) -> p c e", c=NC)
            for c in range(NC):
                last = dve.max(top8[:, c, :], src[:, c, :])
            link(last)
            dve.tensor_tensor(lse[:], src, top8[:, :, 0:1].to_broadcast([P, NC, 8]), ALU.subtract).then_inc(S["lse"], 1)
            for c in range(NC):
                last = dve.max_index(topi[:, c, :], top8[:, c, :], src[:, c, :])
            link(last)
            link(dve.tensor_copy(topf[:], topi[:]))
            iota = con_("iota8").unsqueeze(1).to_broadcast([P, NC, 8])
            dve.tensor_tensor(oh[:], iota, topf[:, :, 0:1].to_broadcast([P, NC, 8]), ALU.is_equal)
            link(dve.tensor_tensor(oh2[:], iota, topf[:, :, 1:2].to_broadcast([P, NC, 8]), ALU.is_equal))
            link(dve.tensor_tensor(oh[:], oh[:], oh2[:], ALU.add))
            dve.wait_ge(S["lexp"], 1)
            dve.tensor_reduce(lsum[:], lexp[:], AX_X, ALU.add)
            link(dve.tensor_tensor(wsel[:], lexp[:], oh[:], ALU.mult))
            link(dve.tensor_reduce(wtot[:], wsel[:], AX_X, ALU.add))
            link(dve.scalar_tensor_tensor(wden[:], lsum[:], 1e-9, wtot[:], ALU.mult, ALU.add))
            link(dve.reciprocal(winv[:], wden[:]))
            link(dve.tensor_tensor(gat[:], wsel[:], winv[:].unsqueeze(2).to_broadcast([P, NC, 8]), ALU.mult))
            link(dve.tensor_copy(gpart[:, :, 0], gat[:]))
            dve.tensor_tensor(gpart[:, :, 1], gat[:], gpart[:, :, 0], ALU.subtract).then_inc(S["gpart"], 1)

            def product(i):
                dve.wait_ge(S["asil"], i + 1)
                dve.wait_ge(S["b_ps"], i + 1)
                if i >= RING:
                    dve.wait_ge(S["hgl"], i - RING + 1)
                dve.tensor_tensor(hgb[:, i % RING], asil[:, i % 2], ps[:, (3, 7)[i % 2], :],
                                  ALU.mult).then_inc(S["sb"], 1)

            for i in range(LEAD):
                product(i)
            for i in range(HC):
                dve.wait_ge(S["sb"], i + 1)
                dve.wait_ge(S["gc_ps"], i + 1)
                dve.tensor_tensor(hgb[:, i % RING], hgb[:, i % RING], ps[:, (1, 5)[i % 2], :],
                                  ALU.mult).then_inc(S["hgb"], 1)
                if i + LEAD < HC:
                    product(i + LEAD)
            for h in range(2):
                link(dve.tensor_tensor(hx[:, chunks(h)], h3[:, chunks(h)], x4[:, chunks(h)], ALU.add))
            for h in range(2):
                dve.wait_ge(S["moeTb_ps"], h + 1)
                src = bank(h, 1)[:, 0:2 * P].rearrange("p (c w d) -> p c w d", c=2, w=2)
                link(dve.tensor_tensor(h4a[:, chunks(h)], src[:, :, 0, :], hx[:, chunks(h)], ALU.add))
                link(dve.tensor_tensor(h4[:, chunks(h)], src[:, :, 1, :], h4a[:, chunks(h)], ALU.add))
                stats("pre_l1", h4[:, chunks(h)], h, 1e-5)
            for h in range(2):
                dve.wait_ge(S["rstd"], norm_count("pre_l1", h))
                for c in range(2 * h, 2 * h + 2):
                    last = dve.tensor_scalar(x5[:, c], h4[:, c], mean("pre_l1", c), rstd("pre_l1", c),
                                             ALU.subtract, ALU.mult)
                last.then_inc(S["x5"], 1)
            dve.wait_ge(S["late_setup"], 1)
            for i in range(2):
                last = dve.memset(v1[i * N:(i + 1) * N, :, i, D:72], 1.0)
            link(last)
            for h in range(2):
                dve.wait_ge(S["lkv_ps"], h + 1)
                src = bank(h, 1)[:, 0:256].rearrange("p (c w d) -> p c w d", c=2, w=2)
                dve.wait_ge(S["ek"], h + 1)
                for i in range(2):
                    rr = slice(i * N, (i + 1) * N)
                    dve.tensor_copy(v1[rr, chunks(h), i, 0:D], src[rr, :, 1, :])
                dve.scalar_tensor_tensor(phk[:, chunks(h)], ek[:, chunks(h)], 1.0, rk[:, chunks(h)], ALU.min,
                                         ALU.add).then_inc(S["phk"], 1)
                dve.wait_ge(S["eq"], h + 1)
                dve.scalar_tensor_tensor(phq[:, half(h)], eq[:, half(h)], 1.0, rq[:, half(h)], ALU.min,
                                         ALU.add).then_inc(S["phq"], 1)
            for h in range(2):
                dve.wait_ge(S["kv_ps"], h + 1)
                dve.tensor_tensor(kv[:, 4 * h:4 * h + 4],
                                  bank(h, 2)[0:D, 0:288].rearrange("p (b d) -> p b d", b=4),
                                  con_("bm", D).unsqueeze(1).to_broadcast([D, 4, 72]), ALU.mult).then_inc(S["kv"], 1)
            for h in range(2):
                cs = chunks(h)
                dve.wait_ge(S["t5_ps"], h + 1)
                src = bank(h, 3)[:, 0:144].rearrange("p (c d) -> p c d", c=2)
                link(dve.tensor_scalar(zden[:, cs], src[:, :, D:72], 1e-6, None, ALU.add))
                link(dve.reciprocal(z[:, cs], zden[:, cs]))
                link(dve.tensor_tensor(t5[:, cs].rearrange("p c (g d) -> p c g d", g=8),
                                       src[:, :, 0:D].rearrange("p c (g d) -> p c g d", g=8),
                                       z[:, cs].unsqueeze(3).to_broadcast([P, 2, 8, 8]), ALU.mult))
                link(dve.tensor_tensor(y5[:, cs], t5[:, cs], x5[:, cs], ALU.add))
                stats("l1a", y5[:, cs], h, 1e-5)
            for h in range(2):
                dve.wait_ge(S["rstd"], norm_count("l1a", h))
                for c in range(2 * h, 2 * h + 2):
                    last = dve.scalar_tensor_tensor(yn5[:, c], y5[:, c], mean("l1a", c), row("ln1_g"),
                                                    ALU.subtract, ALU.mult)
                link(last)
                for c in range(2 * h, 2 * h + 2):
                    last = dve.scalar_tensor_tensor(x1[:, c], yn5[:, c], rstd("l1a", c), row("ln1_b"), ALU.mult,
                                                    ALU.add)
                last.then_inc(S["x1"], 1)
            link(dve.tensor_tensor(h4b[:], h4[:], row("ln2_b").unsqueeze(1).to_broadcast([P, NC, D]), ALU.add))
            for h in range(2):
                dve.wait_ge(S["l1y_ps"], h + 1)
                dve.wait_ge(S["x1"], h + 1)
                link(dve.tensor_tensor(y6[:, chunks(h)], bank(h, 2)[:, 0:P].rearrange("p (c d) -> p c d", c=2),
                                       x1[:, chunks(h)], ALU.add))
                stats("l1b", y6[:, chunks(h)], h, 1e-5)
            for h in range(2):
                cs = chunks(h)
                dve.wait_ge(S["rstd"], norm_count("l1b", h))
                for c in range(2 * h, 2 * h + 2):
                    last = dve.scalar_tensor_tensor(yn6[:, c], y6[:, c], mean("l1b", c), row("ln2_g"),
                                                    ALU.subtract, ALU.mult)
                link(last)
                for c in range(2 * h, 2 * h + 2):
                    last = dve.scalar_tensor_tensor(h5[:, c], yn6[:, c], rstd("l1b", c), h4b[:, c], ALU.mult,
                                                    ALU.add)
                link(last)
                stats("pre_moe", h5[:, cs], h, 1e-5)
            for h in range(2):
                cs = chunks(h)
                dve.wait_ge(S["rstd"], norm_count("pre_moe", h))
                for c in range(2 * h, 2 * h + 2):
                    last = dve.tensor_scalar(x7[:, c], h5[:, c], mean("pre_moe", c), rstd("pre_moe", c),
                                             ALU.subtract, ALU.mult)
                last.then_inc(S["x7"], 1)
                dve.wait_ge(S["x7"], h + 1)
                link(dve.tensor_copy(x7s[:, cs, 0], x7[:, cs]))
                link(dve.tensor_tensor(x7s[:, cs, 1], x7[:, cs], x7s[:, cs, 0], ALU.subtract))
            for h in range(2):
                cs = chunks(h)
                dve.wait_ge(S["g_ps"], h + 1)
                src = bank(h, 0)[:, 0:16].rearrange("p (c e) -> p c e", c=2)
                for c in range(2):
                    last = dve.max(top1[:, 2 * h + c, :], src[:, c, :])
                link(last)
                dve.tensor_tensor(lse1[:, cs], src, top1[:, cs, 0:1].to_broadcast([P, 2, 8]),
                                  ALU.subtract).then_inc(S["lse1"], 1)
                for c in range(2):
                    last = dve.max_index(toi1[:, 2 * h + c, :], top1[:, 2 * h + c, :], src[:, c, :])
                link(last)
                link(dve.tensor_copy(tof1[:, cs], toi1[:, cs]))
                iota = con_("iota8").unsqueeze(1).to_broadcast([P, 2, 8])
                link(dve.tensor_tensor(oh1[:, cs], iota, tof1[:, cs, 0:1].to_broadcast([P, 2, 8]), ALU.is_equal))
                dve.tensor_copy(oh1b[:, cs], oh1[:, cs]).then_inc(S["oh1b"], 1)
            for h in range(2):
                cs = chunks(h)
                dve.wait_ge(S["cum_ps"], h + 1)
                link(dve.tensor_tensor(posn[:, cs], bank(h, 1)[:, 0:16].rearrange("p (c e) -> p c e", c=2),
                                       oh1[:, cs], ALU.mult))
                for c in range(2 * h, 2 * h + 2):
                    dve.tensor_tensor(disp[:, c], con_("slots").unsqueeze(1).to_broadcast([P, NE, CAP]),
                                      posn[:, c].unsqueeze(2).to_broadcast([P, NE, CAP]),
                                      ALU.is_equal).then_inc(S["disp"], 1)
            dve.tensor_scalar(keep[:], posn[:], float(CAP), None, ALU.is_le)
            link(dve.tensor_tensor(codt[:], con_("expert").unsqueeze(1).to_broadcast([P, NC, 8]), posn[:], ALU.add))
            link(dve.tensor_tensor(keep[:], keep[:], oh1[:], ALU.mult))
            link(dve.tensor_tensor(codt[:], codt[:], keep[:], ALU.mult))
            dve.tensor_reduce(code[:], codt[:], AX_X, ALU.add).then_inc(S["code"], 1)
            dve.wait_ge(S["lex1"], 2)
            link(dve.tensor_reduce(lsu1[:], lex1[:], AX_X, ALU.add))
            dve.reciprocal(prob[:], lsu1[:]).then_inc(S["prob"], 1)
            dve.wait_ge(S["cod_ps"], 1)
            dve.tensor_copy(codb[:], ps[0:CAP, 3, :]).then_inc(S["codb"], 1)
            dve.wait_ge(S["codb"], 1)

            def slot_columns(eng, e):
                return eng.tensor_scalar(combT[:, e], codb[:], con_("slotid", CAP), float(128 * e), ALU.subtract,
                                         ALU.is_equal)

            def hidden(e):
                dve.wait_ge(S["hid_ps"], e + 1)
                k = COLS["moe_b1"][0] + 2 * e + 1
                dve.tensor_scalar(hid[:, e, 1], ps[:, (2, 6)[e % 2], 0:CAP], cols_s[:, k:k + 1], 0.0, ALU.add,
                                  ALU.max).then_inc(S["hid_dve"], 1)

            for e in range(NE):
                hidden(e)
                if e in COMB_DVE:
                    slot_columns(dve, e).then_inc(S["combT"], 1)
            for i in range(2):
                es = slice(4 * i, 4 * i + 4)
                dve.wait_ge(S["y_ps"], i + 1)
                link(dve.tensor_tensor(ybf[:, es], ps[0:CAP, (5, 3)[i], 0:4 * D].rearrange("p (e d) -> p e d", e=4),
                                       mb2_s[:, es], ALU.add))
                link(dve.tensor_copy(ybs[:, es, 0], ybf[:, es]))
                dve.tensor_tensor(ybs[:, es, 1], ybf[:, es], ybs[:, es, 0], ALU.subtract).then_inc(S["ybs"], 1)
            for h in range(2):
                cs = chunks(h)
                dve.wait_ge(S["ylow"], h + 1)
                for c in range(2):
                    last = dve.scalar_tensor_tensor(y7[:, 2 * h + c], ps[:, (1, 7)[h], c * P:c * P + D],
                                                    prob[:, 2 * h + c:2 * h + c + 1], ylow[:, 2 * h + c], ALU.mult,
                                                    ALU.add)
                link(last)
                dve.tensor_scalar(finite[:, cs], y7[:, cs], 0.0, 0.0, ALU.mult, ALU.is_equal)
                dve.tensor_scalar(above[:, cs], y7[:, cs], FLOAT_MAX, INF_TO, ALU.is_gt, ALU.mult)
                link(dve.tensor_scalar(below[:, cs], y7[:, cs], -FLOAT_MAX, -INF_TO, ALU.is_lt, ALU.mult))
                link(dve.tensor_tensor(ynum[:, cs], above[:, cs], below[:, cs], ALU.add))
                link(dve.copy_predicated(ynum[:, cs], finite[:, cs], y7[:, cs]))
                dve.tensor_tensor(h6[:, cs], ynum[:, cs], h5[:, cs], ALU.add).then_inc(S["h6"], 1)

        @block.scalar
        def _(act):
            def evac(dst, src, ready, n, done, bias=None):
                act.wait_ge(S[ready], n)
                if bias is None:
                    act.activation(dst, src, ACT.Copy).then_inc(S[done], 1)
                else:
                    act.activation(dst, src, ACT.Identity, bias=bias).then_inc(S[done], 1)

            def load_table(func):
                act.activation(spare[:, 1:2], spare[:, 0:1], func).then_inc(act_step, 1)
                loads[0] += 1
                act.wait_ge(act_step, loads[0])

            loads = [0]
            act.wait_ge(S["idle"], 1)
            load_table(ACT.Gelu_apprx_tanh)
            act.wait_ge(in_conv, 32)
            for h in range(2):
                evac(conv_f[:, half(h)], bank(h, 0)[0:D, 0:HALF], "conv_ps", h + 1, "conv_f", col("conv_b", D))
            for h in range(2):
                evac(h0T[0:D, half(h)], bank(h, 2)[0:D, 0:HALF], "h0_ps", h + 1, "h0T")
            for h in range(2):
                act.wait_ge(S["ff1a_ps"], h + 1)
                act.activation(g0[:, :, half(h)], bank(h, 3).rearrange("p (j t) -> p j t", j=2),
                               ACT.Gelu_apprx_tanh).then_inc(S["g0"], 1)
            load_table(ACT.Exp)
            for h in range(2):
                evac(fT[0:D, half(h)], bank(h, 0)[0:D, 0:HALF], "ff2a_ps", h + 1, "fT", col("ff_b2", D))
            for c in range(NC):
                act.wait_ge(S["s8"], c + 1)
                act.activation(s8[:, c], s8[:, c], ACT.Exp).then_inc(S["p8"], 1)
            load_table(ACT.Gelu_apprx_tanh)
            for h in range(2):
                evac(o8T[0:D, half(h)], bank(h, 0)[0:D, 0:HALF], "o8T_ps", h + 1, "o8T")
            for h in range(2):
                evac(h0T[0:D, half(h)], bank(h, 2)[0:D, 0:HALF], "h1T_ps", h + 1, "h1T")
            for h in range(2):
                act.wait_ge(S["ff1b_ps"], h + 1)
                act.activation(g0[:, :, half(h)], bank(h, 3).rearrange("p (j t) -> p j t", j=2),
                               ACT.Gelu_apprx_tanh).then_inc(S["g1"], 1)
            load_table(ACT.Exp)
            for h in range(2):
                evac(fT[0:D, half(h)], bank(h, 1)[0:D, 0:HALF], "n2T_ps", h + 1, "n2T")
            for h in range(2):
                evac(aqk[:, :, half(h)], bank(h, 2)[0:D, :].rearrange("p (w t) -> p w t", w=2), "aqk_ps", h + 1, "aqk")
            for h in range(2):
                act.wait_ge(S["sa"], h + 1)
                for c in range(2 * h, 2 * h + 2):
                    act.activation(sa[:, c], sa[:, c], ACT.Exp, bias=nmx[:, c:c + 1],
                                   accum_out=suma[:, c:c + 1]).then_inc(S["pa"], 1)
            for h in range(2):
                act.wait_ge(S["r3T_ps"], h + 1)
                act.activation(r3T[:, half(h)], bank(h, 3)[0:D, 0:HALF], ACT.Copy,
                               scale=col("ln1_w", D)).then_inc(S["r3T"], 1)
            for c in range(NC):
                act.wait_ge(S["s4"], c + 1)
                act.activation(s4[:, c], s4[:, c], ACT.Exp).then_inc(S["p4"], 1)
            for h in range(2):
                evac(pT4[:, chunks(h)], bank(h, 0).rearrange("p (c g t) -> p c g t", c=2, g=2), "pT4_ps", h + 1, "pT4")
            for h in range(2):
                evac(o4T[:, half(h)], bank(h, 2)[0:D, 0:HALF], "o4T_ps", h + 1, "o4T")
            act.wait_ge(S["lse"], 1)
            act.activation(lexp[:], lse[:], ACT.Exp).then_inc(S["lexp"], 1)
            load_table(ACT.Silu)

            def silu(i):
                act.wait_ge(S["a_ps"], i + 1)
                if i >= 2:
                    act.wait_ge(S["sb"], i - 1)
                act.activation(asil[:, i % 2], ps[:, (0, 4)[i % 2], :], ACT.Silu).then_inc(S["asil"], 1)

            def first_part(i):
                act.wait_ge(S["hgb"], i + 1)
                if i >= RING:
                    act.wait_ge(S["moe_ps"], i - RING + 1)
                act.activation(hgs[:, i % RING, 0], hgb[:, i % RING], ACT.Copy).then_inc(S["hgh"], 1)

            silu(0)
            silu(1)
            for h in range(2):
                evac(gT[:, half(h)], bank(h, 2)[0:2 * NE, 0:HALF], "gT_ps", h + 1, "gT")
            for i in range(2, LEAD):
                silu(i)
            for i in range(HC):
                if i + LEAD < HC:
                    silu(i + LEAD)
                first_part(i)
            load_table(ACT.Exp)
            act.wait_ge(S["moe_ps"], HC)
            for h in range(2):
                act.activation(moeT[:, half(h)], ps[:, 6, half(h)], ACT.Copy).then_inc(S["moeT"], 1)
            for h in range(2):
                evac(x5T[:, half(h)], bank(h, 3)[0:D, 0:HALF], "x5T_ps", h + 1, "x5T")
            for h in range(2):
                act.wait_ge(S["lkv_ps"], h + 1)
                src = bank(h, 1)[:, 0:256].rearrange("p (c w d) -> p c w d", c=2, w=2)[:, :, 0, :]
                act.activation(rk[:, chunks(h)], src, ACT.Relu)
                act.activation(ek[:, chunks(h)], src, ACT.Exp).then_inc(S["ek"], 1)
                act.wait_ge(S["lq_ps"], h + 1)
                act.activation(rq[:, half(h)], bank(h, 0)[0:D, 0:HALF], ACT.Relu)
                act.activation(eq[:, half(h)], bank(h, 0)[0:D, 0:HALF], ACT.Exp).then_inc(S["eq"], 1)
            load_table(ACT.Gelu)
            for h in range(2):
                evac(x1T[0:D, half(h)], bank(h, 0)[0:D, 0:HALF], "x1T_ps", h + 1, "x1T")
            for h in range(2):
                act.wait_ge(S["l1h_ps"], h + 1)
                act.activation(g5[0:D, half(h)], bank(h, 1)[0:D, 0:HALF], ACT.Gelu).then_inc(S["g5"], 1)
            load_table(ACT.Exp)
            for h in range(2):
                evac(x7T[0:D, half(h)], bank(h, 3)[0:D, 0:HALF], "x7T_ps", h + 1, "x7T")
            for h in range(2):
                act.wait_ge(S["lse1"], h + 1)
                act.activation(lex1[:, chunks(h)], lse1[:, chunks(h)], ACT.Exp).then_inc(S["lex1"], 1)
            for i in range(2):
                act.wait_ge(S["bufT_ps"], i + 1)
                act.activation(bufT[:, 4 * i:4 * i + 4], ps[:, (2, 6)[i], 0:4 * CAP].rearrange("p (e s) -> p e s", e=4),
                               ACT.Copy).then_inc(S["bufT"], 1)
            for e in range(NE):
                act.wait_ge(S["hid_ps"], e + 1)
                k = COLS["moe_b1"][0] + 2 * e
                act.activation(hid[:, e, 0], ps[:, (0, 4)[e % 2], 0:CAP], ACT.Relu,
                               bias=cols_s[:, k:k + 1]).then_inc(S["hid"], 1)
            act.wait_ge(S["prob"], 1)
            for h in range(2):
                act.wait_ge(S["comb_ps"], h + 1)
                for c in range(2):
                    last = act.activation(ylow[:, 2 * h + c], ps[:, (1, 7)[h], c * P + D:(c + 1) * P], ACT.Copy,
                                          scale=prob[:, 2 * h + c:2 * h + c + 1])
                last.then_inc(S["ylow"], 1)

        @block.tensor
        def _(pe):
            def flip(dst, src, n=P):
                return pe.transpose(dst, src, con_s[0:n, 0:n])

            def keep_clock(awaited, i):
                n, b = KEEP_CLOCK.get((awaited, i), (0, 0))
                for _ in range(n):
                    pe.matmul(ps[:, b, 0:HALF], idle[:, 0:P], idle[:, 0:HALF], start=True, stop=True)

            pe.wait_ge(S["idle"], 1)
            keep_clock("in_conv", 0)
            pe.wait_ge(in_conv, 32)
            for n, at in enumerate(PAT_PARTS):
                pe.wait_ge(in_pat[n], 16)
                for h in range(2):
                    for k in range(at.start, at.stop):
                        last = pe.matmul(bank(h, 0)[0:D, 0:HALF], wconv_s[:, k, :], pat_s[:, k, half(h)],
                                         start=(k == 0), stop=(k == KC - 1))
                    if at.stop == KC:
                        last.then_inc(S["conv_ps"], 1)
            keep_clock("in_small", 0)
            pe.wait_ge(in_small, 32)
            for h in range(2):
                keep_clock("conv_f", h)
                pe.wait_ge(S["conv_f"], h + 1)
                for c in range(2):
                    last = flip(bank(h, 1)[:, c * D:(c + 1) * D], conv_f[:, tok(2 * h + c)], D)
                last.then_inc(S["conv_t"], 1)

            def rows_to_features(h, b, src, ready, done, need=None):
                keep_clock(ready, h)
                pe.wait_ge(S[ready], need if need else h + 1)
                for c in range(2):
                    last = flip(bank(h, b)[0:D, tok(c)], src[:, 2 * h + c, :])
                last.then_inc(S[done], 1)

            for h in range(2):
                rows_to_features(h, 2, h0, "h0", "h0_ps")
            keep_clock("in_w", 0)
            pe.wait_ge(in_w, 48)
            pe.wait_ge(S["setup"], 2)

            def ff1(h, src, ready, done):
                keep_clock(ready, h)
                pe.wait_ge(S[ready], h + 1)
                for j in range(2):
                    last = pe.matmul(bank(h, 3)[:, j * HALF:(j + 1) * HALF], w5("ff1")[:, j * P:(j + 1) * P],
                                     src[:, half(h)], start=True, stop=True)
                last.then_inc(S[done], 1)

            for h in range(2):
                ff1(h, h0T, "h0T", "ff1a_ps")
            for h in range(2):
                keep_clock("g0", h)
                pe.wait_ge(S["g0"], h + 1)
                for j in range(2):
                    last = pe.matmul(bank(h, 0)[0:D, 0:HALF], ff2_s[:, j, :], g0[:, j, half(h)],
                                     start=(j == 0), stop=(j == 1))
                last.then_inc(S["ff2a_ps"], 1)
            for h in range(2):
                keep_clock("fT", h)
                pe.wait_ge(S["fT"], h + 1)
                pe.matmul(bank(h, 1)[:, 0:HALF], w5("q8"), fT[:, half(h)], start=True, stop=True)
                pe.matmul(bank(h, 1)[:, HALF:T], w5("k8"), fT[:, half(h)], start=True,
                          stop=True).then_inc(S["qk8_ps"], 1)
                for b in range(4):
                    t0 = h * HALF + b * N
                    for i in range(2):
                        last = pe.matmul(bank(h, 2)[i * N:(i + 1) * N, b * D:(b + 1) * D], fT[:, t0:t0 + N],
                                         w5("v8"), start=True, stop=True)
                last.then_inc(S["v8_ps"], 1)
            for c in range(NC):
                keep_clock("k8x", c)
                pe.wait_ge(S["k8x"], c // 2 + 1)
                pe.matmul(bank(c // 2, (3, 0)[c % 2]), q_bd[:, c, :], k8x[:, c].rearrange("p g k -> p (g k)"),
                          start=True, stop=True).then_inc(S["s8_ps"], 1)
            for c in range(NC):
                keep_clock("p8", c)
                pe.wait_ge(S["p8"], c + 1)
                if c % 2:
                    keep_clock("v8", c)
                    pe.wait_ge(S["v8"], c // 2 + 1)
                for g in range(4):
                    last = flip(bank(c // 2, (1, 2)[c % 2])[:, g * P:(g + 1) * P],
                                s8[:, c].rearrange("p g k -> p (g k)")[:, g * P:(g + 1) * P])
                last.then_inc(S["pT8_ps"], 1)
            for c in range(NC):
                keep_clock("pT8", c)
                pe.wait_ge(S["pT8"], c + 1)
                pe.wait_ge(S["v8"], c // 2 + 1)
                pe.wait_ge(S["s8"], min(NC, 2 * (c // 2) + 2))
                for i in range(2):
                    for g in range(4):
                        at = (c % 2) * 72 + g * 18
                        last = pe.matmul(bank(c // 2, 3)[i * N:(i + 1) * N, at:at + 18],
                                         pT8[:, c, g, i * N:(i + 1) * N], v8[:, 2 * c + i, g, :], start=True, stop=True)
                last.then_inc(S["o8_ps"], 1)
            for h in range(2):
                rows_to_features(h, 0, o8, "o8", "o8T_ps", 2 * h + 2)
            for h in range(2):
                keep_clock("o8T", h)
                pe.wait_ge(S["o8T"], h + 1)
                for c in range(2):
                    last = pe.matmul(bank(h, 1)[:, c * D:(c + 1) * D], o8T[:, tok(2 * h + c)], w5("proj"),
                                     start=True, stop=True)
                last.then_inc(S["proj_ps"], 1)
            for h in range(2):
                rows_to_features(h, 2, h1, "h1", "h1T_ps")
            for h in range(2):
                ff1(h, h0T, "h1T", "ff1b_ps")
            for h in range(2):
                keep_clock("g1", h)
                pe.wait_ge(S["g1"], h + 1)
                for c in range(2):
                    for j in range(2):
                        last = pe.matmul(bank(h, 0)[:, c * D:(c + 1) * D], g0[:, j, tok(2 * h + c)], ff2_s[:, j, :],
                                         start=(j == 0), stop=(j == 1))
                last.then_inc(S["ff2b_ps"], 1)
            for h in range(2):
                rows_to_features(h, 1, n2, "n2", "n2T_ps")
            for h in range(2):
                keep_clock("n2T", h)
                pe.wait_ge(S["n2T"], h + 1)
                pe.matmul(bank(h, 2)[0:D, 0:HALF], w5("aq"), fT[:, half(h)], start=True, stop=True)
                pe.matmul(bank(h, 2)[0:D, HALF:T], w5("ak"), fT[:, half(h)], start=True,
                          stop=True).then_inc(S["aqk_ps"], 1)
                for c in range(2):
                    last = pe.matmul(bank(h, 3)[:, c * D:(c + 1) * D], fT[:, tok(2 * h + c)], w5("av"),
                                     start=True, stop=True)
                last.then_inc(S["av_ps"], 1)
            for h in range(2):
                keep_clock("aqk", h)
                pe.wait_ge(S["aqk"], h + 1)
                for c in range(2):
                    last = pe.matmul(bank(h, 0)[:, c * P:(c + 1) * P], aqk[:, 0, tok(2 * h + c)],
                                     aqk[:, 1, tok(2 * h + c)], start=True, stop=True)
                last.then_inc(S["sa_ps"], 1)
            for h in range(2):
                keep_clock("pa", h)
                pe.wait_ge(S["pa"], 2 * h + 2)
                for c in range(2):
                    last = flip(bank(h, 1)[:, c * P:(c + 1) * P], sa[:, 2 * h + c, :])
                last.then_inc(S["paT_ps"], 1)
            for h in range(2):
                keep_clock("paT", h)
                pe.wait_ge(S["paT"], h + 1)
                pe.wait_ge(S["av"], h + 1)
                for c in range(2):
                    last = pe.matmul(bank(h, 2)[:, c * D:(c + 1) * D], paT[:, 2 * h + c, :], av[:, 2 * h + c, :],
                                     start=True, stop=True)
                last.then_inc(S["oa_ps"], 1)
            for h in range(2):
                rows_to_features(h, 3, r3, "r3", "r3T_ps")
            for h in range(2):
                keep_clock("r3T", h)
                pe.wait_ge(S["r3T"], h + 1)
                for w, (a, b, done) in enumerate((("fq", "fqr", "q4_ps"), ("fk", "fkr", "k4_ps"))):
                    pe.matmul(bank(h, w)[:, 0:HALF], w4(a), r3T[:, half(h)], start=True, stop=True)
                    pe.matmul(bank(h, w)[:, HALF:T], w4(b), r3T[:, half(h)], start=True,
                              stop=True).then_inc(S[done], 1)
                for b in range(4):
                    t0 = h * HALF + b * N
                    for i in range(2):
                        last = pe.matmul(bank(h, 2)[i * N:(i + 1) * N, b * D:(b + 1) * D], r3T[:, t0:t0 + N],
                                         w4("fv"), start=True, stop=True)
                last.then_inc(S["v4_ps"], 1)
            for c in range(NC):
                keep_clock("k4x", c)
                pe.wait_ge(S["k4x"], c // 2 + 1)
                pe.matmul(bank(c // 2, 3)[:, (c % 2) * 256:(c % 2 + 1) * 256], q4_bd[:, c, :],
                          k4x[:, c].rearrange("p g k -> p (g k)"), start=True, stop=True).then_inc(S["s4_ps"], 1)
            for h in range(2):
                for c in range(2 * h, 2 * h + 2):
                    keep_clock("p4", c)
                    pe.wait_ge(S["p4"], c + 1)
                    for g in range(2):
                        at = (c % 2) * 256 + g * P
                        last = flip(bank(h, 0)[:, at:at + P],
                                    s4[:, c].rearrange("p g k -> p (g k)")[:, g * P:(g + 1) * P])
                last.then_inc(S["pT4_ps"], 1)
            for c in range(NC):
                keep_clock("pT4", c)
                pe.wait_ge(S["pT4"], c // 2 + 1)
                pe.wait_ge(S["v4"], c // 2 + 1)
                for i in range(2):
                    for g in range(2):
                        at = (c % 2) * 68 + g * 34
                        last = pe.matmul(bank(c // 2, 1)[i * N:(i + 1) * N, at:at + 34],
                                         pT4[:, c, g, i * N:(i + 1) * N], v4[:, 2 * c + i, g, :], start=True, stop=True)
                last.then_inc(S["o4_ps"], 1)
            for h in range(2):
                rows_to_features(h, 2, o4, "o4", "o4T_ps", 2 * h + 2)
            for h in range(2):
                keep_clock("o4T", h)
                pe.wait_ge(S["o4T"], h + 1)
                for c in range(2):
                    last = pe.matmul(bank(h, 3)[:, c * D:(c + 1) * D], o4T[:, tok(2 * h + c)], w4("fo"),
                                     start=True, stop=True)
                last.then_inc(S["wo_ps"], 1)
            for h in range(2):
                keep_clock("fl", h)
                pe.wait_ge(S["fl"], h + 1)
                for c in range(2):
                    last = flip(bank(h, 0)[:, tok(c)], fl[:, 2 * h + c].rearrange("p w d -> p (w d)"))
                last.then_inc(S["flT_ps"], 1)
            keep_clock("fs", 0)
            pe.wait_ge(S["fs"], 2)
            for c in range(NC):
                last = pe.matmul(ps[:, 1, c * NE:(c + 1) * NE], flT[0:D, tok(c)], w4("router"), start=True, stop=True)
            last.then_inc(S["rt_ps"], 1)
            keep_clock("split", 0)
            pe.wait_ge(S["split"], 4)

            def up(i):
                if i >= 2:
                    pe.wait_ge(S["asil"], i - 1)
                    pe.wait_ge(S["sb"], i - 1)
                for j, b, done in ((0, (0, 4)[i % 2], "a_ps"), (1, (3, 7)[i % 2], "b_ps")):
                    pe.matmul(ps[:, b, :], f13h[:, j, i * P:(i + 1) * P], fs[:], start=True, stop=False)
                    pe.matmul(ps[:, b, :], f13l[:, j, i * P:(i + 1) * P], fs[:], start=False,
                              stop=True).then_inc(S[done], 1)

            def gates(i):
                if i >= 2:
                    pe.wait_ge(S["hgb"], i - 1)
                pe.matmul(ps[:, (1, 5)[i % 2], :], sel_s[:, i * P:(i + 1) * P], gT[:], start=True,
                          stop=True).then_inc(S["gc_ps"], 1)

            up(0)
            up(1)
            keep_clock("gpart", 0)
            pe.wait_ge(S["gpart"], 1)
            for h in range(2):
                for c in range(2):
                    last = flip(bank(h, 2)[0:2 * NE, tok(c)],
                                gpart[:, 2 * h + c].rearrange("p w e -> p (w e)").bitcast(F32))
                last.then_inc(S["gT_ps"], 1)
            keep_clock("gT", 0)
            pe.wait_ge(S["gT"], 2)

            def down(i):
                pe.wait_ge(S["hgl"], i + 1)
                both = fw2s[:, i].rearrange("p w d -> p (w d)")
                pe.matmul(ps[:, 6, :], both, hgs[:, i % RING, 0], start=(i == 0), stop=False)
                pe.matmul(ps[:, 6, :], both, hgs[:, i % RING, 1], start=False,
                          stop=(i == HC - 1)).then_inc(S["moe_ps"], 1)

            for i in range(2, LEAD):
                up(i)
            for i in range(HC + LAG):
                if i < HC:
                    gates(i)
                if i + LEAD < HC:
                    up(i + LEAD)
                if i >= LAG:
                    down(i - LAG)
            for h in range(2):
                keep_clock("moeT", h)
                pe.wait_ge(S["moeT"], h + 1)
                for c in range(2):
                    last = flip(bank(h, 1)[:, tok(c)], moeT[:, tok(2 * h + c)])
                last.then_inc(S["moeTb_ps"], 1)
            for h in range(2):
                rows_to_features(h, 3, x5, "x5", "x5T_ps")
            for h in range(2):
                keep_clock("x5T", h)
                pe.wait_ge(S["x5T"], h + 1)
                for c in range(2):
                    last = pe.matmul(bank(h, 1)[:, c * P:(c + 1) * P], x5T[:, tok(2 * h + c)], w4("lkv"),
                                     start=True, stop=True)
                last.then_inc(S["lkv_ps"], 1)
                pe.matmul(bank(h, 0)[0:D, 0:HALF], w4("lq"), x5T[:, half(h)], start=True,
                          stop=True).then_inc(S["lq_ps"], 1)
            for h in range(2):
                keep_clock("phk", h)
                pe.wait_ge(S["phk"], h + 1)
                for c in range(2):
                    last = pe.matmul(bank(h, 2)[0:D, c * 144:(c + 1) * 144], phk[:, 2 * h + c, :],
                                     v1[:, 2 * h + c].rearrange("p i d -> p (i d)"), start=True, stop=True)
                last.then_inc(S["kv_ps"], 1)
            for h in range(2):
                keep_clock("phq", h)
                pe.wait_ge(S["phq"], h + 1)
                pe.wait_ge(S["kv"], h + 1)
                for b in range(4):
                    last = pe.matmul(bank(h, 3)[(b % 2) * N:(b % 2 + 1) * N, (b // 2) * 72:(b // 2 + 1) * 72],
                                     phq[:, h * HALF + b * N:h * HALF + (b + 1) * N], kv[:, 4 * h + b, :],
                                     start=True, stop=True)
                last.then_inc(S["t5_ps"], 1)
            keep_clock("late_setup", 0)
            pe.wait_ge(S["late_setup"], 4)
            for h in range(2):
                rows_to_features(h, 0, x1, "x1", "x1T_ps")
            for h in range(2):
                keep_clock("x1T", h)
                pe.wait_ge(S["x1T"], h + 1)
                pe.matmul(bank(h, 1)[0:D, 0:HALF], w5("l1w1"), x1T[:, half(h)], start=True,
                          stop=True).then_inc(S["l1h_ps"], 1)
            for h in range(2):
                keep_clock("g5", h)
                pe.wait_ge(S["g5"], h + 1)
                for c in range(2):
                    last = pe.matmul(bank(h, 2)[:, c * D:(c + 1) * D], g5[:, tok(2 * h + c)], w5("l1w2"),
                                     start=True, stop=True)
                last.then_inc(S["l1y_ps"], 1)
            for h in range(2):
                rows_to_features(h, 3, x7, "x7", "x7T_ps")
            for h in range(2):
                keep_clock("x7T", h)
                pe.wait_ge(S["x7T"], h + 1)
                for c in range(2):
                    last = pe.matmul(bank(h, 0)[:, c * NE:(c + 1) * NE], x7T[:, tok(2 * h + c)], w5("gate"),
                                     start=True, stop=True)
                last.then_inc(S["g_ps"], 1)
            for h in range(2):
                keep_clock("oh1b", h)
                pe.wait_ge(S["oh1b"], h + 1)
                for c in range(2 * h, 2 * h + 2):
                    dst = bank(h, 1)[:, (c % 2) * NE:(c % 2 + 1) * NE]
                    for c0 in range(c):
                        pe.matmul(dst, tri_s[:, 1, :], oh1b[:, c0], start=(c0 == 0), stop=False)
                    last = pe.matmul(dst, tri_s[:, 0, :], oh1b[:, c], start=(c == 0), stop=True)
                last.then_inc(S["cum_ps"], 1)
            for c in range(NC):
                keep_clock("disp", c)
                pe.wait_ge(S["disp"], c + 1)
                for i in range(2):
                    last = pe.matmul(ps[:, (2, 6)[i], 0:4 * CAP], x7s[:, c].rearrange("p w d -> p (w d)"),
                                     disp[:, c, 4 * i:4 * i + 4].rearrange("p e s -> p (e s)"),
                                     start=(c == 0), stop=(c == NC - 1))
                    if c == NC - 1:
                        last.then_inc(S["bufT_ps"], 1)
            keep_clock("code", 0)
            pe.wait_ge(S["code"], 1)
            for c in range(NC):
                last = pe.matmul(ps[0:CAP, 3, tok(c)], code[:, c:c + 1].to_broadcast([P, CAP]), ident,
                                 start=True, stop=True)
            last.then_inc(S["cod_ps"], 1)

            def outputs(e):
                pe.wait_ge(S["hid"], e + 1)
                pe.wait_ge(S["hid_dve"], e + 1)
                for j in range(2):
                    last = pe.matmul(ps[0:CAP, (5, 3)[e // 4], (e % 4) * D:(e % 4 + 1) * D], hid[:, e, j],
                                     m2_s[:, e, j, :], start=(j == 0), stop=(j == 1))
                if e % 4 == 3:
                    last.then_inc(S["y_ps"], 1)

            for e in range(NE):
                keep_clock("bufT", e)
                pe.wait_ge(S["bufT"], 2 if e else 1)
                if e >= 2:
                    keep_clock("hid", e)
                    pe.wait_ge(S["hid"], e - 1)
                    pe.wait_ge(S["hid_dve"], e - 1)
                for j in range(2):
                    dst = ps[:, ((0, 4), (2, 6))[j][e % 2], 0:CAP]
                    pe.matmul(dst, m1h[:, e, j * P:(j + 1) * P], bufT[:, e], start=True, stop=False)
                    last = pe.matmul(dst, m1l[:, e, j * P:(j + 1) * P], bufT[:, e], start=False, stop=True)
                last.then_inc(S["hid_ps"], 1)
                if e >= 2:
                    outputs(e - 2)
            outputs(NE - 2)
            outputs(NE - 1)
            keep_clock("combT", 0)
            pe.wait_ge(S["combT"], len(COMB_DVE))
            pe.wait_ge(S["combT_pool"], NE - len(COMB_DVE))
            pe.wait_ge(S["ybs"], 2)
            for h in range(2):
                for c in range(2):
                    for e in range(NE):
                        last = pe.matmul(ps[:, (1, 7)[h], c * P:(c + 1) * P], combT[:, e, tok(2 * h + c)],
                                         ybs[:, e].rearrange("p w d -> p (w d)"), start=(e == 0), stop=(e == NE - 1))
                last.then_inc(S["comb_ps"], 1)


def constants():
    f = np.float32
    con = np.zeros((P, CON_N), f)

    def put(name, a):
        a = np.asarray(a, f)
        con[:a.shape[0], CON[name][0]:CON[name][1]] = a

    feat = np.arange(P) % D
    side = np.arange(P) // D
    put("ident", np.eye(P))
    put("mask8", (feat[:, None] // 8 == np.arange(8)) / np.sqrt(8.0))
    put("vmask8", (np.arange(D)[None] // 8 % 2) == side[:, None])
    put("mask4", (feat[:, None] // 16 == np.arange(4)) / np.sqrt(16.0))
    put("vmask4", (np.arange(D)[None] // 16 % 2) == side[:, None])
    inv = (1.0 / 10000.0 ** (np.arange(0, 16, 2, dtype=f) / 16)).astype(f)
    freqs = np.outer(np.arange(N, dtype=f), inv)
    emb = np.concatenate([freqs, freqs], -1)
    sign = np.where(np.arange(16) < 8, -1.0, 1.0)
    put("cos", np.cos(emb).T[feat % 16])
    put("sin", (np.sin(emb) * sign).T[feat % 16])
    put("causal", np.where(np.arange(N)[None] <= feat[:, None], 0.0, NEG))
    put("pair", np.where(side[:, None] == side[None], 0.0, NEG))
    bm = np.zeros((D, 72))
    bm[:, :D] = np.arange(D)[:, None] // 8 == np.arange(D)[None] // 8
    bm[:, D:] = np.arange(D)[:, None] // 8 == np.arange(8)[None]
    put("bm", bm)
    put("iota8", np.tile(np.arange(NE), (P, 1)))
    put("slots", np.tile(np.arange(1, CAP + 1), (P, 1)))
    put("slotid", np.arange(1, P + 1)[:, None])
    put("expert", np.tile(128 * np.arange(NE) + 0, (P, 1)))
    expert = np.minimum(np.arange(HC * P) // HID, NE - 1)
    sel = np.tile(expert[None] == np.arange(NE)[:, None], (2, 1)).astype(f)
    tri = np.stack([np.triu(np.ones((P, P))), np.ones((P, P))], 1).astype(f)
    pos = np.arange(N, dtype=f)[:, None]
    div = np.exp(-np.log(f(10000.0)) * np.arange(0, D, 2, dtype=f) / D).astype(f)
    ang = (pos * div).astype(f)
    pe = np.stack([np.sin(ang), np.cos(ang)], -1).reshape(N, D).astype(f)
    return con, sel, tri, np.tile(pe, (2, 1))


def kernel(**inputs):
    import concourse.bacc as _bacc
    from concourse.bass_utils import run_bass_kernel_spmd as _run

    a = {k: np.asarray(v) for k, v in inputs.items()}
    f = np.float32
    con, sel, tri, pe = constants()

    pat = a["x"].reshape(B, 3, 8, 2, 8, 8, 16).transpose(4, 6, 1, 3, 0, 2, 5).reshape(P, KC, T)
    wconv = a["L0_tok_conv_w"].reshape(D, 3, 2, 8, 16).transpose(3, 4, 1, 2, 0).reshape(P, KC, D)

    def bcast(v):
        return np.broadcast_to(v[None], (P, D))

    rows = np.concatenate([bcast(a["L0_tok_ln_w"]), bcast(a["L0_tok_ln_b"]), pe, bcast(a["L0_tok_ff_b2"]),
                           bcast(a["L1_attn_ln1_g"]), bcast(a["L1_attn_ln1_b"]), bcast(a["L1_attn_ln2_g"]),
                           bcast(a["L1_attn_ln2_b"])], 1)
    cols = np.concatenate([np.tile(a["L0_tok_conv_b"], 2)[:, None], np.tile(a["L0_tok_ff_b2"], 2)[:, None],
                           np.tile(a["L0_ffn_ln1_w"], 2)[:, None], np.tile(a["L0_ffn_ln2_w"], 2)[:, None],
                           a["L1_ffn_b1"].reshape(NE * 2, P).T], 1)

    def with_bias(w, b):
        return np.concatenate([w, b[None]], 0)

    qkv, qkvb = a["L0_tok_qkv_w"].T, a["L0_tok_qkv_b"]
    q8, k8, v8 = (with_bias(qkv[:, i * D:(i + 1) * D], qkvb[i * D:(i + 1) * D]) for i in range(3))
    w65 = np.concatenate([with_bias(a["L0_tok_ff_w1"].T, a["L0_tok_ff_b1"]), q8, q8, k8, k8, v8,
                          with_bias(a["L0_tok_proj_w"].T, a["L0_tok_proj_b"]),
                          with_bias(a["L0_attn_Wq"], a["L0_attn_bq"]), with_bias(a["L0_attn_Wk"], a["L0_attn_bk"]),
                          with_bias(a["L0_attn_Wv"], a["L0_attn_bv"]), with_bias(a["L1_attn_W1"].T, a["L1_attn_b1"]),
                          with_bias(a["L1_attn_W2"].T, a["L1_attn_b2"]),
                          with_bias(a["L1_ffn_gate_w"], a["L1_ffn_gate_b"])], 1)
    head = np.arange(D) // 16
    other = (np.arange(D) % 16 + 8) % 16
    fq = a["L0_ffn_wq"].T
    fk = a["L0_ffn_wk"].T[:, head // 2 * 16 + np.arange(D) % 16]
    fkr = a["L0_ffn_wk"].T[:, head // 2 * 16 + other]
    fqr = fq[:, head * 16 + other]
    fv = a["L0_ffn_wv"].T[:, head // 2 * 16 + np.arange(D) % 16]
    wl = a["L1_attn_Wqkv"].T
    w64 = np.concatenate([fq, fq, fqr, fqr, fk, fk, fkr, fkr, fv, a["L0_ffn_wo"].T, a["L0_ffn_router_w"].T,
                          wl[:, 0:D], wl[:, D:3 * D]], 1)
    ff2 = a["L0_tok_ff_w2"].T.reshape(2, P, D).transpose(1, 0, 2)
    pad = HC * P - NE * HID

    def stacked(w):
        w = np.pad(w.reshape(NE * HID, D).T, ((0, 0), (0, pad)))
        return np.concatenate([w, w], 0)

    f13 = np.stack([stacked(a["L0_ffn_w1"]), stacked(a["L0_ffn_w3"])], 1)
    fw2 = np.pad(a["L0_ffn_w2"].transpose(0, 2, 1).reshape(NE * HID, D), ((0, pad), (0, 0)))
    fw2 = fw2.reshape(HC, P, D).transpose(1, 0, 2)
    m1 = np.tile(a["L1_ffn_w1"].transpose(1, 0, 2), (2, 1, 1))
    m2 = a["L1_ffn_w2"].reshape(NE, 2, P, D).transpose(2, 0, 1, 3)
    mb2 = np.broadcast_to(a["L1_ffn_b2"][None], (CAP, NE, D))
    sent = dict(pat=pat, wconv=wconv, rows=rows, cols=cols, w65=w65, w64=w64, ff2=ff2, f13=f13, fw2=fw2, m1=m1, m2=m2,
                mb2=mb2, con=con, sel=sel, tri=tri)

    nc = _bacc.Bacc("TRN2", target_bir_lowering=False, num_devices=1)
    arrays, args = {}, {}
    for name, v in sent.items():
        v = np.ascontiguousarray(v)
        arrays[f"in_{name}"] = v
        args[name] = nc.dram_tensor(f"in_{name}", v.shape, mybir.dt.from_np(v.dtype), kind="ExternalInput").ap()
    args["out"] = nc.dram_tensor("out_0", (T, D), F32, kind="ExternalOutput").ap()
    vit_tower(nc, **args)
    r = _run(nc, [arrays], core_ids=[0])
    return r.results[0]["out_0"].reshape(B, N, D)
```

```python
from contextlib import ExitStack

import numpy as np

import concourse.bass as bass
from concourse import mybir

F32 = mybir.dt.float32
F32R = mybir.dt.float32r
BF16 = mybir.dt.bfloat16
U32 = mybir.dt.uint32
ALU = mybir.AluOpType
ACT = mybir.ActivationFunctionType
AX_X = mybir.AxisListType.X

P = 128
B, D, N = 8, 64, 64
T = B * N
NC = T // P
KC = 3 * 16 * 16 // P
HF = 256
NE = 8
HID = int(8 / 3 * D)
HC = -(-NE * HID // P)
HALF = T // 2
CAP = -(-5 * T // (4 * NE))
NEG = -1e30
COMB_DVE = (1, 2, 3, 4, 5, 7)
COMB_BANK = (0, 1, 6, 7)
LOW_DVE = (8, 10)
NORMS = ["emb", "pre_attn", "pre_ffn", "rms", "pre_l1", "l1a", "l1b", "pre_moe"]
KEEP_CLOCK = {
    ("in_conv", 0): (17, 1), ("conv_f", 0): (14, 1), ("conv_f", 1): (10, 0), ("g0", 0): (4, 0), ("fT", 1): (7, 0),
    ("p8", 1): (18, 2), ("o8T", 0): (7, 1), ("g1", 0): (4, 0), ("n2T", 0): (14, 0), ("r3T", 0): (10, 0),
    ("p4", 0): (4, 0), ("pT4", 2): (14, 0), ("fl", 0): (10, 0), ("fs", 0): (10, 1), ("moeT", 0): (4, 0),
    ("x5T", 0): (7, 0), ("late_setup", 0): (10, 0), ("g5", 1): (1, 0), ("oh1b", 1): (10, 0), ("disp", 0): (7, 0),
}
RING = 5
LEAD = 2
LAG = 4
PAT_PARTS = [slice(0, 2), slice(2, 4), slice(4, KC)]
FLOAT_MAX = float(np.finfo(np.float32).max)
INF_TO = 1e4


def layout(parts):
    at, n = {}, 0
    for name, width in parts:
        at[name] = (n, n + width)
        n += width
    return at, n


ROWS, ROWS_N = layout([("ln_w", D), ("ln_b", D), ("pe", D), ("ff_b2", D), ("ln1_g", D), ("ln1_b", D),
                       ("ln2_g", D), ("ln2_b", D)])
COLS, COLS_N = layout([("conv_b", 1), ("ff_b2", 1), ("ln1_w", 1), ("ln2_w", 1), ("moe_b1", 2 * NE)])
W65, W65_N = layout([("ff1", HF), ("q8", D), ("k8", D), ("v8", D), ("proj", D), ("aq", D), ("ak", D), ("av", D),
                     ("l1w1", D), ("l1w2", D), ("gate", NE)])
W64, W64_N = layout([("fq", D), ("fqr", D), ("fk", D), ("fkr", D), ("fv", D), ("fo", D), ("router", NE),
                     ("lq", D), ("lkv", P)])
CON, CON_N = layout([("ident", P), ("mask8", 8), ("vmask8", D), ("mask4", 4), ("vmask4", D), ("cos", N),
                     ("sin", N), ("causal", N), ("pair", P), ("bm", 72), ("iota8", NE), ("slots", CAP),
                     ("slotid", 1), ("expert", NE), ("both", D)])


def vit_tower(nc: bass.Bass, pat, wconv, rows, cols, w65, w64, ff2, f13, fw2, m1, m2, mb2, con, sel, tri, out):
    with ExitStack() as ctx:
        def sb(name, shape, dt=F32):
            return ctx.enter_context(nc.sbuf_tensor(name, shape, dt))

        def sem(name):
            return ctx.enter_context(nc.semaphore(name))

        ps = ctx.enter_context(nc.psum_tensor("ps", [P, 8, 512], F32))

        rows_s = sb("rows_s", [P, ROWS_N])
        cols_s = sb("cols_s", [P, COLS_N])
        w65_s = sb("w65_s", [D + 1, W65_N])
        w64_s = sb("w64_s", [D, W64_N])
        ff2_s = sb("ff2_s", [P, 2, D])
        fw2s = sb("fw2s", [P, HC, 2, D], F32R)
        m2_s = sb("m2_s", [P, NE, 2, D])
        mb2_s = sb("mb2_s", [CAP, NE, D])
        con_s = sb("con_s", [P, CON_N])
        sel_s = sb("sel_s", [2 * NE, HC * P], F32R)
        tri_s = sb("tri_s", [P, 2, P], BF16)
        ident_b = sb("ident_b", [P, P], BF16)
        ident_r = sb("ident_r", [P, P], F32R)
        causal_b = sb("causal_b", [P, N], BF16)
        pair_b = sb("pair_b", [P, P], BF16)

        def row(name):
            return rows_s[:, ROWS[name][0]:ROWS[name][1]]

        def col(name, n=P):
            return cols_s[0:n, COLS[name][0]:COLS[name][1]]

        def w5(name):
            return w65_s[:, W65[name][0]:W65[name][1]]

        def w4(name):
            return w64_s[:, W64[name][0]:W64[name][1]]

        def con_(name, n=P):
            return con_s[0:n, CON[name][0]:CON[name][1]]

        ident = con_("ident")
        idle = sb("idle", [P, 512], BF16)
        spare = sb("spare", [1, 2])
        f13h = sb("f13h", [P, 2, HC * P], F32R)
        f13l = sb("f13l", [P, 2, HC * P], F32R)
        m1h = sb("m1h", [P, NE, 2 * P], F32R)
        m1l = sb("m1l", [P, NE, 2 * P], F32R)

        lnb_pe = sb("lnb_pe", [P, D])
        mhalf = sb("mhalf", [P, 2 * NC])

        def stats_tiles(name):
            return sb(name + "_st", [P, NC, 6]), sb(name + "_mv", [P, NC, 2]), sb(name + "_ve", [P, NC, 2]), \
                sb(name + "_rs", [P, NC, 2])

        ln = {k: stats_tiles(k) for k in NORMS}
        yn = sb("yn", [P, NC, D])
        h0 = sb("h0", [P, NC, D])
        mx8 = sb("mx8", [P, NC, 8])
        ri8 = sb("ri8", [P, NC, 4, 2])
        o8 = sb("o8", [P, NC, D])
        h1 = sb("h1", [P, NC, D])
        h1b = sb("h1b", [P, NC, D])
        h2 = sb("h2", [P, NC, D])
        n2 = sb("n2", [P, NC, D])
        av = sb("av", [P, NC, D])
        nmx = sb("nmx", [P, NC])
        suma = sb("suma", [P, NC])
        ria = sb("ria", [P, NC])
        h3 = sb("h3", [P, NC, D])
        x3 = sb("x3", [P, NC, D])
        r3 = sb("r3", [P, NC, D])
        q4_bd = sb("q4_bd", [P, NC, P])
        k4 = sb("k4", [P, NC, N])
        v4 = sb("v4", [P, B, 2, 34])
        mx4 = sb("mx4", [P, NC, 4])
        ri4 = sb("ri4", [P, NC, 2, 2])
        o4 = sb("o4", [P, NC, D])
        x4 = sb("x4", [P, NC, D])
        hx = sb("hx", [P, NC, D])
        fl = sb("fl", [P, NC, 2, D])
        flT = sb("flT", [P, T])
        fs = sb("fs", [P, T], F32R)
        top8 = sb("top8", [P, NC, 8])
        topi = sb("topi", [P, NC, 8], U32)
        lse = sb("lse", [P, NC, 8])
        lexp = sb("lexp", [P, NC, 8])
        lsum = sb("lsum", [P, NC])
        oh = sb("oh", [P, NC, 8])
        oh2 = sb("oh2", [P, NC, 8])
        wsel = sb("wsel", [P, NC, 8])
        wtot = sb("wtot", [P, NC])
        wden = sb("wden", [P, NC])
        winv = sb("winv", [P, NC])
        gat = sb("gat", [P, NC, 8])
        gpart = sb("gpart", [P, NC, 2, 8], F32R)
        gT = sb("gT", [2 * NE, T], F32R)
        h4 = sb("h4", [P, NC, D])
        x5 = sb("x5", [P, NC, D])
        zden = sb("zden", [P, NC, 8])
        z = sb("z", [P, NC, 8])
        h5 = sb("h5", [P, NC, D])
        top1 = sb("top1", [P, NC, 8])
        toi1 = sb("toi1", [P, NC, 8], U32)
        lse1 = sb("lse1", [P, NC, 8])
        lex1 = sb("lex1", [P, NC, 8])
        lsu1 = sb("lsu1", [P, NC])
        prob = sb("prob", [P, NC])
        oh1 = sb("oh1", [P, NC, 8])
        oh1b = sb("oh1b", [P, NC, 8], BF16)
        code = sb("code", [P, NC])
        code_r = sb("code_r", [P, NC], F32R)

        with ExitStack() as first_stages:
            def early(name, shape, dt=F32):
                return first_stages.enter_context(nc.sbuf_tensor(name, shape, dt))

            pat_s = early("pat_s", [P, KC, T])
            wconv_s = early("wconv_s", [P, KC, D])
            conv_f = early("conv_f", [P, HALF])
            g0 = early("g0", [P, 2, T])
            k8x = early("k8x", [P, NC, 8, N])
            s8 = early("s8", [P, NC, 8, N])
            pT8 = early("pT8", [P, NC, 4, P])
            v8 = early("v8", [P, B, 4, 18])
            q_bd = early("q_bd", [P, NC, P])
            sel_f = early("sel_f", [2 * NE, HC * P])
            tri_f = early("tri_f", [P, 2, P])
            fw2_s = early("fw2_s", [P, HC, D])
            f13_s = early("f13_s", [P, 2, HC * P])
            m1_s = early("m1_s", [P, NE, 2 * P])
            rope = early("rope", [P, 2, NC, 2, N])
            aqk = early("aqk", [P, 2, HALF])
            sa = early("sa", [P, NC, P])
            paT = early("paT", [P, NC, P])
            h0T = early("h0T", [D + 1, T])
            fT = early("fT", [D + 1, T])
            o8T = early("o8T", [D + 1, T])
            o4T = early("o4T", [D, T])
            r3T = early("r3T", [D, T])

            k4x, s4, pT4 = k8x[:, :, 0:4, :], s8[:, :, 0:4, :], pT8[:, :, 0:2, :]

        x1T = sb("x1T", [D + 1, T])
        g5 = sb("g5", [D + 1, T])
        x7T = sb("x7T", [D + 1, T])
        v1 = sb("v1", [P, NC, 2, 72])
        x5T = sb("x5T", [D, T])
        eq = sb("eq", [D, T])
        rq = sb("rq", [D, T])
        phq = sb("phq", [D, T])
        ek = sb("ek", [P, NC, D])
        rk = sb("rk", [P, NC, D])
        phk = sb("phk", [P, NC, D])
        t5 = sb("t5", [P, NC, D])
        y5 = sb("y5", [P, NC, D])
        yn5 = sb("yn5", [P, NC, D])
        x1 = sb("x1", [P, NC, D])
        y6 = sb("y6", [P, NC, D])
        yn6 = sb("yn6", [P, NC, D])
        h4b = sb("h4b", [P, NC, D])
        kv = sb("kv", [D, B, 72])
        x7 = sb("x7", [P, NC, D])
        x7s = sb("x7s", [P, NC, 2, D], F32R)
        posn = sb("posn", [P, NC, 8])
        codt = sb("codt", [P, NC, 8])
        keep = sb("keep", [P, NC, 8])

        with ExitStack() as first_experts:
            def moe(name, shape, dt=F32):
                return first_experts.enter_context(nc.sbuf_tensor(name, shape, dt))

            asil = moe("asil", [P, 2, T])
            hgb = moe("hgb", [P, RING, T])
            hgs = moe("hgs", [P, RING, 2, T], F32R)
            moeT = moe("moeT", [P, T])

        disp = sb("disp", [P, NC, NE, CAP], F32R)
        bufT = sb("bufT", [P, NE, CAP], F32R)
        codb = sb("codb", [CAP, T])
        combT = sb("combT", [CAP, NE, T], F32R)
        hid = sb("hid", [P, NE, 2, CAP])
        ybs = sb("ybs", [CAP, NE, 2, D], F32R)
        ysum = sb("ysum", [P, NC, D])
        y7 = sb("y7", [P, NC, D])
        finite = sb("finite", [P, NC, D], U32)
        above = sb("above", [P, NC, D])
        below = sb("below", [P, NC, D])
        ynum = sb("ynum", [P, NC, D])
        h6 = sb("h6", [P, NC, D])

        in_conv, in_pat, in_small, in_w, in_big = sem("in_conv"), [sem("in_pat%d" % n) for n in range(len(PAT_PARTS))], \
            sem("in_small"), sem("in_w"), sem("in_big")
        out_stored = sem("out_stored")
        dve_step, act_step, pool_step = sem("dve_step"), sem("act_step"), sem("pool_step")
        S = {}
        for name in """hgl_dve masks split_down q8_copy pT8_act flT hid_dve combT_pool idle late_setup hgh
            hgl setup mconst conv_ps conv_f conv_t h0 h0_ps h0T ff1a_ps g0 ff2a_ps fT k8_ps q8_ps v8_ps k8 k8x
            v8 s8_ps s8 p8 pT8_ps pT8 o8_ps o8 o8T_ps o8T proj_ps h1 h1T_ps h1T ff1b_ps g1 ff2b_ps n2 n2T_ps n2T
            aqk_ps av_ps aqk av sa_ps sa pa paT_ps paT oa_ps h3 r3 r3T_ps r3T q4_ps k4_ps v4_ps q4bd k4x v4
            s4_ps s4 p4 pT4_ps pT4 o4_ps o4 o4T_ps o4T wo_ps fl flT_ps fs rt_ps lse lexp gpart gT_ps gT split
            a_ps b_ps gc_ps asil sb hgb moe_ps moeT moeTb_ps x5 x5T_ps x5T lq_ps lkv_ps eq ek phq phk kv_ps kv
            t5_ps x1 x1T_ps x1T l1h_ps g5 l1y_ps x7 x7T_ps x7T g_ps lse1 lex1 oh1b cum_ps disp bufT_ps bufT code
            cod_ps codb combT hid_ps hid y_ps ybs comb_ps h6 variance rstd""".split():
            S[name] = sem(name)

        block = ctx.enter_context(nc.Block())

        def norm_count(name, h):
            return 2 * NORMS.index(name) + h + 1

        def half(h):
            return slice(h * HALF, (h + 1) * HALF)

        def chunks(h):
            return slice(2 * h, 2 * h + 2)

        def tok(c):
            return slice(c * P, (c + 1) * P)

        def bank(h, i):
            return ps[:, 4 * h + i, :]

        def by_pool(i):
            return sum(n not in LOW_DVE for n in range(i + 1))

        @block.sync
        def _(sp):
            sp.dma_start(wconv_s[:], wconv).then_inc(in_conv, 16)
            sp.dma_start(cols_s[:], cols).then_inc(in_conv, 16)
            for n, at in enumerate(PAT_PARTS):
                sp.dma_start(pat_s[:, at], pat[:, at]).then_inc(in_pat[n], 16)
            sp.dma_start(con_s[:], con).then_inc(in_small, 16)
            sp.dma_start(rows_s[:], rows).then_inc(in_small, 16)
            sp.dma_start(w65_s[:], w65).then_inc(in_w, 16)
            sp.dma_start(ff2_s[:], ff2).then_inc(in_w, 16)
            sp.dma_start(w64_s[:], w64).then_inc(in_w, 16)
            sp.dma_start(f13_s[:], f13).then_inc(in_big, 16)
            sp.dma_start(m1_s[:], m1).then_inc(in_big, 16)
            sp.dma_start(fw2_s[:], fw2).then_inc(in_big, 16)
            sp.dma_start(sel_f[:], sel).then_inc(in_big, 16)
            sp.dma_start(m2_s[:], m2).then_inc(in_big, 16)
            sp.dma_start(mb2_s[:], mb2).then_inc(in_big, 16)
            sp.dma_start(tri_f[:], tri).then_inc(in_big, 16)
            for h in range(2):
                sp.wait_ge(S["h6"], h + 1)
                sp.dma_start(out.rearrange("(c p) d -> p c d", p=P)[:, chunks(h)], h6[:, chunks(h)]).then_inc(
                    out_stored, 16)
            sp.wait_ge(out_stored, 32)

        @block.gpsimd
        def _(pool):
            pool.memset(mhalf[:], -0.5).then_inc(S["mconst"], 1)
            pool.memset(q_bd[:], 0.0)
            pool.memset(q4_bd[:], 0.0).then_inc(S["setup"], 1)

            def rsqrt(name, n):
                for h in range(2):
                    pool.wait_ge(S["variance"], norm_count(name, h))
                    ve, rs = ln[name][2], ln[name][3]
                    pool.tensor_tensor(rs[:, chunks(h), 0:n], ve[:, chunks(h), 0:n],
                                       mhalf[:, 0:2 * n].rearrange("p (c n) -> p c n", n=n),
                                       ALU.pow).then_inc(S["rstd"], 1)

            pool.wait_ge(S["mconst"], 1)
            rsqrt("emb", 1)
            pool.wait_ge(in_big, 16 * 7)
            pool.tensor_copy(sel_s[:], sel_f[:])
            pool.tensor_copy(tri_s[:], tri_f[:]).then_inc(S["split"], 1)
            pool.wait_ge(S["split"], 2)
            for j in range(2):
                pool.tensor_tensor(f13l[:, j], f13_s[:, j], f13h[:, j], ALU.subtract)
            pool.wait_ge(S["split_down"], 1)
            pool.tensor_tensor(fw2s[:, :, 1], fw2_s[:], fw2s[:, :, 0], ALU.subtract)
            pool.tensor_tensor(m1l[:], m1_s[:], m1h[:], ALU.subtract).then_inc(S["split"], 1)
            rsqrt("pre_attn", 1)
            rsqrt("pre_ffn", 2)
            rsqrt("rms", 1)
            pool.memset(v1[:], 0.0).then_inc(S["late_setup"], 1)
            for n, tile in enumerate((x1T, g5, x7T)):
                pool.wait_ge(S["late_setup"], n + 1)
                pool.memset(tile[D:D + 1, :], 1.0).then_inc(S["late_setup"], 1)
            pool.wait_ge(S["late_setup"], 4)
            for i in range(HC):
                if i in LOW_DVE:
                    continue
                pool.wait_ge(S["hgh"], i + 1)
                if i >= RING:
                    pool.wait_ge(S["moe_ps"], i - RING + 1)
                pool.tensor_tensor(hgs[:, i % RING, 1], hgb[:, i % RING], hgs[:, i % RING, 0],
                                   ALU.subtract).then_inc(S["hgl"], 1)
            rsqrt("pre_l1", 1)
            rsqrt("l1a", 1)
            rsqrt("l1b", 1)
            rsqrt("pre_moe", 1)
            pool.wait_ge(S["codb"], 1)
            for e in range(NE):
                if e not in COMB_DVE:
                    pool.tensor_scalar(combT[:, e], codb[:], con_("slotid", CAP), float(128 * e), ALU.subtract,
                                       ALU.is_equal).then_inc(S["combT_pool"], 1)

        @block.vector
        def _(dve):
            steps = [0]

            def link(ins):
                steps[0] += 1
                ins.then_inc(dve_step, 1)
                dve.wait_ge(dve_step, steps[0])

            def step(ins):
                steps[0] += 1
                ins.then_inc(dve_step, 1)
                return steps[0]

            def bn_stats(name, src, h):
                for c in range(2 * h, 2 * h + 2):
                    last = dve.bn_stats(ln[name][0][:, c, :], src[:, c - 2 * h, :])
                return step(last)

            def bn_aggr(name, h, done):
                dve.wait_ge(dve_step, done)
                for c in range(2 * h, 2 * h + 2):
                    last = dve.bn_aggr(ln[name][1][:, c, :], ln[name][0][:, c, :])
                return step(last)

            def variance(name, h, done):
                dve.wait_ge(dve_step, done)
                dve.tensor_scalar(ln[name][2][:, chunks(h), 0:1], ln[name][1][:, chunks(h), 1:2], 1e-5, None,
                                  ALU.add).then_inc(S["variance"], 1)

            def stats(name, src, h):
                variance(name, h, bn_aggr(name, h, bn_stats(name, src, h)))

            def stats_both(name, x, ready):
                for h in range(2):
                    dve.wait_ge(dve_step, ready[h])
                    ready[h] = bn_stats(name, x[:, chunks(h)], h)
                for h in range(2):
                    ready[h] = bn_aggr(name, h, ready[h])
                for h in range(2):
                    variance(name, h, ready[h])

            def mean(name, c):
                return ln[name][1][:, c, 0:1]

            def rstd(name, c, i=0):
                return ln[name][3][:, c, i:i + 1]

            dve.memset(spare[:], 0.0)
            dve.memset(idle[:], 0.0).then_inc(S["idle"], 1)
            for tile in (h0T, fT, o8T):
                dve.memset(tile[D:D + 1, :], 1.0)
            dve.memset(v8[:, :, :, 16:18], 0.0)
            link(dve.memset(v4[:, :, :, 32:34], 0.0))
            for i in range(2):
                dve.memset(v8[i * N:(i + 1) * N, :, :, 16 + i:17 + i], 1.0)
                last = dve.memset(v4[i * N:(i + 1) * N, :, :, 32 + i:33 + i], 1.0)
            last.then_inc(S["setup"], 1)
            dve.wait_ge(in_small, 32)
            link(dve.tensor_tensor(lnb_pe[:], row("ln_b"), row("pe"), ALU.add))
            dve.tensor_copy(ident_b[:], ident)
            dve.tensor_copy(ident_r[:], ident)
            dve.tensor_copy(causal_b[:], con_("causal"))
            dve.tensor_copy(pair_b[:], con_("pair")).then_inc(S["masks"], 1)

            for h in range(2):
                dve.wait_ge(S["conv_t"], h + 1)
                stats("emb", bank(h, 1)[:, 0:P].rearrange("p (c d) -> p c d", c=2), h)
            for h in range(2):
                dve.wait_ge(S["rstd"], norm_count("emb", h))
                for c in range(2 * h, 2 * h + 2):
                    src = bank(h, 1)[:, (c % 2) * D:(c % 2 + 1) * D]
                    last = dve.scalar_tensor_tensor(yn[:, c, :], src, mean("emb", c), row("ln_w"), ALU.subtract,
                                                    ALU.mult)
                link(last)
                for c in range(2 * h, 2 * h + 2):
                    last = dve.scalar_tensor_tensor(h0[:, c, :], yn[:, c, :], rstd("emb", c), lnb_pe[:], ALU.mult,
                                                    ALU.add)
                last.then_inc(S["h0"], 1)

            dve.wait_ge(S["setup"], 2)
            for h in range(2):
                dve.wait_ge(S["k8_ps"], h + 1)
                dve.tensor_tensor(k8x[:, chunks(h)],
                                  bank(h, 3)[:, 0:2 * N].rearrange("p (c t) -> p c t", c=2).unsqueeze(2)
                                  .to_broadcast([P, 2, 8, N]),
                                  con_("mask8").unsqueeze(1).unsqueeze(3).to_broadcast([P, 2, 8, N]),
                                  ALU.mult).then_inc(S["k8x"], 1)
                dve.wait_ge(S["v8_ps"], h + 1)
                dve.tensor_tensor(v8[:, 4 * h:4 * h + 4, :, 0:16],
                                  bank(h, 2)[:, 0:4 * D].rearrange("p (b g d) -> p b g d", b=4, g=4),
                                  con_("vmask8").rearrange("p (g d) -> p g d", g=4).unsqueeze(1)
                                  .to_broadcast([P, 4, 4, 16]), ALU.mult).then_inc(S["v8"], 1)
            found = {}
            for c in range(NC + 1):
                if c < NC:
                    dve.wait_ge(S["s8_ps"], c + 1)
                    found[c] = step(dve.tensor_reduce(
                        mx8[:, c, :], bank(c // 2, (3, 0)[c % 2]).rearrange("p (g k) -> p g k", g=8), AX_X, ALU.max))
                if c > 0:
                    b = c - 1
                    dve.wait_ge(dve_step, found[b])
                    dve.tensor_tensor(s8[:, b], bank(b // 2, (3, 0)[b % 2]).rearrange("p (g k) -> p g k", g=8),
                                      mx8[:, b, :].unsqueeze(2).to_broadcast([P, 8, N]),
                                      ALU.subtract).then_inc(S["s8"], 1)
            for c in range(0, NC, 2):
                dve.wait_ge(S["pT8_ps"], c + 1)
                dve.tensor_copy(pT8[:, c], bank(c // 2, 1).rearrange("p (g t) -> p g t", g=4)).then_inc(
                    S["pT8"], 1)
            for c in range(NC):
                dve.wait_ge(S["o8_ps"], 2 * (c // 2) + 2)
                src = bank(c // 2, 3)[:, (c % 2) * 72:(c % 2 + 1) * 72].rearrange("p (g d) -> p g d", g=4)
                link(dve.reciprocal(ri8[:, c], src[:, :, 16:18]))
                dve.tensor_tensor(o8[:, c, :].rearrange("p (g i d) -> p g i d", g=4, i=2),
                                  src[:, :, 0:16].rearrange("p g (i d) -> p g i d", i=2),
                                  ri8[:, c].unsqueeze(3).to_broadcast([P, 4, 2, 8]), ALU.mult).then_inc(S["o8"], 1)
            for h in range(2):
                dve.wait_ge(S["proj_ps"], h + 1)
                dve.tensor_tensor(h1[:, chunks(h)], bank(h, 1)[:, 0:P].rearrange("p (c d) -> p c d", c=2),
                                  h0[:, chunks(h)], ALU.add).then_inc(S["h1"], 1)
            for h in range(2):
                dve.wait_ge(S["h1"], h + 1)
                link(dve.tensor_tensor(h1b[:, chunks(h)], h1[:, chunks(h)],
                                       row("ff_b2").unsqueeze(1).to_broadcast([P, 2, D]), ALU.add))
            for h in range(2):
                dve.wait_ge(S["ff2b_ps"], h + 1)
                link(dve.tensor_tensor(h2[:, chunks(h)], bank(h, 0)[:, 0:P].rearrange("p (c d) -> p c d", c=2),
                                       h1b[:, chunks(h)], ALU.add))
                stats("pre_attn", h2[:, chunks(h)], h)
            for h in range(2):
                dve.wait_ge(S["rstd"], norm_count("pre_attn", h))
                for c in range(2 * h, 2 * h + 2):
                    last = dve.tensor_scalar(n2[:, c], h2[:, c], mean("pre_attn", c), rstd("pre_attn", c),
                                             ALU.subtract, ALU.mult)
                last.then_inc(S["n2"], 1)

            for h in range(2):
                dve.wait_ge(S["av_ps"], h + 1)
                dve.tensor_copy(av[:, chunks(h)], bank(h, 3)[:, 0:P].rearrange("p (c d) -> p c d", c=2)).then_inc(
                    S["av"], 1)
            for h in range(2):
                dve.wait_ge(S["sa_ps"], h + 1)
                dve.tensor_reduce(nmx[:, chunks(h)], ps[:, 4 * h:4 * h + 2, 0:P], AX_X,
                                  ALU.max, negate=True).then_inc(S["sa"], 1)
            for h in range(2):
                dve.wait_ge(S["paT_ps"], h + 1)
                dve.tensor_copy(paT[:, chunks(h)], bank(h, 1)[:, 0:2 * P].rearrange("p (c d) -> p c d", c=2)).then_inc(
                    S["paT"], 1)
            for h in range(2):
                dve.wait_ge(S["pa"], 2 * h + 2)
                link(dve.reciprocal(ria[:, chunks(h)], suma[:, chunks(h)]))
                dve.wait_ge(S["oa_ps"], h + 1)
                for c in range(2 * h, 2 * h + 2):
                    last = dve.scalar_tensor_tensor(h3[:, c], bank(h, 2)[:, (c % 2) * D:(c % 2 + 1) * D],
                                                    ria[:, c:c + 1], h2[:, c], ALU.mult, ALU.add)
                last.then_inc(S["h3"], 1)
            for h in range(2):
                dve.wait_ge(S["h3"], h + 1)
                st, mv_, ve, _ = ln["pre_ffn"]
                for c in range(2 * h, 2 * h + 2):
                    last = dve.bn_stats(st[:, c, :], h3[:, c, :])
                link(last)
                for c in range(2 * h, 2 * h + 2):
                    last = dve.bn_aggr(mv_[:, c, :], st[:, c, :])
                link(last)
                dve.tensor_scalar(ve[:, chunks(h), 0:1], mv_[:, chunks(h), 1:2], 1e-5, None, ALU.add)
                dve.tensor_scalar(ve[:, chunks(h), 1:2], mv_[:, chunks(h), 1:2], 1.0 + 1e-6, 1e-11, ALU.mult,
                                  ALU.add).then_inc(S["variance"], 1)
            for h in range(2):
                dve.wait_ge(S["rstd"], norm_count("pre_ffn", h))
                for c in range(2 * h, 2 * h + 2):
                    last = dve.tensor_scalar(r3[:, c], h3[:, c], mean("pre_ffn", c), rstd("pre_ffn", c, 1),
                                             ALU.subtract, ALU.mult)
                last.then_inc(S["r3"], 1)
            for h in range(2):
                for c in range(2 * h, 2 * h + 2):
                    last = dve.tensor_scalar(x3[:, c], h3[:, c], mean("pre_ffn", c), rstd("pre_ffn", c),
                                             ALU.subtract, ALU.mult)
                link(last)
            for h in range(2):
                for w, ready in ((0, "q4_ps"), (1, "k4_ps")):
                    dve.wait_ge(S[ready], h + 1)
                    link(dve.tensor_tensor(
                        rope[:, w, chunks(h)], bank(h, w)[:, 0:4 * N].rearrange("p (r c t) -> p c r t", r=2, c=2),
                        con_s[:, CON["cos"][0]:CON["sin"][1]].rearrange("p (r t) -> p r t", r=2).unsqueeze(1)
                        .to_broadcast([P, 2, 2, N]), ALU.mult))
                    if w == 0:
                        for i in range(2):
                            rr = slice(i * D, (i + 1) * D)
                            last = dve.tensor_tensor(q4_bd[rr, chunks(h), i * N:(i + 1) * N],
                                                     rope[rr, 0, chunks(h), 0, :], rope[rr, 0, chunks(h), 1, :], ALU.add)
                        last.then_inc(S["q4bd"], 1)
                    else:
                        link(dve.tensor_tensor(k4[:, chunks(h)], rope[:, 1, chunks(h), 0, :],
                                               rope[:, 1, chunks(h), 1, :], ALU.add))
                        dve.tensor_tensor(k4x[:, chunks(h)],
                                          k4[:, chunks(h), :].unsqueeze(2).to_broadcast([P, 2, 4, N]),
                                          con_("mask4").unsqueeze(1).unsqueeze(3).to_broadcast([P, 2, 4, N]),
                                          ALU.mult).then_inc(S["k4x"], 1)
                dve.wait_ge(S["v4_ps"], h + 1)
                dve.tensor_tensor(v4[:, 4 * h:4 * h + 4, :, 0:32],
                                  bank(h, 2)[:, 0:4 * D].rearrange("p (b g d) -> p b g d", b=4, g=2),
                                  con_("vmask4").rearrange("p (g d) -> p g d", g=2).unsqueeze(1)
                                  .to_broadcast([P, 4, 2, 32]), ALU.mult).then_inc(S["v4"], 1)
            scores = [bank(c // 2, 3)[:, (c % 2) * 256:(c % 2 + 1) * 256].rearrange("p (g k) -> p g k", g=4)
                      for c in range(NC)]
            for h in range(2):
                dve.wait_ge(S["s4_ps"], 2 * h + 2)
                for c in range(2 * h, 2 * h + 2):
                    found[c] = step(dve.tensor_reduce(mx4[:, c, :], scores[c], AX_X, ALU.max))
                for c in range(2 * h, 2 * h + 2):
                    dve.wait_ge(dve_step, found[c])
                    dve.tensor_tensor(s4[:, c], scores[c], mx4[:, c, :].unsqueeze(2).to_broadcast([P, 4, N]),
                                      ALU.subtract).then_inc(S["s4"], 1)
            for c in range(NC):
                dve.wait_ge(S["o4_ps"], 2 * (c // 2) + 2)
                src = bank(c // 2, 1)[:, (c % 2) * 68:(c % 2 + 1) * 68].rearrange("p (g d) -> p g d", g=2)
                link(dve.reciprocal(ri4[:, c], src[:, :, 32:34]))
                dve.tensor_tensor(o4[:, c, :].rearrange("p (g i d) -> p g i d", g=2, i=2),
                                  src[:, :, 0:32].rearrange("p g (i d) -> p g i d", i=2),
                                  ri4[:, c].unsqueeze(3).to_broadcast([P, 2, 2, 16]), ALU.mult).then_inc(S["o4"], 1)
            for h in range(2):
                dve.wait_ge(S["wo_ps"], h + 1)
                link(dve.tensor_tensor(x4[:, chunks(h)], bank(h, 3)[:, 0:P].rearrange("p (c d) -> p c d", c=2),
                                       x3[:, chunks(h)], ALU.add))
                st, mv_, ve, _ = ln["rms"]
                for c in range(2 * h, 2 * h + 2):
                    last = dve.bn_stats(st[:, c, :], x4[:, c, :])
                link(last)
                for c in range(2 * h, 2 * h + 2):
                    last = dve.bn_aggr(mv_[:, c, :], st[:, c, :])
                link(last)
                link(dve.tensor_tensor(ve[:, chunks(h), 1:2], mv_[:, chunks(h), 0:1], mv_[:, chunks(h), 0:1],
                                       ALU.mult))
                dve.scalar_tensor_tensor(ve[:, chunks(h), 0], mv_[:, chunks(h), 1], 1e-6,
                                         ve[:, chunks(h), 1], ALU.add, ALU.add).then_inc(S["variance"], 1)
            for h in range(2):
                dve.wait_ge(S["rstd"], norm_count("rms", h))
                for c in range(2 * h, 2 * h + 2):
                    last = dve.tensor_scalar(fl[:, c], x4[:, c].unsqueeze(1).to_broadcast([P, 2, D]),
                                             rstd("rms", c), None, ALU.mult)
                last.then_inc(S["fl"], 1)
            for h in range(2):
                dve.wait_ge(S["flT_ps"], h + 1)
                dve.tensor_scalar(flT[:, half(h)], bank(h, 0)[:, 0:HALF], col("ln2_w"), None, ALU.mult).then_inc(
                    S["flT"], 1)
            for h in range(2):
                dve.wait_ge(S["flT"], h + 1)
                link(dve.tensor_copy(fs[:, half(h)], flT[:, half(h)]))
                dve.tensor_tensor(fs[D:P, half(h)], flT[D:P, half(h)], fs[D:P, half(h)],
                                  ALU.subtract).then_inc(S["fs"], 1)
            dve.wait_ge(S["rt_ps"], 1)
            src = ps[:, 1, 0:NC * NE].rearrange("p (c e) -> p c e", c=NC)
            for c in range(NC):
                last = dve.max(top8[:, c, :], src[:, c, :])
            link(last)
            dve.tensor_tensor(lse[:], src, top8[:, :, 0:1].to_broadcast([P, NC, 8]), ALU.subtract).then_inc(S["lse"], 1)
            for c in range(NC):
                last = dve.max_index(topi[:, c, :], top8[:, c, :], src[:, c, :])
            link(last)
            iota = con_("iota8").unsqueeze(1).to_broadcast([P, NC, 8])
            dve.tensor_tensor(oh[:], iota, topi[:, :, 0:1].to_broadcast([P, NC, 8]), ALU.is_equal)
            link(dve.tensor_tensor(oh2[:], iota, topi[:, :, 1:2].to_broadcast([P, NC, 8]), ALU.is_equal))
            link(dve.tensor_tensor(oh[:], oh[:], oh2[:], ALU.add))
            dve.wait_ge(S["lexp"], 1)
            dve.tensor_reduce(lsum[:], lexp[:], AX_X, ALU.add)
            link(dve.tensor_tensor(wsel[:], lexp[:], oh[:], ALU.mult))
            link(dve.tensor_reduce(wtot[:], wsel[:], AX_X, ALU.add))
            link(dve.scalar_tensor_tensor(wden[:], lsum[:], 1e-9, wtot[:], ALU.mult, ALU.add))
            link(dve.reciprocal(winv[:], wden[:]))
            link(dve.tensor_tensor(gat[:], wsel[:], winv[:].unsqueeze(2).to_broadcast([P, NC, 8]), ALU.mult))
            link(dve.tensor_copy(gpart[:, :, 0], gat[:]))
            dve.tensor_tensor(gpart[:, :, 1], gat[:], gpart[:, :, 0], ALU.subtract).then_inc(S["gpart"], 1)

            def product(i):
                dve.wait_ge(S["asil"], i + 1)
                dve.wait_ge(S["b_ps"], i + 1)
                if i >= RING:
                    dve.wait_ge(S["hgl"], by_pool(i - RING))
                dve.tensor_tensor(hgb[:, i % RING], asil[:, i % 2], ps[:, (3, 7)[i % 2], :],
                                  ALU.mult).then_inc(S["sb"], 1)

            def second_part(i):
                dve.wait_ge(S["hgh"], i + 1)
                if i >= RING:
                    dve.wait_ge(S["moe_ps"], i - RING + 1)
                dve.tensor_tensor(hgs[:, i % RING, 1], hgb[:, i % RING], hgs[:, i % RING, 0],
                                  ALU.subtract).then_inc(S["hgl_dve"], 1)

            for i in range(LEAD):
                product(i)
            for i in range(HC):
                dve.wait_ge(S["sb"], i + 1)
                dve.wait_ge(S["gc_ps"], i + 1)
                dve.tensor_tensor(hgb[:, i % RING], hgb[:, i % RING], ps[:, (1, 5)[i % 2], :],
                                  ALU.mult).then_inc(S["hgb"], 1)
                if i + LEAD < HC:
                    product(i + LEAD)
                if i - 1 in LOW_DVE:
                    second_part(i - 1)
            if HC - 1 in LOW_DVE:
                second_part(HC - 1)
            for h in range(2):
                link(dve.tensor_tensor(hx[:, chunks(h)], h3[:, chunks(h)], x4[:, chunks(h)], ALU.add))
            ready = [0, 0]
            for h in range(2):
                dve.wait_ge(S["moeTb_ps"], h + 1)
                ready[h] = step(dve.tensor_tensor(h4[:, chunks(h)],
                                                  bank(h, 1)[:, 0:P].rearrange("p (c d) -> p c d", c=2),
                                                  hx[:, chunks(h)], ALU.add))
            stats_both("pre_l1", h4, ready)
            for h in range(2):
                dve.wait_ge(S["rstd"], norm_count("pre_l1", h))
                for c in range(2 * h, 2 * h + 2):
                    last = dve.tensor_scalar(x5[:, c], h4[:, c], mean("pre_l1", c), rstd("pre_l1", c),
                                             ALU.subtract, ALU.mult)
                last.then_inc(S["x5"], 1)
            dve.wait_ge(S["late_setup"], 1)
            for i in range(2):
                last = dve.memset(v1[i * N:(i + 1) * N, :, i, D:72], 1.0)
            link(last)
            for h in range(2):
                dve.wait_ge(S["lkv_ps"], h + 1)
                src = bank(h, 1)[:, 0:256].rearrange("p (c w d) -> p c w d", c=2, w=2)
                dve.wait_ge(S["ek"], h + 1)
                for i in range(2):
                    rr = slice(i * N, (i + 1) * N)
                    dve.tensor_copy(v1[rr, chunks(h), i, 0:D], src[rr, :, 1, :])
                dve.scalar_tensor_tensor(phk[:, chunks(h)], ek[:, chunks(h)], 1.0, rk[:, chunks(h)], ALU.min,
                                         ALU.add).then_inc(S["phk"], 1)
                dve.wait_ge(S["eq"], h + 1)
                dve.scalar_tensor_tensor(phq[:, half(h)], eq[:, half(h)], 1.0, rq[:, half(h)], ALU.min,
                                         ALU.add).then_inc(S["phq"], 1)
            for h in range(2):
                dve.wait_ge(S["kv_ps"], h + 1)
                dve.tensor_tensor(kv[:, 4 * h:4 * h + 4],
                                  bank(h, 2)[0:D, 0:288].rearrange("p (b d) -> p b d", b=4),
                                  con_("bm", D).unsqueeze(1).to_broadcast([D, 4, 72]), ALU.mult).then_inc(S["kv"], 1)
            sums = [bank(h, 3)[:, 0:144].rearrange("p (c d) -> p c d", c=2) for h in range(2)]
            for h in range(2):
                dve.wait_ge(S["t5_ps"], h + 1)
                ready[h] = step(dve.tensor_scalar(zden[:, chunks(h)], sums[h][:, :, D:72], 1e-6, None, ALU.add))
            for h in range(2):
                dve.wait_ge(dve_step, ready[h])
                ready[h] = step(dve.reciprocal(z[:, chunks(h)], zden[:, chunks(h)]))
            for h in range(2):
                dve.wait_ge(dve_step, ready[h])
                ready[h] = step(dve.tensor_tensor(t5[:, chunks(h)].rearrange("p c (g d) -> p c g d", g=8),
                                                  sums[h][:, :, 0:D].rearrange("p c (g d) -> p c g d", g=8),
                                                  z[:, chunks(h)].unsqueeze(3).to_broadcast([P, 2, 8, 8]), ALU.mult))
            for h in range(2):
                dve.wait_ge(dve_step, ready[h])
                ready[h] = step(dve.tensor_tensor(y5[:, chunks(h)], t5[:, chunks(h)], x5[:, chunks(h)], ALU.add))
            stats_both("l1a", y5, ready)
            for h in range(2):
                dve.wait_ge(S["rstd"], norm_count("l1a", h))
                for c in range(2 * h, 2 * h + 2):
                    last = dve.scalar_tensor_tensor(yn5[:, c], y5[:, c], mean("l1a", c), row("ln1_g"),
                                                    ALU.subtract, ALU.mult)
                link(last)
                for c in range(2 * h, 2 * h + 2):
                    last = dve.scalar_tensor_tensor(x1[:, c], yn5[:, c], rstd("l1a", c), row("ln1_b"), ALU.mult,
                                                    ALU.add)
                last.then_inc(S["x1"], 1)
            link(dve.tensor_tensor(h4b[:], h4[:], row("ln2_b").unsqueeze(1).to_broadcast([P, NC, D]), ALU.add))
            for h in range(2):
                dve.wait_ge(S["l1y_ps"], h + 1)
                dve.wait_ge(S["x1"], h + 1)
                ready[h] = step(dve.tensor_tensor(y6[:, chunks(h)],
                                                  bank(h, 2)[:, 0:P].rearrange("p (c d) -> p c d", c=2),
                                                  x1[:, chunks(h)], ALU.add))
            stats_both("l1b", y6, ready)

            def centred(h):
                dve.wait_ge(S["rstd"], norm_count("l1b", h))
                for c in range(2 * h, 2 * h + 2):
                    last = dve.scalar_tensor_tensor(yn6[:, c], y6[:, c], mean("l1b", c), row("ln2_g"),
                                                    ALU.subtract, ALU.mult)
                return step(last)

            def summed(h, done):
                dve.wait_ge(dve_step, done)
                for c in range(2 * h, 2 * h + 2):
                    last = dve.scalar_tensor_tensor(h5[:, c], yn6[:, c], rstd("l1b", c), h4b[:, c], ALU.mult,
                                                    ALU.add)
                return step(last)

            ready[0] = summed(0, centred(0))
            dve.wait_ge(dve_step, ready[0])
            ready[0] = bn_stats("pre_moe", h5[:, chunks(0)], 0)
            ready[1] = centred(1)
            ready[0] = bn_aggr("pre_moe", 0, ready[0])
            ready[1] = summed(1, ready[1])
            variance("pre_moe", 0, ready[0])
            dve.wait_ge(dve_step, ready[1])
            stats("pre_moe", h5[:, chunks(1)], 1)
            for h in range(2):
                cs = chunks(h)
                dve.wait_ge(S["rstd"], norm_count("pre_moe", h))
                for c in range(2 * h, 2 * h + 2):
                    last = dve.tensor_scalar(x7[:, c], h5[:, c], mean("pre_moe", c), rstd("pre_moe", c),
                                             ALU.subtract, ALU.mult)
                last.then_inc(S["x7"], 1)
            dve.wait_ge(S["x7"], 2)
            link(dve.tensor_copy(x7s[:, :, 0], x7[:]))
            link(dve.tensor_tensor(x7s[:, :, 1], x7[:], x7s[:, :, 0], ALU.subtract))
            for h in range(2):
                cs = chunks(h)
                dve.wait_ge(S["g_ps"], h + 1)
                src = bank(h, 0)[:, 0:16].rearrange("p (c e) -> p c e", c=2)
                for c in range(2):
                    last = dve.max(top1[:, 2 * h + c, :], src[:, c, :])
                link(last)
                dve.tensor_tensor(lse1[:, cs], src, top1[:, cs, 0:1].to_broadcast([P, 2, 8]),
                                  ALU.subtract).then_inc(S["lse1"], 1)
                for c in range(2):
                    last = dve.max_index(toi1[:, 2 * h + c, :], top1[:, 2 * h + c, :], src[:, c, :])
                link(last)
                iota = con_("iota8").unsqueeze(1).to_broadcast([P, 2, 8])
                dve.tensor_tensor(oh1b[:, cs], iota, toi1[:, cs, 0:1].to_broadcast([P, 2, 8]),
                                  ALU.is_equal).then_inc(S["oh1b"], 1)
                link(dve.tensor_tensor(oh1[:, cs], iota, toi1[:, cs, 0:1].to_broadcast([P, 2, 8]), ALU.is_equal))
            for h in range(2):
                cs = chunks(h)
                if h == 1:
                    dve.wait_ge(S["lex1"], 2)
                    link(dve.tensor_reduce(lsu1[:], lex1[:], AX_X, ALU.add))
                    step(dve.reciprocal(prob[:], lsu1[:]))
                dve.wait_ge(S["cum_ps"], h + 1)
                link(dve.tensor_tensor(posn[:, cs], bank(h, 1)[:, 0:16].rearrange("p (c e) -> p c e", c=2),
                                       oh1[:, cs], ALU.mult))
                if h == 1:
                    dve.scalar_tensor_tensor(keep[:], posn[:], float(CAP), oh1[:], ALU.is_le, ALU.mult)
                    link(dve.tensor_tensor(codt[:], con_("expert").unsqueeze(1).to_broadcast([P, NC, 8]), posn[:],
                                           ALU.add))
                    link(dve.tensor_tensor(codt[:], codt[:], keep[:], ALU.mult))
                    link(dve.tensor_reduce(code[:], codt[:], AX_X, ALU.add))
                    dve.tensor_copy(code_r[:], code[:]).then_inc(S["code"], 1)
                for c in range(2 * h, 2 * h + 2):
                    dve.tensor_tensor(disp[:, c], con_("slots").unsqueeze(1).to_broadcast([P, NE, CAP]),
                                      posn[:, c].unsqueeze(2).to_broadcast([P, NE, CAP]),
                                      ALU.is_equal).then_inc(S["disp"], 1)
            dve.wait_ge(S["cod_ps"], 1)
            dve.tensor_copy(codb[:], ps[0:CAP, 7, :]).then_inc(S["codb"], 1)
            dve.wait_ge(S["codb"], 1)

            def slot_columns(eng, e):
                return eng.tensor_scalar(combT[:, e], codb[:], con_("slotid", CAP), float(128 * e), ALU.subtract,
                                         ALU.is_equal)

            def hidden(e):
                dve.wait_ge(S["hid_ps"], e + 1)
                k = COLS["moe_b1"][0] + 2 * e + 1
                dve.tensor_scalar(hid[:, e, 1], ps[:, (2, 6)[e % 2], 0:CAP], cols_s[:, k:k + 1], 0.0, ALU.add,
                                  ALU.max).then_inc(S["hid_dve"], 1)

            for e in range(NE):
                if e % 2 == 0:
                    hidden(e)
                if e in COMB_DVE:
                    slot_columns(dve, e).then_inc(S["combT"], 1)
            for i in range(2):
                es = slice(4 * i, 4 * i + 4)
                dve.wait_ge(S["y_ps"], i + 1)
                src = ps[0:CAP, (5, 3)[i], 0:4 * D].rearrange("p (e d) -> p e d", e=4)
                link(dve.tensor_copy(ybs[:, es, 0], src))
                dve.tensor_tensor(ybs[:, es, 1], src, ybs[:, es, 0], ALU.subtract).then_inc(S["ybs"], 1)

            def combined(h):
                b = COMB_BANK[2 * h]
                dve.wait_ge(S["comb_ps"], h + 1)
                return step(dve.tensor_reduce(ysum[:, chunks(h)],
                                              ps[:, b:b + 2, 0:P].rearrange("p c (w d) -> p c d w", w=2), AX_X,
                                              ALU.add))

            def weighted(h, done):
                dve.wait_ge(dve_step, done)
                return step(dve.tensor_tensor(y7[:, chunks(h)], ysum[:, chunks(h)],
                                              prob[:, chunks(h)].unsqueeze(2).to_broadcast([P, 2, D]), ALU.mult))

            def compared(h, done):
                dve.wait_ge(dve_step, done)
                y = y7[:, chunks(h)]
                dve.tensor_scalar(finite[:, chunks(h)], y, 0.0, 0.0, ALU.mult, ALU.is_equal)
                dve.tensor_scalar(above[:, chunks(h)], y, FLOAT_MAX, INF_TO, ALU.is_gt, ALU.mult)
                return step(dve.tensor_scalar(below[:, chunks(h)], y, -FLOAT_MAX, -INF_TO, ALU.is_lt, ALU.mult))

            def infinities(h, done):
                dve.wait_ge(dve_step, done)
                return step(dve.tensor_tensor(ynum[:, chunks(h)], above[:, chunks(h)], below[:, chunks(h)], ALU.add))

            def finites(h, done):
                dve.wait_ge(dve_step, done)
                return step(dve.copy_predicated(ynum[:, chunks(h)], finite[:, chunks(h)], y7[:, chunks(h)]))

            def result(h, done):
                dve.wait_ge(dve_step, done)
                dve.tensor_tensor(h6[:, chunks(h)], ynum[:, chunks(h)], h5[:, chunks(h)], ALU.add).then_inc(
                    S["h6"], 1)

            ready[0] = weighted(0, combined(0))
            ready[0] = compared(0, ready[0])
            ready[1] = combined(1)
            ready[0] = infinities(0, ready[0])
            ready[1] = weighted(1, ready[1])
            ready[0] = finites(0, ready[0])
            ready[1] = compared(1, ready[1])
            result(0, ready[0])
            ready[1] = infinities(1, ready[1])
            ready[1] = finites(1, ready[1])
            result(1, ready[1])

        @block.scalar
        def _(act):
            def evac(dst, src, ready, n, done, bias=None):
                act.wait_ge(S[ready], n)
                if bias is None:
                    act.activation(dst, src, ACT.Copy).then_inc(S[done], 1)
                else:
                    act.activation(dst, src, ACT.Identity, bias=bias).then_inc(S[done], 1)

            def load_table(func):
                act.activation(spare[:, 1:2], spare[:, 0:1], func).then_inc(act_step, 1)
                loads[0] += 1
                act.wait_ge(act_step, loads[0])

            loads = [0]
            act.wait_ge(S["idle"], 1)
            load_table(ACT.Gelu_apprx_tanh)
            act.wait_ge(in_conv, 32)
            for h in range(2):
                evac(conv_f[:, h * P:(h + 1) * P], bank(h, 0)[:, 0:P], "conv_ps", h + 1, "conv_f", col("conv_b"))
            for h in range(2):
                evac(h0T[0:D, half(h)], bank(h, 2)[0:D, 0:HALF], "h0_ps", h + 1, "h0T")
            for h in range(2):
                act.wait_ge(S["ff1a_ps"], h + 1)
                act.activation(g0[:, :, half(h)], bank(h, 3).rearrange("p (j t) -> p j t", j=2),
                               ACT.Gelu_apprx_tanh).then_inc(S["g0"], 1)
            load_table(ACT.Exp)
            for h in range(2):
                evac(fT[0:D, half(h)], bank(h, 0)[0:D, 0:HALF], "ff2a_ps", h + 1, "fT", col("ff_b2", D))
            act.wait_ge(S["setup"], 2)
            for h in range(2):
                act.wait_ge(S["q8_ps"], h + 1)
                for i in range(2):
                    rr = slice(i * D, (i + 1) * D)
                    last = act.activation(q_bd[rr, chunks(h), i * N:(i + 1) * N],
                                          bank(h, 1)[rr, 0:2 * N].rearrange("p (c t) -> p c t", c=2), ACT.Copy)
                last.then_inc(S["q8_copy"], 1)
            act.wait_ge(in_big, 16 * 7)
            for j in range(2):
                last = act.activation(f13h[:, j], f13_s[:, j], ACT.Copy)
            last.then_inc(S["split"], 1)
            for c in range(NC):
                act.wait_ge(S["s8"], c + 1)
                act.activation(s8[:, c], s8[:, c], ACT.Exp).then_inc(S["p8"], 1)
            for c in range(1, NC, 2):
                evac(pT8[:, c], bank(c // 2, 2).rearrange("p (g t) -> p g t", g=4), "pT8_ps", c + 1, "pT8_act")
            act.activation(fw2s[:, :, 0], fw2_s[:], ACT.Copy)
            act.activation(m1h[:], m1_s[:], ACT.Copy).then_inc(S["split_down"], 1)
            load_table(ACT.Gelu_apprx_tanh)
            for h in range(2):
                evac(o8T[0:D, half(h)], bank(h, 0)[0:D, 0:HALF], "o8T_ps", h + 1, "o8T")
            for h in range(2):
                evac(h0T[0:D, half(h)], bank(h, 2)[0:D, 0:HALF], "h1T_ps", h + 1, "h1T")
            for h in range(2):
                act.wait_ge(S["ff1b_ps"], h + 1)
                act.activation(g0[:, :, half(h)], bank(h, 3).rearrange("p (j t) -> p j t", j=2),
                               ACT.Gelu_apprx_tanh).then_inc(S["g1"], 1)
            load_table(ACT.Exp)
            for h in range(2):
                evac(fT[0:D, half(h)], bank(h, 1)[0:D, 0:HALF], "n2T_ps", h + 1, "n2T")
            for h in range(2):
                act.wait_ge(S["aqk_ps"], h + 1)
                act.activation(aqk[:, 0, h * P:(h + 1) * P], bank(h, 2)[:, 0:P], ACT.Copy, scale=float(D) ** -0.5)
                act.activation(aqk[:, 1, h * P:(h + 1) * P], bank(h, 2)[:, P:2 * P], ACT.Copy).then_inc(S["aqk"], 1)
            for h in range(2):
                act.wait_ge(S["sa"], h + 1)
                for c in range(2 * h, 2 * h + 2):
                    act.activation(sa[:, c], bank(h, c % 2)[:, 0:P], ACT.Exp, bias=nmx[:, c:c + 1],
                                   accum_out=suma[:, c:c + 1]).then_inc(S["pa"], 1)
            for h in range(2):
                act.wait_ge(S["r3T_ps"], h + 1)
                act.activation(r3T[:, half(h)], bank(h, 3)[0:D, 0:HALF], ACT.Copy,
                               scale=col("ln1_w", D)).then_inc(S["r3T"], 1)
            for c in range(NC):
                act.wait_ge(S["s4"], c + 1)
                act.activation(s4[:, c], s4[:, c], ACT.Exp).then_inc(S["p4"], 1)
            for h in range(2):
                evac(pT4[:, chunks(h)], bank(h, 0).rearrange("p (c g t) -> p c g t", c=2, g=2), "pT4_ps", h + 1, "pT4")
            for h in range(2):
                evac(o4T[:, half(h)], bank(h, 2)[0:D, 0:HALF], "o4T_ps", h + 1, "o4T")
            act.wait_ge(S["lse"], 1)
            act.activation(lexp[:], lse[:], ACT.Exp).then_inc(S["lexp"], 1)
            load_table(ACT.Silu)

            def silu(i):
                act.wait_ge(S["a_ps"], i + 1)
                if i >= 2:
                    act.wait_ge(S["sb"], i - 1)
                act.activation(asil[:, i % 2], ps[:, (0, 4)[i % 2], :], ACT.Silu).then_inc(S["asil"], 1)

            def first_part(i):
                act.wait_ge(S["hgb"], i + 1)
                if i >= RING:
                    act.wait_ge(S["moe_ps"], i - RING + 1)
                act.activation(hgs[:, i % RING, 0], hgb[:, i % RING], ACT.Copy).then_inc(S["hgh"], 1)

            silu(0)
            silu(1)
            for h in range(2):
                evac(gT[:, half(h)], bank(h, 2)[0:2 * NE, 0:HALF], "gT_ps", h + 1, "gT")
            for i in range(2, LEAD):
                silu(i)
            for i in range(HC):
                if i + LEAD < HC:
                    silu(i + LEAD)
                first_part(i)
            load_table(ACT.Exp)
            act.wait_ge(S["moe_ps"], HC)
            for h in range(2):
                act.activation(moeT[:, half(h)], ps[:, 6, half(h)], ACT.Copy).then_inc(S["moeT"], 1)
            for h in range(2):
                evac(x5T[:, half(h)], bank(h, 3)[0:D, 0:HALF], "x5T_ps", h + 1, "x5T")
            for h in range(2):
                act.wait_ge(S["lkv_ps"], h + 1)
                src = bank(h, 1)[:, 0:256].rearrange("p (c w d) -> p c w d", c=2, w=2)[:, :, 0, :]
                act.activation(rk[:, chunks(h)], src, ACT.Relu)
                act.activation(ek[:, chunks(h)], src, ACT.Exp).then_inc(S["ek"], 1)
                act.wait_ge(S["lq_ps"], h + 1)
                act.activation(rq[:, half(h)], bank(h, 0)[0:D, 0:HALF], ACT.Relu)
                act.activation(eq[:, half(h)], bank(h, 0)[0:D, 0:HALF], ACT.Exp).then_inc(S["eq"], 1)
            load_table(ACT.Gelu)
            for h in range(2):
                evac(x1T[0:D, half(h)], bank(h, 0)[0:D, 0:HALF], "x1T_ps", h + 1, "x1T")
            for h in range(2):
                act.wait_ge(S["l1h_ps"], h + 1)
                act.activation(g5[0:D, half(h)], bank(h, 1)[0:D, 0:HALF], ACT.Gelu).then_inc(S["g5"], 1)
            load_table(ACT.Exp)
            for h in range(2):
                evac(x7T[0:D, half(h)], bank(h, 3)[0:D, 0:HALF], "x7T_ps", h + 1, "x7T")
            for h in range(2):
                act.wait_ge(S["lse1"], h + 1)
                act.activation(lex1[:, chunks(h)], lse1[:, chunks(h)], ACT.Exp).then_inc(S["lex1"], 1)
            for i in range(2):
                act.wait_ge(S["bufT_ps"], i + 1)
                act.activation(bufT[:, 4 * i:4 * i + 4], ps[:, (2, 6)[i], 0:4 * CAP].rearrange("p (e s) -> p e s", e=4),
                               ACT.Copy).then_inc(S["bufT"], 1)
            for e in range(NE):
                act.wait_ge(S["hid_ps"], e + 1)
                for j in range(1 + e % 2):
                    k = COLS["moe_b1"][0] + 2 * e + j
                    last = act.activation(hid[:, e, j], ps[:, ((0, 4), (2, 6))[j][e % 2], 0:CAP], ACT.Relu,
                                          bias=cols_s[:, k:k + 1])
                last.then_inc(S["hid"], 1)

        @block.tensor
        def _(pe):
            def flip(dst, src, n=P):
                return pe.transpose(dst, src, con_s[0:n, 0:n])

            def keep_clock(awaited, i):
                n, b = KEEP_CLOCK.get((awaited, i), (0, 0))
                for _ in range(n):
                    pe.matmul(ps[:, b, 0:HALF], idle[:, 0:P], idle[:, 0:HALF], start=True, stop=True)

            pe.wait_ge(S["idle"], 1)
            keep_clock("in_conv", 0)
            pe.wait_ge(in_conv, 32)
            for n, at in enumerate(PAT_PARTS):
                pe.wait_ge(in_pat[n], 16)
                for h in range(2):
                    for k in range(at.start, at.stop):
                        for c in range(2):
                            last = pe.matmul(bank(h, 0)[c * D:(c + 1) * D, 0:P], wconv_s[:, k, :],
                                             pat_s[:, k, tok(2 * h + c)], start=(k == 0), stop=(k == KC - 1))
                    if at.stop == KC:
                        last.then_inc(S["conv_ps"], 1)
            keep_clock("in_small", 0)
            pe.wait_ge(in_small, 32)
            for h in range(2):
                keep_clock("conv_f", h)
                pe.wait_ge(S["conv_f"], h + 1)
                flip(bank(h, 1)[:, 0:P], conv_f[:, h * P:(h + 1) * P]).then_inc(S["conv_t"], 1)

            def rows_to_features(h, b, src, ready, done, need=None):
                keep_clock(ready, h)
                pe.wait_ge(S[ready], need if need else h + 1)
                for c in range(2):
                    last = flip(bank(h, b)[0:D, tok(c)], src[:, 2 * h + c, :])
                last.then_inc(S[done], 1)

            def by_image(h, b, at, weights, src):
                for i in range(2):
                    last = pe.matmul(bank(h, b)[i * D:(i + 1) * D, at:at + 2 * N], weights,
                                     src[:, half(h)].rearrange("p (c i t) -> p c i t", c=2, i=2)[:, :, i, :],
                                     start=True, stop=True)
                return last

            for h in range(2):
                rows_to_features(h, 2, h0, "h0", "h0_ps")
            keep_clock("in_w", 0)
            pe.wait_ge(in_w, 48)
            pe.wait_ge(S["setup"], 2)

            def ff1(h, src, ready, done):
                keep_clock(ready, h)
                pe.wait_ge(S[ready], h + 1)
                for j in range(2):
                    last = pe.matmul(bank(h, 3)[:, j * HALF:(j + 1) * HALF], w5("ff1")[:, j * P:(j + 1) * P],
                                     src[:, half(h)], start=True, stop=True)
                last.then_inc(S[done], 1)

            for h in range(2):
                ff1(h, h0T, "h0T", "ff1a_ps")
            for h in range(2):
                keep_clock("g0", h)
                pe.wait_ge(S["g0"], h + 1)
                for j in range(2):
                    last = pe.matmul(bank(h, 0)[0:D, 0:HALF], ff2_s[:, j, :], g0[:, j, half(h)],
                                     start=(j == 0), stop=(j == 1))
                last.then_inc(S["ff2a_ps"], 1)
            for h in range(2):
                keep_clock("fT", h)
                pe.wait_ge(S["fT"], h + 1)
                by_image(h, 1, 0, w5("q8"), fT).then_inc(S["q8_ps"], 1)
                by_image(h, 3, 0, w5("k8"), fT).then_inc(S["k8_ps"], 1)
                for b in range(4):
                    t0 = h * HALF + b * N
                    for i in range(2):
                        last = pe.matmul(bank(h, 2)[i * N:(i + 1) * N, b * D:(b + 1) * D], fT[:, t0:t0 + N],
                                         w5("v8"), start=True, stop=True)
                last.then_inc(S["v8_ps"], 1)
            for c in range(NC):
                keep_clock("k8x", c)
                pe.wait_ge(S["k8x"], c // 2 + 1)
                pe.wait_ge(S["q8_copy"], c // 2 + 1)
                pe.matmul(bank(c // 2, (3, 0)[c % 2]), q_bd[:, c, :], k8x[:, c].rearrange("p g k -> p (g k)"),
                          start=True, stop=True).then_inc(S["s8_ps"], 1)
            for c in range(NC):
                keep_clock("p8", c)
                pe.wait_ge(S["p8"], c + 1)
                if c % 2:
                    keep_clock("v8", c)
                    pe.wait_ge(S["v8"], c // 2 + 1)
                for g in range(4):
                    last = flip(bank(c // 2, (1, 2)[c % 2])[:, g * P:(g + 1) * P],
                                s8[:, c].rearrange("p g k -> p (g k)")[:, g * P:(g + 1) * P])
                last.then_inc(S["pT8_ps"], 1)
            for c in range(NC):
                keep_clock("pT8", c)
                pe.wait_ge(S["pT8_act"] if c % 2 else S["pT8"], c // 2 + 1)
                pe.wait_ge(S["v8"], c // 2 + 1)
                pe.wait_ge(S["s8"], min(NC, 2 * (c // 2) + 2))
                for i in range(2):
                    for g in range(4):
                        at = (c % 2) * 72 + g * 18
                        last = pe.matmul(bank(c // 2, 3)[i * N:(i + 1) * N, at:at + 18],
                                         pT8[:, c, g, i * N:(i + 1) * N], v8[:, 2 * c + i, g, :], start=True, stop=True)
                last.then_inc(S["o8_ps"], 1)
            for h in range(2):
                rows_to_features(h, 0, o8, "o8", "o8T_ps", 2 * h + 2)
            for h in range(2):
                keep_clock("o8T", h)
                pe.wait_ge(S["o8T"], h + 1)
                for c in range(2):
                    last = pe.matmul(bank(h, 1)[:, c * D:(c + 1) * D], o8T[:, tok(2 * h + c)], w5("proj"),
                                     start=True, stop=True)
                last.then_inc(S["proj_ps"], 1)
            for h in range(2):
                rows_to_features(h, 2, h1, "h1", "h1T_ps")
            for h in range(2):
                ff1(h, h0T, "h1T", "ff1b_ps")
            for h in range(2):
                keep_clock("g1", h)
                pe.wait_ge(S["g1"], h + 1)
                for c in range(2):
                    for j in range(2):
                        last = pe.matmul(bank(h, 0)[:, c * D:(c + 1) * D], g0[:, j, tok(2 * h + c)], ff2_s[:, j, :],
                                         start=(j == 0), stop=(j == 1))
                last.then_inc(S["ff2b_ps"], 1)
            for h in range(2):
                rows_to_features(h, 1, n2, "n2", "n2T_ps")
            for h in range(2):
                keep_clock("n2T", h)
                pe.wait_ge(S["n2T"], h + 1)
                for w, weights in enumerate((w5("aq"), w5("ak"))):
                    for c in range(2):
                        last = pe.matmul(bank(h, 2)[c * D:(c + 1) * D, w * P:(w + 1) * P], weights,
                                         fT[:, tok(2 * h + c)], start=True, stop=True)
                last.then_inc(S["aqk_ps"], 1)
                for c in range(2):
                    last = pe.matmul(bank(h, 3)[:, c * D:(c + 1) * D], fT[:, tok(2 * h + c)], w5("av"),
                                     start=True, stop=True)
                last.then_inc(S["av_ps"], 1)
            pe.wait_ge(S["masks"], 1)
            for c in range(NC):
                pe.matmul(bank(c // 2, c % 2)[:, 0:P], ident_b[:], pair_b[:], start=True, stop=False)
            for h in range(2):
                keep_clock("aqk", h)
                pe.wait_ge(S["aqk"], h + 1)
                for c in range(2):
                    rr = slice(c * D, (c + 1) * D)
                    last = pe.matmul(bank(h, c)[:, 0:P], aqk[rr, 0, h * P:(h + 1) * P],
                                     aqk[rr, 1, h * P:(h + 1) * P], start=False, stop=True)
                last.then_inc(S["sa_ps"], 1)
            for h in range(2):
                keep_clock("pa", h)
                pe.wait_ge(S["pa"], 2 * h + 2)
                for c in range(2):
                    last = flip(bank(h, 1)[:, c * P:(c + 1) * P], sa[:, 2 * h + c, :])
                last.then_inc(S["paT_ps"], 1)
            for h in range(2):
                keep_clock("paT", h)
                pe.wait_ge(S["paT"], h + 1)
                pe.wait_ge(S["av"], h + 1)
                for c in range(2):
                    last = pe.matmul(bank(h, 2)[:, c * D:(c + 1) * D], paT[:, 2 * h + c, :], av[:, 2 * h + c, :],
                                     start=True, stop=True)
                last.then_inc(S["oa_ps"], 1)
            for h in range(2):
                rows_to_features(h, 3, r3, "r3", "r3T_ps")
            for h in range(2):
                keep_clock("r3T", h)
                pe.wait_ge(S["r3T"], h + 1)
                for w, (a, b, done) in enumerate((("fq", "fqr", "q4_ps"), ("fk", "fkr", "k4_ps"))):
                    by_image(h, w, 0, w4(a), r3T)
                    by_image(h, w, 2 * N, w4(b), r3T).then_inc(S[done], 1)
                for b in range(4):
                    t0 = h * HALF + b * N
                    for i in range(2):
                        last = pe.matmul(bank(h, 2)[i * N:(i + 1) * N, b * D:(b + 1) * D], r3T[:, t0:t0 + N],
                                         w4("fv"), start=True, stop=True)
                last.then_inc(S["v4_ps"], 1)
            for h in range(2):
                pe.matmul(bank(h, 3), ident_b[:], causal_b[:].unsqueeze(1).to_broadcast([P, 2 * 4, N]),
                          start=True, stop=False)
            for c in range(NC):
                keep_clock("k4x", c)
                pe.wait_ge(S["k4x"], c // 2 + 1)
                pe.matmul(bank(c // 2, 3)[:, (c % 2) * 256:(c % 2 + 1) * 256], q4_bd[:, c, :],
                          k4x[:, c].rearrange("p g k -> p (g k)"), start=False,
                          stop=(c % 2 == 1)).then_inc(S["s4_ps"], 1)
            for h in range(2):
                for c in range(2 * h, 2 * h + 2):
                    keep_clock("p4", c)
                    pe.wait_ge(S["p4"], c + 1)
                    for g in range(2):
                        at = (c % 2) * 256 + g * P
                        last = flip(bank(h, 0)[:, at:at + P],
                                    s4[:, c].rearrange("p g k -> p (g k)")[:, g * P:(g + 1) * P])
                last.then_inc(S["pT4_ps"], 1)
            for c in range(NC):
                keep_clock("pT4", c)
                pe.wait_ge(S["pT4"], c // 2 + 1)
                pe.wait_ge(S["v4"], c // 2 + 1)
                for i in range(2):
                    for g in range(2):
                        at = (c % 2) * 68 + g * 34
                        last = pe.matmul(bank(c // 2, 1)[i * N:(i + 1) * N, at:at + 34],
                                         pT4[:, c, g, i * N:(i + 1) * N], v4[:, 2 * c + i, g, :], start=True, stop=True)
                last.then_inc(S["o4_ps"], 1)
            for h in range(2):
                rows_to_features(h, 2, o4, "o4", "o4T_ps", 2 * h + 2)
            for h in range(2):
                keep_clock("o4T", h)
                pe.wait_ge(S["o4T"], h + 1)
                for c in range(2):
                    last = pe.matmul(bank(h, 3)[:, c * D:(c + 1) * D], o4T[:, tok(2 * h + c)], w4("fo"),
                                     start=True, stop=True)
                last.then_inc(S["wo_ps"], 1)
            for h in range(2):
                keep_clock("fl", h)
                pe.wait_ge(S["fl"], h + 1)
                for c in range(2):
                    last = flip(bank(h, 0)[:, tok(c)], fl[:, 2 * h + c].rearrange("p w d -> p (w d)"))
                last.then_inc(S["flT_ps"], 1)
            keep_clock("fs", 0)
            pe.wait_ge(S["flT"], 2)
            for c in range(NC):
                last = pe.matmul(ps[:, 1, c * NE:(c + 1) * NE], flT[0:D, tok(c)], w4("router"), start=True, stop=True)
            last.then_inc(S["rt_ps"], 1)
            pe.wait_ge(S["fs"], 2)
            keep_clock("split", 0)
            pe.wait_ge(S["split"], 3)

            def up(i):
                if i >= 2:
                    pe.wait_ge(S["asil"], i - 1)
                    pe.wait_ge(S["sb"], i - 1)
                for j, b, done in ((0, (0, 4)[i % 2], "a_ps"), (1, (3, 7)[i % 2], "b_ps")):
                    pe.matmul(ps[:, b, :], f13h[:, j, i * P:(i + 1) * P], fs[:], start=True, stop=False)
                    pe.matmul(ps[:, b, :], f13l[:, j, i * P:(i + 1) * P], fs[:], start=False,
                              stop=True).then_inc(S[done], 1)

            def gates(i):
                if i >= 2:
                    pe.wait_ge(S["hgb"], i - 1)
                pe.matmul(ps[:, (1, 5)[i % 2], :], sel_s[:, i * P:(i + 1) * P], gT[:], start=True,
                          stop=True).then_inc(S["gc_ps"], 1)

            up(0)
            up(1)
            keep_clock("gpart", 0)
            pe.wait_ge(S["gpart"], 1)
            for h in range(2):
                for c in range(2):
                    last = flip(bank(h, 2)[0:2 * NE, tok(c)],
                                gpart[:, 2 * h + c].rearrange("p w e -> p (w e)").bitcast(F32))
                last.then_inc(S["gT_ps"], 1)
            keep_clock("gT", 0)
            pe.wait_ge(S["gT"], 2)

            def down(i):
                if i in LOW_DVE:
                    pe.wait_ge(S["hgl_dve"], LOW_DVE.index(i) + 1)
                else:
                    pe.wait_ge(S["hgl"], by_pool(i))
                both = fw2s[:, i].rearrange("p w d -> p (w d)")
                pe.matmul(ps[:, 6, :], both, hgs[:, i % RING, 0], start=(i == 0), stop=False)
                pe.matmul(ps[:, 6, :], both, hgs[:, i % RING, 1], start=False,
                          stop=(i == HC - 1)).then_inc(S["moe_ps"], 1)

            for i in range(2, LEAD):
                up(i)
            for i in range(HC + LAG):
                if i < HC:
                    gates(i)
                if i + LEAD < HC:
                    up(i + LEAD)
                if i >= LAG:
                    down(i - LAG)
            for h in range(2):
                keep_clock("moeT", h)
                pe.wait_ge(S["moeT"], h + 1)
                for c in range(2):
                    last = pe.matmul(bank(h, 1)[:, c * D:(c + 1) * D], moeT[:, tok(2 * h + c)], con_("both"),
                                     start=True, stop=True)
                last.then_inc(S["moeTb_ps"], 1)
            for h in range(2):
                rows_to_features(h, 3, x5, "x5", "x5T_ps")
            for h in range(2):
                keep_clock("x5T", h)
                pe.wait_ge(S["x5T"], h + 1)
                for c in range(2):
                    last = pe.matmul(bank(h, 1)[:, c * P:(c + 1) * P], x5T[:, tok(2 * h + c)], w4("lkv"),
                                     start=True, stop=True)
                last.then_inc(S["lkv_ps"], 1)
                pe.matmul(bank(h, 0)[0:D, 0:HALF], w4("lq"), x5T[:, half(h)], start=True,
                          stop=True).then_inc(S["lq_ps"], 1)
            for h in range(2):
                keep_clock("phk", h)
                pe.wait_ge(S["phk"], h + 1)
                for c in range(2):
                    last = pe.matmul(bank(h, 2)[0:D, c * 144:(c + 1) * 144], phk[:, 2 * h + c, :],
                                     v1[:, 2 * h + c].rearrange("p i d -> p (i d)"), start=True, stop=True)
                last.then_inc(S["kv_ps"], 1)
            for h in range(2):
                keep_clock("phq", h)
                pe.wait_ge(S["phq"], h + 1)
                pe.wait_ge(S["kv"], h + 1)
                for b in range(4):
                    last = pe.matmul(bank(h, 3)[(b % 2) * N:(b % 2 + 1) * N, (b // 2) * 72:(b // 2 + 1) * 72],
                                     phq[:, h * HALF + b * N:h * HALF + (b + 1) * N], kv[:, 4 * h + b, :],
                                     start=True, stop=True)
                last.then_inc(S["t5_ps"], 1)
            keep_clock("late_setup", 0)
            pe.wait_ge(S["late_setup"], 4)
            for h in range(2):
                rows_to_features(h, 0, x1, "x1", "x1T_ps")
            for h in range(2):
                keep_clock("x1T", h)
                pe.wait_ge(S["x1T"], h + 1)
                pe.matmul(bank(h, 1)[0:D, 0:HALF], w5("l1w1"), x1T[:, half(h)], start=True,
                          stop=True).then_inc(S["l1h_ps"], 1)
            for h in range(2):
                keep_clock("g5", h)
                pe.wait_ge(S["g5"], h + 1)
                for c in range(2):
                    last = pe.matmul(bank(h, 2)[:, c * D:(c + 1) * D], g5[:, tok(2 * h + c)], w5("l1w2"),
                                     start=True, stop=True)
                last.then_inc(S["l1y_ps"], 1)
            for h in range(2):
                rows_to_features(h, 3, x7, "x7", "x7T_ps")
            for h in range(2):
                keep_clock("x7T", h)
                pe.wait_ge(S["x7T"], h + 1)
                for c in range(2):
                    last = pe.matmul(bank(h, 0)[:, c * NE:(c + 1) * NE], x7T[:, tok(2 * h + c)], w5("gate"),
                                     start=True, stop=True)
                last.then_inc(S["g_ps"], 1)
            def output_bias(i):
                pe.matmul(ps[0:CAP, (5, 3)[i], 0:4 * D], x1T[D:D + 1, 0:CAP],
                          mb2_s[D:D + 1, 4 * i:4 * i + 4].rearrange("p e d -> p (e d)"), start=True, stop=False)

            output_bias(1)
            for h in range(2):
                keep_clock("oh1b", h)
                pe.wait_ge(S["oh1b"], h + 1)
                for c in range(2 * h, 2 * h + 2):
                    dst = bank(h, 1)[:, (c % 2) * NE:(c % 2 + 1) * NE]
                    for c0 in range(c):
                        pe.matmul(dst, tri_s[:, 1, :], oh1b[:, c0], start=(c0 == 0), stop=False)
                    last = pe.matmul(dst, tri_s[:, 0, :], oh1b[:, c], start=(c == 0), stop=True)
                last.then_inc(S["cum_ps"], 1)
            for c in range(NC):
                if c == 2:
                    keep_clock("code", 0)
                    pe.wait_ge(S["code"], 1)
                    for k in range(NC):
                        last = pe.matmul(ps[0:CAP, 7, tok(k)], code_r[:, k:k + 1].to_broadcast([P, CAP]), ident_r[:],
                                         start=True, stop=True)
                    last.then_inc(S["cod_ps"], 1)
                keep_clock("disp", c)
                pe.wait_ge(S["disp"], c + 1)
                if c == 2:
                    output_bias(0)
                for i in range(2):
                    last = pe.matmul(ps[:, (2, 6)[i], 0:4 * CAP], x7s[:, c].rearrange("p w d -> p (w d)"),
                                     disp[:, c, 4 * i:4 * i + 4].rearrange("p e s -> p (e s)"),
                                     start=(c == 0), stop=(c == NC - 1))
                    if c == NC - 1:
                        last.then_inc(S["bufT_ps"], 1)

            def outputs(e):
                pe.wait_ge(S["hid"], e + 1)
                if e % 2 == 0:
                    pe.wait_ge(S["hid_dve"], e // 2 + 1)
                for j in range(2):
                    last = pe.matmul(ps[0:CAP, (5, 3)[e // 4], (e % 4) * D:(e % 4 + 1) * D], hid[:, e, j],
                                     m2_s[:, e, j, :], start=False, stop=(j == 1 and e % 4 == 3))
                if e % 4 == 3:
                    last.then_inc(S["y_ps"], 1)

            for e in range(NE):
                keep_clock("bufT", e)
                pe.wait_ge(S["bufT"], 2 if e else 1)
                if e >= 2:
                    keep_clock("hid", e)
                    pe.wait_ge(S["hid"], e - 1)
                    if e % 2 == 0:
                        pe.wait_ge(S["hid_dve"], e // 2)
                for j in range(2):
                    dst = ps[:, ((0, 4), (2, 6))[j][e % 2], 0:CAP]
                    pe.matmul(dst, m1h[:, e, j * P:(j + 1) * P], bufT[:, e], start=True, stop=False)
                    last = pe.matmul(dst, m1l[:, e, j * P:(j + 1) * P], bufT[:, e], start=False, stop=True)
                last.then_inc(S["hid_ps"], 1)
                if e >= 2:
                    outputs(e - 2)
            outputs(NE - 2)
            outputs(NE - 1)
            keep_clock("combT", 0)
            for i in range(2):
                of_dve = sum(e in COMB_DVE for e in range(4 * i + 4))
                pe.wait_ge(S["combT"], of_dve)
                pe.wait_ge(S["combT_pool"], 4 * i + 4 - of_dve)
                pe.wait_ge(S["ybs"], i + 1)
                for h in range(2):
                    for c in range(2 * h, 2 * h + 2):
                        for e in range(4 * i, 4 * i + 4):
                            last = pe.matmul(ps[:, COMB_BANK[c], 0:P], combT[:, e, tok(c)],
                                             ybs[:, e].rearrange("p w d -> p (w d)"), start=(e == 0),
                                             stop=(e == NE - 1))
                    if i == 1:
                        last.then_inc(S["comb_ps"], 1)


def constants():
    f = np.float32
    con = np.zeros((P, CON_N), f)

    def put(name, a):
        a = np.asarray(a, f)
        con[:a.shape[0], CON[name][0]:CON[name][1]] = a

    feat = np.arange(P) % D
    side = np.arange(P) // D
    put("ident", np.eye(P))
    put("both", feat[:, None] == np.arange(D))
    put("mask8", (feat[:, None] // 8 == np.arange(8)) / np.sqrt(8.0))
    put("vmask8", (np.arange(D)[None] // 8 % 2) == side[:, None])
    put("mask4", (feat[:, None] // 16 == np.arange(4)) / np.sqrt(16.0))
    put("vmask4", (np.arange(D)[None] // 16 % 2) == side[:, None])
    inv = (1.0 / 10000.0 ** (np.arange(0, 16, 2, dtype=f) / 16)).astype(f)
    freqs = np.outer(np.arange(N, dtype=f), inv)
    emb = np.concatenate([freqs, freqs], -1)
    sign = np.where(np.arange(16) < 8, -1.0, 1.0)
    put("cos", np.cos(emb).T[feat % 16])
    put("sin", (np.sin(emb) * sign).T[feat % 16])
    put("causal", np.where(np.arange(N)[None] <= feat[:, None], 0.0, NEG))
    put("pair", np.where(side[:, None] == side[None], 0.0, NEG))
    bm = np.zeros((D, 72))
    bm[:, :D] = np.arange(D)[:, None] // 8 == np.arange(D)[None] // 8
    bm[:, D:] = np.arange(D)[:, None] // 8 == np.arange(8)[None]
    put("bm", bm)
    put("iota8", np.tile(np.arange(NE), (P, 1)))
    put("slots", np.tile(np.arange(1, CAP + 1), (P, 1)))
    put("slotid", np.arange(1, P + 1)[:, None])
    put("expert", np.tile(128 * np.arange(NE) + 0, (P, 1)))
    expert = np.minimum(np.arange(HC * P) // HID, NE - 1)
    sel = np.tile(expert[None] == np.arange(NE)[:, None], (2, 1)).astype(f)
    tri = np.stack([np.triu(np.ones((P, P))), np.ones((P, P))], 1).astype(f)
    pos = np.arange(N, dtype=f)[:, None]
    div = np.exp(-np.log(f(10000.0)) * np.arange(0, D, 2, dtype=f) / D).astype(f)
    ang = (pos * div).astype(f)
    pe = np.stack([np.sin(ang), np.cos(ang)], -1).reshape(N, D).astype(f)
    return con, sel, tri, np.tile(pe, (2, 1))


def kernel(**inputs):
    import concourse.bacc as _bacc
    from concourse.bass_utils import run_bass_kernel_spmd as _run

    a = {k: np.asarray(v) for k, v in inputs.items()}
    f = np.float32
    con, sel, tri, pe = constants()

    pat = a["x"].reshape(B, 3, 8, 2, 8, 8, 16).transpose(4, 6, 1, 3, 0, 2, 5).reshape(P, KC, T)
    wconv = a["L0_tok_conv_w"].reshape(D, 3, 2, 8, 16).transpose(3, 4, 1, 2, 0).reshape(P, KC, D)

    def bcast(v):
        return np.broadcast_to(v[None], (P, D))

    rows = np.concatenate([bcast(a["L0_tok_ln_w"]), bcast(a["L0_tok_ln_b"]), pe, bcast(a["L0_tok_ff_b2"]),
                           bcast(a["L1_attn_ln1_g"]), bcast(a["L1_attn_ln1_b"]), bcast(a["L1_attn_ln2_g"]),
                           bcast(a["L1_attn_ln2_b"])], 1)
    cols = np.concatenate([np.tile(a["L0_tok_conv_b"], 2)[:, None], np.tile(a["L0_tok_ff_b2"], 2)[:, None],
                           np.tile(a["L0_ffn_ln1_w"], 2)[:, None], np.tile(a["L0_ffn_ln2_w"], 2)[:, None],
                           a["L1_ffn_b1"].reshape(NE * 2, P).T], 1)

    def with_bias(w, b):
        return np.concatenate([w, b[None]], 0)

    qkv, qkvb = a["L0_tok_qkv_w"].T, a["L0_tok_qkv_b"]
    q8, k8, v8 = (with_bias(qkv[:, i * D:(i + 1) * D], qkvb[i * D:(i + 1) * D]) for i in range(3))
    w65 = np.concatenate([with_bias(a["L0_tok_ff_w1"].T, a["L0_tok_ff_b1"]), q8, k8, v8,
                          with_bias(a["L0_tok_proj_w"].T, a["L0_tok_proj_b"]),
                          with_bias(a["L0_attn_Wq"], a["L0_attn_bq"]), with_bias(a["L0_attn_Wk"], a["L0_attn_bk"]),
                          with_bias(a["L0_attn_Wv"], a["L0_attn_bv"]), with_bias(a["L1_attn_W1"].T, a["L1_attn_b1"]),
                          with_bias(a["L1_attn_W2"].T, a["L1_attn_b2"]),
                          with_bias(a["L1_ffn_gate_w"], a["L1_ffn_gate_b"])], 1)
    head = np.arange(D) // 16
    other = (np.arange(D) % 16 + 8) % 16
    fq = a["L0_ffn_wq"].T
    fk = a["L0_ffn_wk"].T[:, head // 2 * 16 + np.arange(D) % 16]
    fkr = a["L0_ffn_wk"].T[:, head // 2 * 16 + other]
    fqr = fq[:, head * 16 + other]
    fv = a["L0_ffn_wv"].T[:, head // 2 * 16 + np.arange(D) % 16]
    wl = a["L1_attn_Wqkv"].T
    w64 = np.concatenate([fq, fqr, fk, fkr, fv, a["L0_ffn_wo"].T, a["L0_ffn_router_w"].T,
                          wl[:, 0:D], wl[:, D:3 * D]], 1)
    ff2 = a["L0_tok_ff_w2"].T.reshape(2, P, D).transpose(1, 0, 2)
    pad = HC * P - NE * HID

    def stacked(w):
        w = np.pad(w.reshape(NE * HID, D).T, ((0, 0), (0, pad)))
        return np.concatenate([w, w], 0)

    f13 = np.stack([stacked(a["L0_ffn_w1"]), stacked(a["L0_ffn_w3"])], 1)
    fw2 = np.pad(a["L0_ffn_w2"].transpose(0, 2, 1).reshape(NE * HID, D), ((0, pad), (0, 0)))
    fw2 = fw2.reshape(HC, P, D).transpose(1, 0, 2)
    m1 = np.tile(a["L1_ffn_w1"].transpose(1, 0, 2), (2, 1, 1))
    m2 = a["L1_ffn_w2"].reshape(NE, 2, P, D).transpose(2, 0, 1, 3)
    mb2 = np.broadcast_to(a["L1_ffn_b2"][None], (CAP, NE, D))
    sent = dict(pat=pat, wconv=wconv, rows=rows, cols=cols, w65=w65, w64=w64, ff2=ff2, f13=f13, fw2=fw2, m1=m1, m2=m2,
                mb2=mb2, con=con, sel=sel, tri=tri)

    nc = _bacc.Bacc("TRN2", target_bir_lowering=False, num_devices=1)
    arrays, args = {}, {}
    for name, v in sent.items():
        v = np.ascontiguousarray(v)
        arrays[f"in_{name}"] = v
        args[name] = nc.dram_tensor(f"in_{name}", v.shape, mybir.dt.from_np(v.dtype), kind="ExternalInput").ap()
    args["out"] = nc.dram_tensor("out_0", (T, D), F32, kind="ExternalOutput").ap()
    vit_tower(nc, **args)
    r = _run(nc, [arrays], core_ids=[0])
    return r.results[0]["out_0"].reshape(B, N, D)
```
